# Optimizing a Trainium2 kernel written in Bass

```python
import numpy as np
import jax
import jax.numpy as jnp

def _softmax(x, axis=-1):
    return jax.nn.softmax(x, axis=axis)

def _gelu(x):
    return jax.nn.gelu(x, approximate=True)

def _silu(x):
    return jax.nn.silu(x)

def _sigmoid(x):
    return jax.nn.sigmoid(x)

def _layernorm(x, axis=-1, eps=1e-05):
    m = jnp.mean(x, axis=axis, keepdims=True)
    v = jnp.var(x, axis=axis, keepdims=True)
    return (x - m) / jnp.sqrt(v + eps)

def _scatter_add(tgt, idx, src, axis=0):
    return tgt.at[idx].add(src)

def _segment_sum(src, seg, n):
    return jax.ops.segment_sum(src, seg, n)
kernel_name = 'mk_vit_tower_d1_tok_img768_r4_67cdeb'

def setup_inputs(seed: int=0):
    np.random.seed(seed)
    _w = jnp.asarray

    def _rec_inputs():
        import jax
        import jax.numpy as jnp
        _rk = jax.random.key(seed)
        x = -0.00016672 + 0.999947 * jax.random.normal(jax.random.fold_in(_rk, 1), (16, 3, 128, 128), jnp.float32)
        return x
    x = _rec_inputs()

    def _L0_tok_setup():
        import jax, jax.numpy as jnp
        import numpy as np
        PATCH = (16, 16)
        EPS = 1e-05

        def img2patches(x, ph, pw):
            B, C, H, W = x.shape
            h, w = (H // ph, W // pw)
            x = x.reshape(B, C, h, ph, w, pw)
            x = x.transpose(0, 2, 4, 3, 5, 1)
            return x.reshape(B, h * w, ph * pw * C)

        def layernorm(x, g, b):
            mu = jnp.mean(x, axis=-1, keepdims=True)
            var = jnp.mean(jnp.square(x - mu), axis=-1, keepdims=True)
            return (x - mu) * jax.lax.rsqrt(var + EPS) * g + b
        key = jax.random.key(seed)
        ks = jax.random.split(key, 7)
        B, C, H, W_ = (64, 3, 96, 96)
        patch_dim = PATCH[0] * PATCH[1] * C
        model_dim = 192
        return {'x': jax.random.normal(ks[0], (B, C, H, W_), dtype=jnp.float32), 'ln1_g': jax.random.uniform(ks[1], (patch_dim,), dtype=jnp.float32), 'ln1_b': jax.random.normal(ks[2], (patch_dim,), dtype=jnp.float32) * 0.02, 'W': jax.random.normal(ks[3], (patch_dim, model_dim), dtype=jnp.float32) * (1.0 / np.sqrt(patch_dim)), 'b': jax.random.normal(ks[4], (model_dim,), dtype=jnp.float32) * 0.02, 'ln2_g': jax.random.uniform(ks[5], (model_dim,), dtype=jnp.float32), 'ln2_b': jax.random.normal(ks[6], (model_dim,), dtype=jnp.float32) * 0.02}
    _L0_tok_all = _L0_tok_setup()
    _L0_tok_in = {k: v for k, v in _L0_tok_all.items() if k in ('ln1_g', 'ln1_b', 'W', 'b', 'ln2_g', 'ln2_b')}
    del _L0_tok_all

    def _L0_attn_setup():
        import jax, jax.numpy as jnp
        import numpy as np
        NUM_HEADS = 12
        NUM_LANDMARKS = 64
        DIM = 192

        def _iterative_inv(mat, n_iter=6):
            L = mat.shape[-1]
            I = jnp.eye(L, dtype=mat.dtype)
            K = mat
            denom = jnp.max(jnp.sum(K, axis=-2), axis=-1)[:, :, None, None]
            V = 1.0 / denom * jnp.swapaxes(K, -1, -2)
            for _ in range(n_iter):
                KV = jnp.matmul(K, V)
                V = jnp.matmul(0.25 * V, 13.0 * I - jnp.matmul(KV, 15.0 * I - jnp.matmul(KV, 7.0 * I - KV)))
            return V
        key = jax.random.key(seed)
        k1, k2, k3, k4 = jax.random.split(key, 4)
        B, N, C = (4, 1024, DIM)
        x = jax.random.normal(k1, (B, N, C), dtype=jnp.float32)
        w_qkv = jax.random.normal(k2, (3 * C, C), dtype=jnp.float32) * C ** (-0.5)
        w_proj = jax.random.normal(k3, (C, C), dtype=jnp.float32) * C ** (-0.5)
        b_proj = jax.random.normal(k4, (C,), dtype=jnp.float32) * 0.01
        return {'x': x, 'w_qkv': w_qkv, 'w_proj': w_proj, 'b_proj': b_proj}
    _L0_attn_all = _L0_attn_setup()
    _L0_attn_in = {k: v for k, v in _L0_attn_all.items() if k in ('w_qkv', 'w_proj', 'b_proj')}
    del _L0_attn_all

    def _L0_ffn_setup():
        import jax, jax.numpy as jnp
        import numpy as np
        B_SZ, S, D = (8, 128, 192)
        H = 12
        N_EXP = 8
        RANK = 16
        ALPHA = 32
        TOP_K = 2
        key = jax.random.key(seed)
        ks = jax.random.split(key, 9)
        x = jax.random.normal(ks[0], (B_SZ, S, D), jnp.float32)
        W_qkv = jax.random.normal(ks[1], (3 * D, D), jnp.float32) * 0.02
        b_qkv = jnp.zeros((3 * D,), jnp.float32)
        W_gate = jax.random.normal(ks[2], (N_EXP, D), jnp.float32) * 0.02
        b_gate = jnp.zeros((N_EXP,), jnp.float32)
        A = jax.random.normal(ks[3], (N_EXP, RANK, D), jnp.float32) * 0.02
        B_lora = jax.random.normal(ks[4], (N_EXP, 3 * D, RANK), jnp.float32) * 0.02
        W_proj = jax.random.normal(ks[5], (D, D), jnp.float32) * 0.02
        b_proj = jnp.zeros((D,), jnp.float32)
        return {'x': x, 'W_qkv': W_qkv, 'b_qkv': b_qkv, 'W_gate': W_gate, 'b_gate': b_gate, 'A': A, 'B_lora': B_lora, 'W_proj': W_proj, 'b_proj': b_proj}
    _L0_ffn_all = _L0_ffn_setup()
    _L0_ffn_in = {k: v for k, v in _L0_ffn_all.items() if k in ('W_qkv', 'b_qkv', 'W_gate', 'b_gate', 'A', 'B_lora', 'W_proj', 'b_proj')}
    del _L0_ffn_all
    return {'x': x, 'L0_tok_ln1_g': _L0_tok_in['ln1_g'], 'L0_tok_ln1_b': _L0_tok_in['ln1_b'], 'L0_tok_W': _L0_tok_in['W'], 'L0_tok_b': _L0_tok_in['b'], 'L0_tok_ln2_g': _L0_tok_in['ln2_g'], 'L0_tok_ln2_b': _L0_tok_in['ln2_b'], 'L0_attn_w_qkv': _L0_attn_in['w_qkv'], 'L0_attn_w_proj': _L0_attn_in['w_proj'], 'L0_attn_b_proj': _L0_attn_in['b_proj'], 'L0_ffn_W_qkv': _L0_ffn_in['W_qkv'], 'L0_ffn_b_qkv': _L0_ffn_in['b_qkv'], 'L0_ffn_W_gate': _L0_ffn_in['W_gate'], 'L0_ffn_b_gate': _L0_ffn_in['b_gate'], 'L0_ffn_A': _L0_ffn_in['A'], 'L0_ffn_B_lora': _L0_ffn_in['B_lora'], 'L0_ffn_W_proj': _L0_ffn_in['W_proj'], 'L0_ffn_b_proj': _L0_ffn_in['b_proj']}

def reference(x, L0_tok_ln1_g, L0_tok_ln1_b, L0_tok_W, L0_tok_b, L0_tok_ln2_g, L0_tok_ln2_b, L0_attn_w_qkv, L0_attn_w_proj, L0_attn_b_proj, L0_ffn_W_qkv, L0_ffn_b_qkv, L0_ffn_W_gate, L0_ffn_b_gate, L0_ffn_A, L0_ffn_B_lora, L0_ffn_W_proj, L0_ffn_b_proj):
    import jax
    import jax.numpy as jnp

    def _L0_tok_ref(x, ln1_g, ln1_b, W, b, ln2_g, ln2_b):
        import jax, jax.numpy as jnp
        import numpy as np
        PATCH = (16, 16)
        EPS = 1e-05

        def img2patches(x, ph, pw):
            B, C, H, W = x.shape
            h, w = (H // ph, W // pw)
            x = x.reshape(B, C, h, ph, w, pw)
            x = x.transpose(0, 2, 4, 3, 5, 1)
            return x.reshape(B, h * w, ph * pw * C)

        def layernorm(x, g, b):
            mu = jnp.mean(x, axis=-1, keepdims=True)
            var = jnp.mean(jnp.square(x - mu), axis=-1, keepdims=True)
            return (x - mu) * jax.lax.rsqrt(var + EPS) * g + b
        p = img2patches(x, PATCH[0], PATCH[1])
        h = layernorm(p, ln1_g, ln1_b)
        h = jnp.einsum('bsd,dm->bsm', h, W) + b
        return layernorm(h, ln2_g, ln2_b)

    def _L0_attn_ref(x, w_qkv, w_proj, b_proj):
        import jax, jax.numpy as jnp
        import numpy as np
        NUM_HEADS = 12
        NUM_LANDMARKS = 64
        DIM = 192

        def _iterative_inv(mat, n_iter=6):
            L = mat.shape[-1]
            I = jnp.eye(L, dtype=mat.dtype)
            K = mat
            denom = jnp.max(jnp.sum(K, axis=-2), axis=-1)[:, :, None, None]
            V = 1.0 / denom * jnp.swapaxes(K, -1, -2)
            for _ in range(n_iter):
                KV = jnp.matmul(K, V)
                V = jnp.matmul(0.25 * V, 13.0 * I - jnp.matmul(KV, 15.0 * I - jnp.matmul(KV, 7.0 * I - KV)))
            return V
        B, N, C = x.shape
        H, Lm = (NUM_HEADS, NUM_LANDMARKS)
        hd = C // H
        scale = hd ** 0.5
        qkv = (x @ w_qkv.T).reshape(B, N, 3, H, hd).transpose(2, 0, 3, 1, 4)
        q, k, v = (qkv[0], qkv[1], qkv[2])
        q = q / scale
        segs = N // Lm
        keys_landmarks = k.reshape(B, H, Lm, segs, hd).mean(axis=-2)
        queries_landmarks = q.reshape(B, H, Lm, segs, hd).mean(axis=-2)
        kernel_1 = jax.nn.softmax(jnp.einsum('bhnd,bhld->bhnl', q, keys_landmarks), axis=-1)
        kernel_2 = jax.nn.softmax(jnp.einsum('bhmd,bhld->bhml', queries_landmarks, keys_landmarks), axis=-1)
        kernel_3 = jax.nn.softmax(jnp.einsum('bhld,bhnd->bhln', queries_landmarks, k), axis=-1)
        out = jnp.matmul(jnp.matmul(kernel_1, _iterative_inv(kernel_2)), jnp.matmul(kernel_3, v))
        out = out.transpose(0, 2, 1, 3).reshape(B, N, C)
        return out @ w_proj.T + b_proj

    def _L0_ffn_ref(x, W_qkv, b_qkv, W_gate, b_gate, A, B_lora, W_proj, b_proj):
        import jax, jax.numpy as jnp
        import numpy as np
        B_SZ, S, D = (8, 128, 192)
        H = 12
        N_EXP = 8
        RANK = 16
        ALPHA = 32
        TOP_K = 2
        b, s, d = x.shape
        n_exp, rank = (A.shape[0], A.shape[1])
        scaling = ALPHA / rank
        head_dim = d // H
        scale = head_dim ** (-0.5)
        t = b * s
        x_flat = x.reshape(t, d)
        qkv_base = x @ W_qkv.T + b_qkv
        logits = x_flat @ W_gate.T + b_gate
        router_probs = jax.nn.softmax(logits, axis=-1)
        top_k_weights, top_k_indices = jax.lax.top_k(router_probs, TOP_K)
        a_down = jnp.einsum('td,nrd->tnr', x_flat, A)
        expert_out = jnp.einsum('tnr,nor->tno', a_down, B_lora) * scaling
        dispatch = jnp.zeros((t, n_exp), x.dtype).at[jnp.arange(t)[:, None], top_k_indices].add(top_k_weights)
        sparse_out = jnp.einsum('tno,tn->to', expert_out, dispatch)
        qkv = qkv_base + sparse_out.reshape(b, s, 3 * d)
        qkv = qkv.reshape(b, s, 3, H, head_dim).transpose(2, 0, 3, 1, 4)
        q, k, v = (qkv[0], qkv[1], qkv[2])
        attn = jax.nn.softmax(jnp.einsum('bhqd,bhkd->bhqk', q, k) * scale, axis=-1)
        out = jnp.einsum('bhqk,bhkd->bhqd', attn, v)
        out = out.transpose(0, 2, 1, 3).reshape(b, s, d)
        return out @ W_proj.T + b_proj
    h = _L0_tok_ref(x, L0_tok_ln1_g, L0_tok_ln1_b, L0_tok_W, L0_tok_b, L0_tok_ln2_g, L0_tok_ln2_b)
    h = h + _L0_attn_ref(_layernorm(h, axis=-1), L0_attn_w_qkv, L0_attn_w_proj, L0_attn_b_proj)
    h = h + _L0_ffn_ref(_layernorm(h, axis=-1), L0_ffn_W_qkv, L0_ffn_b_qkv, L0_ffn_W_gate, L0_ffn_b_gate, L0_ffn_A, L0_ffn_B_lora, L0_ffn_W_proj, L0_ffn_b_proj)
    return h

_drawn_inputs = setup_inputs


def setup_inputs(seed=0):
    import zlib

    import numpy as np

    out = dict(_drawn_inputs(seed))
    spreads = {'L0_ffn_b_qkv': (0.0, 0.1), 'L0_ffn_b_gate': (0.0, 0.8), 'L0_ffn_b_proj': (0.0, 0.1)}
    factors = {'L0_attn_b_proj': 3.884, 'L0_ffn_W_gate': 8.0, 'L0_ffn_A': 8.0, 'L0_ffn_B_lora': 8.0}
    for name, (base, spread) in spreads.items():
        noise = np.random.default_rng([zlib.crc32(name.encode()), seed]).standard_normal(out[name].shape)
        drawn = base * np.exp(spread * noise) if base else spread * noise
        out[name] = jnp.asarray(drawn.astype(out[name].dtype))
    for name, factor in factors.items():
        out[name] = (out[name] * factor).astype(out[name].dtype)
    return out
```

```python
from contextlib import ExitStack

import concourse.bass as bass
from concourse import mybir

F32 = mybir.dt.float32
ALU = mybir.AluOpType
ACT = mybir.ActivationFunctionType
AX = mybir.AxisListType

P = 128
IMAGES, CHANNELS, SIDE, PATCH = 16, 3, 128, 16
GRID = SIDE // PATCH
TOKENS = GRID * GRID
PIXELS = PATCH * PATCH * CHANNELS
DIM, HEADS = 192, 12
HEAD = DIM // HEADS
HALF = DIM // 2
GROUPS = 3
PAIRS = HEADS // 2
EXPERTS, RANK = 8, 16
LORA = EXPERTS * RANK
LORA_SCALE = 2.0
TOP = 2
EPS = 1e-5
STEPS = 6
SCALE = float(HEAD) ** -0.5
CHUNKS = PIXELS // P
BANK = 512
QUAD = 4
ROUNDS = IMAGES // QUAD
ROUND_TOKENS = QUAD * TOKENS
BLOCKS = 8
SLOTS = 4


def vit_tower_kernel(nc, x, tok_ln1_g, tok_ln1_b, tok_W, tok_b, tok_ln2_g, tok_ln2_b,
                     attn_w_qkv, attn_w_proj, attn_b_proj, ffn_W_qkv, ffn_b_qkv, ffn_W_gate,
                     ffn_b_gate, ffn_A, ffn_B_lora, ffn_W_proj, ffn_b_proj, out):
    with ExitStack() as ctx:
        def sb(name, shape):
            return ctx.enter_context(nc.sbuf_tensor(name, shape, F32))

        def sem(name):
            return ctx.enter_context(nc.semaphore(name))

        def sems(name, n=GROUPS):
            return [sem(f"{name}_{i}") for i in range(n)]

        bank = [ctx.enter_context(nc.psum_tensor(f"bank{i}", [P, BANK], F32)) for i in range(8)]

        ident = sb("ident", [P, P])
        ident_pair = sb("ident_pair", [P, TOKENS])
        mask_even = sb("mask_even", [P, 1])
        mask_odd = sb("mask_odd", [P, 1])
        eps = sb("eps", [P, 1])
        earlier = sb("earlier", [P, EXPERTS, EXPERTS])
        w_tok = sb("w_tok", [P, 2, CHANNELS, DIM])
        w_tok_g = sb("w_tok_g", [P, 2, CHANNELS, DIM])
        ln1_g = sb("ln1_g", [P, 2, CHANNELS])
        ln1_b = sb("ln1_b", [P, 2, CHANNELS])
        tok_bias = sb("tok_bias", [P, DIM])
        ln2_g = sb("ln2_g", [P, DIM])
        ln2_b = sb("ln2_b", [P, DIM])
        attn_bias = sb("attn_bias", [P, DIM])
        ffn_bias = sb("ffn_bias", [P, DIM])
        v_bias = sb("v_bias", [P, DIM])
        gate_bias = sb("gate_bias", [P, EXPERTS])
        qk_bias = sb("qk_bias", [HALF, 4])
        k_bias_odd = sb("k_bias_odd", [HALF, 2])
        qkv_raw = [sb(f"qkv_raw{i}", [HALF, 6, DIM]) for i in range(2)]
        proj_raw = [sb(f"proj_raw{i}", [HALF, 2, DIM]) for i in range(2)]
        proj_parity = [sb(f"proj_parity{i}", [HALF, 2, DIM]) for i in range(2)]
        qk_bias_raw = sb("qk_bias_raw", [4, HALF])
        a_raw = sb("a_raw", [LORA, DIM])
        gate_raw = sb("gate_raw", [EXPERTS, DIM])
        b_raw = sb("b_raw", [HALF, 6, EXPERTS, RANK])
        wT = [sb(f"wT{i}", [HALF, 2, 3 * DIM]) for i in range(2)]
        projT = [sb(f"projT{i}", [HALF, 2, DIM]) for i in range(2)]
        aT_gate = sb("aT_gate", [HALF, 2, LORA + EXPERTS])
        bT = sb("bT", [LORA, 3 * DIM])
        pix_stats = sb("pix_stats", [P, GRID, CHANNELS * 6])
        stats = sb("stats", [P, GRID, 6])
        mean_var = sb("mean_var", [P, GRID, 2])
        std = sb("std", [P, GRID])
        rstd = sb("rstd", [P, GRID])
        shift = sb("shift", [P, GRID])
        h = sb("h", [P, GRID, DIM])
        h_plus = sb("h_plus", [P, GRID, DIM])
        y = sb("y", [P, GRID, DIM])
        yT = sb("yT", [HALF, 2, IMAGES * TOKENS])
        loraT = sb("loraT", [LORA, IMAGES * TOKENS])
        mixedT = sb("mixedT", [HALF, 2, GRID, IMAGES * GRID])
        halves = (slice(0, TOKENS), slice(TOKENS, P))

        with ExitStack() as stage:
            def sem_a(name):
                return stage.enter_context(nc.semaphore(name))

            def sb_a(name, shape):
                return stage.enter_context(nc.sbuf_tensor(name, shape, F32))

            pixels = sb_a("pixels", [P, CHANNELS, PATCH, GRID, PATCH])
            patches = sb_a("patches", [P, GRID, PIXELS])
            patchesT = sb_a("patchesT", [P, GRID, PIXELS])
            pix_loaded = [sem_a(f"pix_loaded{c}") for c in range(CHANNELS)]
            tok_w_loaded = sem_a("tok_w_loaded")
            tok_rows_loaded = sem_a("tok_rows_loaded")
            attn_w_loaded = sem_a("attn_w_loaded")
            ffn_w_loaded = sem_a("ffn_w_loaded")
            ffn_rows_loaded = sem_a("ffn_rows_loaded")
            ident_zeroed = sem_a("ident_zeroed")
            ident_ready = sem_a("ident_ready")
            consts_ready = sem_a("consts_ready")
            w_scaled = sem_a("w_scaled")
            parity_ready = sem_a("parity_ready")
            dve_step = sem_a("dve_step_a")
            var_ready = sem_a("var_ready")
            std_ready = sem_a("std_ready")
            rstd_ready = sem_a("rstd_ready")
            patch_dve = sem_a("patch_dve")
            patch_act = sem_a("patch_act")
            patchT_ready = sem_a("patchT_ready")
            patchT_copied = [sem_a("patchT_copied_act"), sem_a("patchT_copied_dve")]
            bias_row_ready = sem_a("bias_row_ready")
            bias_row_copied = sem_a("bias_row_copied")
            tok_ready = sem_a("tok_ready")
            wT_ready = sem_a("wT_ready")
            wT_copied = sem_a("wT_copied")
            h_ready = sem_a("h_ready")
            h_plus_ready = sem_a("h_plus_ready")
            y_ready = sem_a("y_ready")
            yT_ready = sem_a("yT_ready")
            yT_copied = sem_a("yT_copied")

            def weight_groups():
                groups = []
                for i in range(2):
                    for kc in range(2):
                        for th in range(2):
                            ins = [qkv_raw[i][:, 3 * th + t, kc * HALF:(kc + 1) * HALF] for t in range(3)]
                            groups.append((ins, HALF, wT[i][:, kc, th * 3 * HALF:(th + 1) * 3 * HALF]))
                    ins = [proj_parity[i][:, o, e * HALF:(e + 1) * HALF] for e in range(2) for o in range(2)]
                    groups.append((ins, HALF, projT[i][:, :, :].rearrange("p e o -> p (e o)")))
                for kc in range(2):
                    ins = [a_raw[:, kc * HALF:(kc + 1) * HALF], gate_raw[:, kc * HALF:(kc + 1) * HALF]]
                    groups.append((ins, HALF, aT_gate[:, kc, :]))
                for th in range(2):
                    ins = [b_raw[:, 3 * th + t, :, :].rearrange("p n r -> p (n r)") for t in range(3)]
                    groups.append((ins, LORA, bT[:, th * 3 * HALF:(th + 1) * 3 * HALF]))
                groups.append(([qk_bias_raw[:, :]], HALF, qk_bias[:, :]))
                return groups

            w_groups = weight_groups()
            attn_groups = 5

            with nc.Block() as block:
                @block.sync
                def _(sp):
                    for c in range(CHANNELS):
                        sp.dma_start(pixels[:, c, :, :, :].rearrange("p r w s -> p (r w s)"),
                                     x_channel(x, c)).then_inc(pix_loaded[c], 16)
                    sp.dma_start(w_tok[:, :, :, :],
                                 tok_W.rearrange("(a p c) m -> p a c m", a=2, c=CHANNELS)).then_inc(tok_w_loaded, 16)
                    sp.dma_start(qkv_raw[0][:, :, :],
                                 attn_w_qkv.rearrange("(t p) i -> p t i", p=HALF)).then_inc(attn_w_loaded, 16)
                    sp.dma_start(proj_raw[0][:, :, :],
                                 attn_w_proj.rearrange("(t p) i -> p t i", p=HALF)).then_inc(attn_w_loaded, 16)
                    sp.dma_start(qkv_raw[1][:, :, :],
                                 ffn_W_qkv.rearrange("(t p) i -> p t i", p=HALF)).then_inc(ffn_w_loaded, 16)
                    sp.dma_start(proj_raw[1][:, :, :],
                                 ffn_W_proj.rearrange("(t p) i -> p t i", p=HALF)).then_inc(ffn_w_loaded, 16)
                    sp.dma_start(a_raw[:, :], ffn_A.rearrange("n r d -> (n r) d")).then_inc(ffn_w_loaded, 16)
                    sp.dma_start(gate_raw[:, :], ffn_W_gate).then_inc(ffn_w_loaded, 16)
                    sp.dma_start(qk_bias_raw[:, :],
                                 ffn_b_qkv[0:2 * DIM].rearrange("(t p) -> t p", p=HALF)).then_inc(ffn_w_loaded, 16)
                    for t in range(6):
                        sp.dma_start(b_raw[:, t, :, :],
                                     ffn_B_lora[:, t * HALF:(t + 1) * HALF, :].rearrange("n p r -> p n r"))\
                            .then_inc(ffn_w_loaded, 16)
                    sp.wait_ge(ffn_rows_loaded, 3 * 16)

                def row(dram):
                    return dram.rearrange("(a d) -> a d", a=1).to_broadcast([P, dram.shape[0]])

                @block.gpsimd
                def _(pool):
                    pool.memset(ident[:, :], 0.0).then_inc(ident_zeroed, 1)
                    pool.memset(eps[:, :], EPS).then_inc(consts_ready, 1)
                    pool.memset(earlier[:, :, :], 1.0).then_inc(ident_zeroed, 1)
                    pool.wait_ge(ident_zeroed, 2)
                    pool.affine_select(out=ident[:, :], in_=ident[:, :], compare_op=ALU.not_equal, fill=1.0,
                                       base=0, pattern=[[-1, P]], channel_multiplier=1).then_inc(ident_ready, 1)
                    pool.affine_select(out=earlier[:, :, :], in_=earlier[:, :, :], compare_op=ALU.is_gt, fill=0.0,
                                       base=0, pattern=[[1, EXPERTS], [-1, EXPERTS]], channel_multiplier=0)\
                        .then_inc(consts_ready, 1)
                    pool.wait_ge(tok_w_loaded, 3 * 16)
                    pool.tensor_tensor(w_tok_g[:, :, :, :].rearrange("p a c m -> p (a c) m"),
                                       w_tok[:, :, :, :].rearrange("p a c m -> p (a c) m"),
                                       ln1_g[:, :, :].rearrange("p a c -> p (a c)").unsqueeze(2)
                                       .to_broadcast([P, CHUNKS, DIM]), ALU.mult).then_inc(w_scaled, 1)
                    for i, (loaded, n) in enumerate(((attn_w_loaded, 2), (ffn_w_loaded, 11))):
                        pool.wait_ge(loaded, n * 16)
                        for o in range(2):
                            last = pool.tensor_copy(
                                proj_parity[i][:, o, :].rearrange("p (e g d) -> p e g d", e=2, d=HEAD),
                                proj_raw[i][:, o, :].rearrange("p (g e d) -> p e g d", e=2, d=HEAD))
                        last.then_inc(parity_ready, 1)
                    pool.wait_ge(h_ready, 1)
                    pool.tensor_tensor(h_plus[:, :, :], h[:, :, :],
                                       attn_bias[:, :].unsqueeze(1).to_broadcast([P, GRID, DIM]), ALU.add)\
                        .then_inc(h_plus_ready, 1)

                @block.vector
                def _(dve):
                    done = [0]

                    def chain(ins):
                        ins.then_inc(dve_step, 1)
                        done[0] += 1
                        dve.wait_ge(dve_step, done[0])

                    for c in range(CHANNELS):
                        dve.wait_ge(pix_loaded[c], 16)
                        for w in range(GRID):
                            last = dve.bn_stats(pix_stats[:, w, 6 * c:6 * c + 6], pixels[:, c, :, w, :])
                    chain(last)
                    for w in range(GRID):
                        last = dve.bn_aggr(mean_var[:, w, :], pix_stats[:, w, :])
                    last.then_inc(var_ready, 1)
                    dve.wait_ge(ident_ready, 1)
                    dve.tensor_tensor(ident_pair[:, :], ident[:, 0:TOKENS], ident[:, TOKENS:P], ALU.add)
                    chain(dve.tensor_reduce(mask_even[:, :],
                                            ident[:, :].rearrange("p (g e d) -> p g e d", e=2, d=HEAD)[:, :, 0, :],
                                            AX.XY, ALU.add))
                    dve.tensor_scalar(mask_odd[:, :], mask_even[:, :], -1.0, 1.0, ALU.mult, ALU.add)

                    def inverse_std(n):
                        dve.wait_ge(std_ready, n)
                        chain(dve.reciprocal(rstd[:, :], std[:, :]))
                        dve.scalar_tensor_tensor(out=shift[:, :], in0=mean_var[:, :, 0], scalar=-1.0,
                                                 in1=rstd[:, :], op0=ALU.mult, op1=ALU.mult)\
                            .then_inc(rstd_ready, 1)
                        dve.wait_ge(rstd_ready, n)

                    inverse_std(1)
                    for w in range(0, GRID, 2):
                        dve.tensor_scalar(patches[:, w, :].rearrange("p (a s) -> p a s", s=PATCH),
                                          pixels[:, :, :, w, :].rearrange("p c r s -> p (c r) s"),
                                          rstd[:, w:w + 1], shift[:, w:w + 1], ALU.mult, ALU.add)\
                            .then_inc(patch_dve, 1)
                    for w in range(1, GRID, 2):
                        dve.wait_ge(patchT_ready, 2 * w + 2)
                        for b in range(2):
                            last = dve.tensor_copy(patchesT[:, w, b * 384:(b + 1) * 384],
                                                   bank[2 * (w % 2) + b][:, 0:384])
                        last.then_inc(patchT_copied[1], 1)
                    dve.wait_ge(bias_row_ready, 1)
                    dve.wait_ge(tok_rows_loaded, 4 * 16)
                    dve.tensor_tensor(tok_bias[:, :], bank[0][:, 0:DIM], tok_bias[:, :], ALU.add)\
                        .then_inc(bias_row_copied, 1)
                    dve.wait_ge(bias_row_copied, 1)
                    for j in range(4):
                        dve.wait_ge(tok_ready, 2 * j + 2)
                        last = dve.tensor_tensor(y[:, 2 * j:2 * j + 2, :],
                                                 bank[4 + j][:, 0:2 * DIM].rearrange("p (w m) -> p w m", w=2),
                                                 tok_bias[:, :].unsqueeze(1).to_broadcast([P, 2, DIM]), ALU.add)
                    chain(last)

                    def norm_stats(src):
                        for w in range(GRID):
                            last = dve.bn_stats(stats[:, w, :], src[:, w, :])
                        chain(last)
                        for w in range(GRID):
                            last = dve.bn_aggr(mean_var[:, w, :], stats[:, w, :])
                        last.then_inc(var_ready, 1)

                    def normalise(dst, src):
                        for w in range(GRID):
                            last = dve.tensor_scalar(dst[:, w, :], src[:, w, :], rstd[:, w:w + 1],
                                                     shift[:, w:w + 1], ALU.mult, ALU.add)
                        return last

                    norm_stats(y)
                    inverse_std(2)
                    chain(normalise(y, y))
                    chain(dve.tensor_tensor(y[:, :, :], y[:, :, :],
                                            ln2_g[:, :].unsqueeze(1).to_broadcast([P, GRID, DIM]), ALU.mult))
                    dve.tensor_tensor(h[:, :, :], y[:, :, :],
                                      ln2_b[:, :].unsqueeze(1).to_broadcast([P, GRID, DIM]), ALU.add)\
                        .then_inc(h_ready, 1)
                    dve.wait_ge(h_ready, 1)
                    norm_stats(h)
                    inverse_std(3)
                    normalise(y, h).then_inc(y_ready, 1)
                    for g in (1, 3):
                        dve.wait_ge(yT_ready, g + 1)
                        dve.tensor_copy(yT_columns(yT, g), transposed_tiles(bank[4 + g])).then_inc(yT_copied, 1)

                @block.scalar
                def _(act):
                    act.dma_start(ln1_g[:, :, :],
                                  tok_ln1_g.rearrange("(a p c) -> p a c", a=2, c=CHANNELS)).then_inc(tok_w_loaded, 16)
                    act.dma_start(ln1_b[:, :, :],
                                  tok_ln1_b.rearrange("(a p c) -> p a c", a=2, c=CHANNELS)).then_inc(tok_w_loaded, 16)
                    act.dma_start(tok_bias[:, :], row(tok_b)).then_inc(tok_rows_loaded, 16)
                    act.dma_start(ln2_g[:, :], row(tok_ln2_g)).then_inc(tok_rows_loaded, 16)
                    act.dma_start(ln2_b[:, :], row(tok_ln2_b)).then_inc(tok_rows_loaded, 16)
                    act.dma_start(attn_bias[:, :], row(attn_b_proj)).then_inc(tok_rows_loaded, 16)
                    act.dma_start(ffn_bias[:, :], row(ffn_b_proj)).then_inc(ffn_rows_loaded, 16)
                    act.dma_start(v_bias[:, :], row(ffn_b_qkv[2 * DIM:3 * DIM])).then_inc(ffn_rows_loaded, 16)
                    act.dma_start(gate_bias[:, :], row(ffn_b_gate)).then_inc(ffn_rows_loaded, 16)

                    def std_of(n):
                        act.wait_ge(var_ready, n)
                        act.wait_ge(consts_ready, 1)
                        act.activation(std[:, :], mean_var[:, :, 1], ACT.Sqrt, bias=eps[:, :])\
                            .then_inc(std_ready, 1)

                    std_of(1)
                    act.wait_ge(rstd_ready, 1)
                    for w in range(1, GRID, 2):
                        act.activation(patches[:, w, :].rearrange("p (a s) -> p a s", s=PATCH),
                                       pixels[:, :, :, w, :].rearrange("p c r s -> p (c r) s"),
                                       ACT.Identity, scale=rstd[:, w:w + 1], bias=shift[:, w:w + 1])\
                            .then_inc(patch_act, 1)
                    for w in range(0, GRID, 2):
                        act.wait_ge(patchT_ready, 2 * w + 2)
                        for b in range(2):
                            last = act.copy(patchesT[:, w, b * 384:(b + 1) * 384],
                                            bank[2 * (w % 2) + b][:, 0:384])
                        last.then_inc(patchT_copied[0], 1)

                    def weights(first, end):
                        for g in range(first, end):
                            ins, rows, dst = w_groups[g]
                            act.wait_ge(wT_ready, g + 1)
                            act.copy(dst, bank[g % 4][0:rows, 0:dst.free_size()]).then_inc(wT_copied, 1)

                    weights(0, 4)
                    std_of(2)
                    weights(4, 9)
                    std_of(3)
                    weights(9, len(w_groups))
                    for g in (0, 2):
                        act.wait_ge(yT_ready, g + 1)
                        act.copy(yT_columns(yT, g), transposed_tiles(bank[4 + g])).then_inc(yT_copied, 1)

                @block.tensor
                def _(pe):
                    pe.wait_ge(ident_ready, 1)

                    def transpose_tile(w):
                        pe.wait_ge(patch_act if w % 2 else patch_dve, w // 2 + 1)
                        if w >= 2:
                            pe.wait_ge(patchT_copied[w % 2], w // 2)
                        for k in range(CHUNKS):
                            t = pe.transpose(bank[2 * (w % 2) + k // 3][:, (k % 3) * P:(k % 3 + 1) * P],
                                             patches[:, w, k * P:(k + 1) * P], ident[:, :])
                            if k % 3 == 2:
                                t.then_inc(patchT_ready, 1)

                    def project_tile(w):
                        pe.wait_ge(patchT_copied[w % 2], w // 2 + 1)
                        dst = bank[4 + w // 2][:, (w % 2) * DIM:(w % 2 + 1) * DIM]
                        for k in range(CHUNKS):
                            t = pe.matmul(dst, patchesT[:, w, k * P:(k + 1) * P], w_tok_g[:, k % 2, k // 2, :],
                                          start=(k == 0), stop=(k == CHUNKS - 1))
                        t.then_inc(tok_ready, 1)

                    transpose_tile(0)
                    transpose_tile(1)
                    pe.wait_ge(w_scaled, 1)
                    for w in range(GRID):
                        project_tile(w)
                        if w + 2 < GRID:
                            transpose_tile(w + 2)
                    for k in range(CHUNKS):
                        t = pe.matmul(bank[0][:, 0:DIM], ln1_b[:, k % 2, k // 2:k // 2 + 1].to_broadcast([P, P]),
                                      w_tok[:, k % 2, k // 2, :], start=(k == 0), stop=(k == CHUNKS - 1))
                    t.then_inc(bias_row_ready, 1)
                    for g, (ins, rows, dst) in enumerate(w_groups):
                        if g == 0:
                            pe.wait_ge(attn_w_loaded, 2 * 16)
                            pe.wait_ge(parity_ready, 1)
                            pe.wait_ge(bias_row_copied, 1)
                        if g == attn_groups:
                            pe.wait_ge(ffn_w_loaded, 11 * 16)
                            pe.wait_ge(parity_ready, 2)
                        if g >= 4:
                            pe.wait_ge(wT_copied, g - 3)
                        at = 0
                        for src in ins:
                            cols = src.shape[0]
                            t = pe.transpose(bank[g % 4][0:rows, at:at + cols], src, ident[0:cols, 0:cols])
                            at += cols
                        t.then_inc(wT_ready, 1)
                    pe.wait_ge(y_ready, 1)
                    for g in range(4):
                        for w in range(4):
                            t = pe.transpose(bank[4 + g][0:HALF, w * P:(w + 1) * P],
                                             y[:, 4 * (g // 2) + w, (g % 2) * HALF:(g % 2 + 1) * HALF], ident[:, :])
                        t.then_inc(yT_ready, 1)

        yT_round = sb("yT_round", [HALF, 2, QUAD, 2, TOKENS])
        loraT_round = sb("loraT_round", [LORA, QUAD, 2, TOKENS])
        q_round = sb("q_round", [HALF, 2, ROUND_TOKENS])
        k_round = sb("k_round", [HALF, 2, 2, ROUND_TOKENS])
        v_round = sb("v_round", [P, QUAD, DIM])
        row_max = sb("row_max", [P, GROUPS, BLOCKS])
        row_sum = sb("row_sum", [P, GROUPS, BLOCKS])
        row_inv = sb("row_inv", [P, GROUPS, BLOCKS])
        expd = sb("expd", [P, GROUPS, BLOCKS, TOKENS])
        probs = sb("probs", [P, GROUPS, BLOCKS, TOKENS])
        probsT = sb("probsT", [P, GROUPS, BLOCKS, TOKENS])
        probsT_scaled = sb("probsT_scaled", [P, GROUPS, BLOCKS, TOKENS])
        col_sum = sb("col_sum", [P, GROUPS, BLOCKS])
        neg_max = sb("neg_max", [BLOCKS, GROUPS, 2])
        neg_inv = sb("neg_inv", [BLOCKS, GROUPS, 2, TOKENS])
        neg_inv_all = sb("neg_inv_all", [P, GROUPS, BLOCKS])
        resid = sb("resid", [P, GROUPS, BLOCKS, TOKENS])
        square = sb("square", [P, GROUPS, BLOCKS, TOKENS])
        step = sb("step", [P, GROUPS, BLOCKS, TOKENS])
        kv = sb("kv", [P, GROUPS, BLOCKS, HEAD])
        step_kv = sb("step_kv", [P, GROUPS, BLOCKS, HEAD])
        mixed = sb("mixed", [P, QUAD, PAIRS, HEAD])
        logits = sb("logits", [P, GRID, EXPERTS])
        route_max = sb("route_max", [P, GRID])
        route_sum = sb("route_sum", [P, GRID])
        route_exp = sb("route_exp", [P, GRID, EXPERTS])
        route = sb("route", [P, GRID, EXPERTS])
        beaten = sb("beaten", [P, GRID, EXPERTS, EXPERTS])
        tied = sb("tied", [P, GRID, EXPERTS, EXPERTS])
        rank = sb("rank", [P, GRID, EXPERTS])
        dispatch = sb("dispatch", [P, GRID, EXPERTS])
        lora = sb("lora", [P, GRID, LORA])

        tokens_ready = sem("tokens_ready")
        q_ready, k_ready, v_ready = sem("q_ready"), sem("k_ready"), sem("v_ready")
        q_copied, k_even_copied, k_odd_copied = sem("q_copied"), sem("k_even_copied"), sem("k_odd_copied")
        v_copied = sem("v_copied")
        scores_ready = sems("scores_ready")
        max_ready = sems("max_ready")
        shifted = sems("shifted")
        exp_ready = sems("exp_ready")
        sum_ready = sems("sum_ready")
        inv_ready = sems("inv_ready")
        probs_ready = sems("probs_ready")
        probsT_ready = sems("probsT_ready")
        probsT_copied = sems("probsT_copied")
        col_sum_ready = sems("col_sum_ready")
        col_sumT_ready = sems("col_sumT_ready")
        neg_max_ready = sems("neg_max_ready")
        neg_inv_ready = sems("neg_inv_ready")
        neg_inv_spread = sems("neg_inv_spread")
        neg_inv_copied = sems("neg_inv_copied")
        probsT_scaled_ready = sems("probsT_scaled_ready")
        gram_ready = sems("gram_ready")
        kv_ready = sems("kv_ready")
        kv_copied = sems("kv_copied")
        first_resid_ready = sems("first_resid_ready")
        square_ready = sems("square_ready")
        square_copied = sems("square_copied")
        step_ready = sems("step_ready")
        resid_ready = sems("resid_ready")
        resid_copied = sems("resid_copied")
        step_kv_ready = sems("step_kv_ready")
        step_kv_copied = sems("step_kv_copied")
        tail_ready = sems("tail_ready")
        mixed_ready = sem("mixed_ready")
        mixedT_ready = sem("mixedT_ready")
        mixedT_copied = sem("mixedT_copied")
        round_sems = range(tokens_ready.num, mixedT_copied.num + 1)

        Q_BANK, K_BANK, V_BANK = bank[6], bank[7], (bank[3], bank[4])

        def first(c):
            return bank[c]

        def second(c):
            return bank[3 + c]

        def blocks(ap):
            return ap.rearrange("p (n t) -> p n t", t=TOKENS)

        def chunk_blocks(c):
            for n in range(BLOCKS):
                image_pair, half, image = n // 4, n // 2 % 2, n % 2
                b = 2 * image_pair + image
                yield n, b, GROUPS * half + c, (2 * b + half) * HEAD

        def project_q_k(pe, weights, lora_on):
            for dst, ready, at in ((Q_BANK, q_ready, 0), (K_BANK, k_ready, DIM)):
                for m in range(2):
                    o = at + m * HALF
                    for kc in range(2):
                        t = pe.matmul(dst[0:HALF, m * ROUND_TOKENS:(m + 1) * ROUND_TOKENS],
                                      weights[:, kc, o:o + HALF], yT_round[:, kc, :, 0, :],
                                      start=(kc == 0), stop=(kc == 1 and not lora_on))
                    if lora_on:
                        t = pe.matmul(dst[0:HALF, m * ROUND_TOKENS:(m + 1) * ROUND_TOKENS],
                                      bT[:, o:o + HALF], loraT_round[:, :, 0, :], start=False, stop=True)
                t.then_inc(ready, 1)

        def project_v(pe, weights, lora_on):
            for b in range(QUAD):
                dst = V_BANK[b // 2][:, (b % 2) * DIM:(b % 2 + 1) * DIM]
                for kc in range(2):
                    t = pe.matmul(dst, yT_round[:, kc, b, :, :].rearrange("p r t -> p (r t)"),
                                  weights[:, kc, 2 * DIM:3 * DIM], start=(kc == 0),
                                  stop=(kc == 1 and not lora_on))
                if lora_on:
                    t = pe.matmul(dst, loraT_round[:, b, :, :].rearrange("p r t -> p (r t)"),
                                  bT[:, 2 * DIM:3 * DIM], start=False, stop=True)
                if b % 2:
                    t.then_inc(v_ready, 1)

        def scores(pe, c):
            rows = slice(32 * c, 32 * c + 32)
            for slot in range(SLOTS):
                image_pair, half = slot // 2, slot % 2
                for image in range(2):
                    cols = slice((2 * image_pair + image) * TOKENS, (2 * image_pair + image + 1) * TOKENS)
                    t = pe.matmul(first(c)[halves[image], slot * P:(slot + 1) * P],
                                  q_round[rows, half, cols], k_round[rows, :, half, cols],
                                  start=True, stop=True)
            t.then_inc(scores_ready[c], 1)

        def transpose_probs(pe, c):
            pe.wait_ge(probs_ready[c], 1)
            if c < 2:
                pe.wait_ge(v_copied, 2)
            for slot in range(SLOTS):
                t = pe.transpose(second(c)[:, slot * P:(slot + 1) * P],
                                 probs[:, c, 2 * slot:2 * slot + 2, :].rearrange("p n t -> p (n t)"), ident[:, :])
            t.then_inc(probsT_ready[c], 1)

        def head_matmuls(pe, dst, lhsT, rhs_of, width, c):
            for n, b, pair, narrow in chunk_blocks(c):
                for e in range(2):
                    at = n * TOKENS if width == TOKENS else narrow
                    t = pe.matmul(dst[halves[e], at:at + width], lhsT[halves[e], c, n, :],
                                  rhs_of(e, n, b, pair, narrow), start=True, stop=True)
            return t

        def v_of(e, n, b, pair, narrow):
            head = 2 * pair + e
            return v_round[halves[e], b, head * HEAD:(head + 1) * HEAD]

        def kv_of(src, c):
            flat = src[:, c, :, :].rearrange("p n d -> p (n d)")
            return lambda e, n, b, pair, at: flat[halves[e], at:at + HEAD]

        def transpose_mixed(pe):
            pe.wait_ge(mixed_ready, GROUPS)
            for b in range(QUAD):
                t = pe.transpose(Q_BANK[0:HALF, b * P:(b + 1) * P],
                                 mixed[:, b, :, :].rearrange("p g d -> p (g d)"), ident[:, :])
            t.then_inc(mixedT_ready, 1)

        def shift_scores(dve, c):
            dve.wait_ge(scores_ready[c], 1)
            dve.tensor_reduce(row_max[:, c, :], blocks(first(c)[:, :]), AX.X, ALU.max).then_inc(max_ready[c], 1)
            dve.wait_ge(max_ready[c], 1)
            dve.tensor_tensor(expd[:, c, :, :], blocks(first(c)[:, :]),
                              row_max[:, c, :].unsqueeze(2).to_broadcast([P, BLOCKS, TOKENS]), ALU.subtract)\
                .then_inc(shifted[c], 1)

        def exponentiate(act, c):
            act.wait_ge(shifted[c], 1)
            act.activation(expd[:, c, :, :], expd[:, c, :, :], ACT.Exp, scale=SCALE).then_inc(exp_ready[c], 1)

        def invert_sums(dve, c):
            dve.wait_ge(exp_ready[c], 1)
            dve.tensor_reduce(row_sum[:, c, :], expd[:, c, :, :], AX.X, ALU.add).then_inc(sum_ready[c], 1)
            dve.wait_ge(sum_ready[c], 1)
            dve.reciprocal(row_inv[:, c, :], row_sum[:, c, :]).then_inc(inv_ready[c], 1)

        def normalise_rows(pool, c):
            pool.wait_ge(inv_ready[c], 1)
            pool.tensor_tensor(probs[:, c, :, :], expd[:, c, :, :],
                               row_inv[:, c, :].unsqueeze(2).to_broadcast([P, BLOCKS, TOKENS]), ALU.mult)\
                .then_inc(probs_ready[c], 1)

        def mixed_of(c):
            return mixed[:, :, :, :].rearrange("p b (m g) d -> p b m g d", m=2)[:, :, :, c, :]

        def round_mixedT(q, e):
            return mixedT[:, e, :, bass.ds(q * QUAD * GRID, QUAD * GRID)].rearrange("p w (b h) -> p w b h", b=QUAD)

        def mixedT_psum(e):
            return Q_BANK[0:HALF, :].rearrange("p (b e w h) -> p e w b h", b=QUAD, e=2, w=GRID)[:, e, :, :, :]

        def narrow(ap):
            return ap.rearrange("p (b m d) -> p b m d", m=2, d=HEAD)

        def narrow_sb(ap):
            return ap.rearrange("p (b m) d -> p b m d", m=2)

        with nc.Fori(0, ROUNDS) as q:
            with nc.Block(no_gpsimd_drain=True) as block:
                @block.tensor
                def _(pe):
                    pe.wait_ge(tokens_ready, 2)
                    project_q_k(pe, wT[0], False)
                    project_v(pe, wT[0], False)
                    pe.wait_ge(q_copied, 1)
                    pe.wait_ge(k_even_copied, 1)
                    pe.wait_ge(k_odd_copied, 1)
                    for c in range(GROUPS):
                        scores(pe, c)
                    for c in range(GROUPS):
                        transpose_probs(pe, c)
                    for c in range(GROUPS):
                        pe.wait_ge(col_sum_ready[c], 1)
                        pe.transpose(first(c)[0:BLOCKS, 0:P], col_sum[:, c, :], ident[:, :])\
                            .then_inc(col_sumT_ready[c], 1)
                    for c in range(GROUPS):
                        pe.wait_ge(probsT_copied[c], 1)
                        head_matmuls(pe, second(c), probsT, v_of, HEAD, c).then_inc(kv_ready[c], 1)
                    for c in range(GROUPS):
                        pe.wait_ge(neg_inv_ready[c], 1)
                        pe.matmul(first(c)[:, P:P + BLOCKS],
                                  neg_inv[:, c, :, :].rearrange("p e t -> p (e t)"),
                                  ident[0:BLOCKS, 0:BLOCKS], start=True, stop=True).then_inc(neg_inv_spread[c], 1)
                    for c in range(GROUPS):
                        pe.wait_ge(probsT_scaled_ready[c], 1)
                        head_matmuls(pe, first(c), probsT,
                                     lambda e, n, b, pair, at: probsT_scaled[halves[e], c, n, :], TOKENS, c)\
                            .then_inc(gram_ready[c], 1)
                    for t in range(STEPS):
                        for c in range(GROUPS):
                            if t == 0:
                                pe.wait_ge(first_resid_ready[c], 1)
                                pe.wait_ge(kv_copied[c], 1)
                            else:
                                pe.wait_ge(resid_copied[c], t)
                            head_matmuls(pe, second(c), resid,
                                         lambda e, n, b, pair, at: resid[halves[e], c, n, :], TOKENS, c)\
                                .then_inc(square_ready[c], 1)
                        if t == STEPS - 1:
                            break
                        for c in range(GROUPS):
                            pe.wait_ge(square_copied[c], t + 1)
                            pe.wait_ge(step_ready[c], t + 1)
                            head_matmuls(pe, first(c), square,
                                         lambda e, n, b, pair, at: step[halves[e], c, n, :], TOKENS, c)\
                                .then_inc(resid_ready[c], 1)
                    for c in range(GROUPS):
                        pe.wait_ge(step_ready[c], STEPS)
                        head_matmuls(pe, first(c), step, kv_of(kv, c), HEAD, c).then_inc(step_kv_ready[c], 1)
                    for c in range(GROUPS):
                        pe.wait_ge(square_copied[c], STEPS)
                        pe.wait_ge(step_kv_copied[c], 1)
                        head_matmuls(pe, second(c), square, kv_of(step_kv, c), HEAD, c)\
                            .then_inc(tail_ready[c], 1)
                    transpose_mixed(pe)

                @block.vector
                def _(dve):
                    for kc in range(2):
                        dve.tensor_copy(yT_round[:, kc, :, :, :], twice(yT[:, kc, :], q)).then_inc(tokens_ready, 1)
                    dve.wait_ge(k_ready, 1)
                    dve.tensor_scalar(k_round[:, 0, :, :].rearrange("p m t -> p (m t)"), K_BANK[0:HALF, :],
                                      mask_even[0:HALF, :], None, ALU.mult).then_inc(k_even_copied, 1)
                    for c in range(GROUPS):
                        shift_scores(dve, c)
                    for c in range(GROUPS):
                        invert_sums(dve, c)
                    for c in range(GROUPS):
                        dve.wait_ge(probsT_copied[c], 1)
                        dve.tensor_reduce(col_sum[:, c, :], probsT[:, c, :, :], AX.X, ALU.add)\
                            .then_inc(col_sum_ready[c], 1)
                    for c in range(GROUPS):
                        dve.wait_ge(col_sumT_ready[c], 1)
                        dve.tensor_reduce(neg_max[:, c, :], blocks(first(c)[0:BLOCKS, 0:P]), AX.X, ALU.max,
                                          negate=True).then_inc(neg_max_ready[c], 1)
                        dve.wait_ge(neg_max_ready[c], 1)
                        dve.reciprocal(neg_inv[:, c, :, :],
                                       neg_max[:, c, :].unsqueeze(2).to_broadcast([BLOCKS, 2, TOKENS])).then_inc(neg_inv_ready[c], 1)
                    for c in range(GROUPS):
                        dve.wait_ge(neg_inv_spread[c], 1)
                        dve.tensor_copy(neg_inv_all[:, c, :], first(c)[:, P:P + BLOCKS])\
                            .then_inc(neg_inv_copied[c], 1)
                    for c in range(GROUPS):
                        dve.wait_ge(gram_ready[c], 1)
                        dve.tensor_tensor(resid[:, c, :, :], blocks(first(c)[:, :]),
                                          ident_pair[:, :].unsqueeze(1).to_broadcast([P, BLOCKS, TOKENS]), ALU.add)\
                            .then_inc(first_resid_ready[c], 1)
                    for t in range(STEPS):
                        for c in range(GROUPS):
                            dve.wait_ge(square_copied[c], t + 1)
                            dve.scalar_tensor_tensor(out=step[:, c, :, :], in0=resid[:, c, :, :], scalar=3.0,
                                                     in1=square[:, c, :, :], op0=ALU.mult, op1=ALU.add)\
                                .then_inc(step_ready[c], 1)
                    for c in range(GROUPS):
                        dve.wait_ge(tail_ready[c], 1)
                        dve.tensor_tensor(mixed_of(c), narrow_sb(kv[:, c, :, :]),
                                          narrow(second(c)[:, 0:BLOCKS * HEAD]), ALU.subtract)\
                            .then_inc(mixed_ready, 1)

                @block.scalar
                def _(act):
                    act.wait_ge(q_ready, 1)
                    act.copy(q_round[:, :, :].rearrange("p m t -> p (m t)"), Q_BANK[0:HALF, :]).then_inc(q_copied, 1)
                    act.wait_ge(k_ready, 1)
                    act.wait_ge(k_even_copied, 1)
                    act.activation(k_round[:, 1, :, :].rearrange("p m t -> p (m t)"), K_BANK[0:HALF, :],
                                   ACT.Copy, scale=mask_odd[0:HALF, :]).then_inc(k_odd_copied, 1)
                    for j in range(2):
                        act.wait_ge(v_ready, j + 1)
                        act.copy(v_round[:, 2 * j:2 * j + 2, :].rearrange("p b m -> p (b m)"),
                                 V_BANK[j][:, 0:2 * DIM]).then_inc(v_copied, 1)
                    for c in range(GROUPS):
                        exponentiate(act, c)
                    for c in range(GROUPS):
                        act.wait_ge(probsT_ready[c], 1)
                        act.copy(probsT[:, c, :, :], blocks(second(c)[:, :])).then_inc(probsT_copied[c], 1)
                    for c in range(GROUPS):
                        act.wait_ge(kv_ready[c], 1)
                        act.copy(kv[:, c, :, :].rearrange("p n d -> p (n d)"), second(c)[:, 0:BLOCKS * HEAD])\
                            .then_inc(kv_copied[c], 1)
                    for t in range(STEPS):
                        for c in range(GROUPS):
                            act.wait_ge(square_ready[c], t + 1)
                            act.copy(square[:, c, :, :], blocks(second(c)[:, :])).then_inc(square_copied[c], 1)
                        if t == STEPS - 1:
                            break
                        for c in range(GROUPS):
                            act.wait_ge(resid_ready[c], t + 1)
                            act.mul(resid[:, c, :, :], blocks(first(c)[:, :]), 0.25).then_inc(resid_copied[c], 1)
                    for c in range(GROUPS):
                        act.wait_ge(step_kv_ready[c], 1)
                        act.mul(step_kv[:, c, :, :].rearrange("p n d -> p (n d)"),
                                first(c)[:, 0:BLOCKS * HEAD], 0.25).then_inc(step_kv_copied[c], 1)
                    act.wait_ge(mixedT_ready, 1)
                    for e in range(2):
                        act.copy(round_mixedT(q, e), mixedT_psum(e)).then_inc(mixedT_copied, 1)

                @block.gpsimd
                def _(pool):
                    for c in range(GROUPS):
                        normalise_rows(pool, c)
                    for c in range(GROUPS):
                        pool.wait_ge(probsT_copied[c], 1)
                        pool.wait_ge(neg_inv_copied[c], 1)
                        pool.tensor_tensor(probsT_scaled[:, c, :, :], probsT[:, c, :, :],
                                           neg_inv_all[:, c, :].unsqueeze(2).to_broadcast([P, BLOCKS, TOKENS]),
                                           ALU.mult).then_inc(probsT_scaled_ready[c], 1)
            nc.all_engine_barrier(sems_to_clear=round_sems)

        def project_out(pe, i, ready):
            for w in range(GRID):
                for e in range(2):
                    t = pe.matmul(bank[w // 2][:, (w % 2) * DIM:(w % 2 + 1) * DIM], mixedT[:, e, w, :],
                                  projT[i][:, e, :], start=(e == 0), stop=(e == 1))
                t.then_inc(ready, 1)

        with ExitStack() as stage:
            def sem_b(name):
                return stage.enter_context(nc.semaphore(name))

            proj_ready = sem_b("proj_ready")
            dve_step_b = sem_b("dve_step_b")
            h_ready_b = sem_b("h_ready_b")
            h_plus_b = sem_b("h_plus_b")
            var_b = sem_b("var_b")
            std_b = sem_b("std_b")
            y_b = sem_b("y_b")
            yT_b = sem_b("yT_b")
            yT_even = sem_b("yT_even")
            yT_odd = sem_b("yT_odd")
            gate_ready = sem_b("gate_ready")
            route_shifted = sem_b("route_shifted")
            route_exped = sem_b("route_exped")
            lora_ready = sem_b("lora_ready")
            loraT_ready = sem_b("loraT_ready")
            loraT_copied = sem_b("loraT_copied")
            PER_BANK = 3
            WIDE = LORA + EXPERTS

            def gate_tiles(j):
                n = min(PER_BANK, GRID - PER_BANK * j)
                return slice(PER_BANK * j, PER_BANK * j + n), n, \
                    bank[4 + j][:, 0:n * WIDE].rearrange("p (t e) -> p t e", e=WIDE)

            with nc.Block() as block:
                @block.tensor
                def _(pe):
                    project_out(pe, 0, proj_ready)
                    pe.wait_ge(y_b, 1)
                    for g in range(4):
                        for w in range(4):
                            t = pe.transpose(bank[4 + g][0:HALF, w * P:(w + 1) * P],
                                             y[:, 4 * (g // 2) + w, (g % 2) * HALF:(g % 2 + 1) * HALF], ident[:, :])
                        t.then_inc(yT_b, 1)
                    pe.wait_ge(yT_even, 2)
                    pe.wait_ge(yT_odd, 2)
                    for t in range(GRID):
                        for kc in range(2):
                            m = pe.matmul(bank[4 + t // PER_BANK][:, (t % PER_BANK) * WIDE:(t % PER_BANK + 1) * WIDE],
                                          yT[:, kc, t * P:(t + 1) * P], aT_gate[:, kc, :],
                                          start=(kc == 0), stop=(kc == 1))
                        m.then_inc(gate_ready, 1)
                    for j in range(3):
                        pe.wait_ge(lora_ready, j + 1)
                        tiles = gate_tiles(j)[0]
                        for t in range(tiles.start, tiles.stop):
                            pe.transpose(bank[t // 4][:, (t % 4) * P:(t % 4 + 1) * P], lora[:, t, :], ident[:, :])\
                                .then_inc(loraT_ready, 1)

                @block.vector
                def _(dve):
                    done = [0]

                    def chain(ins):
                        ins.then_inc(dve_step_b, 1)
                        done[0] += 1
                        dve.wait_ge(dve_step_b, done[0])

                    dve.tensor_scalar(k_bias_odd[:, :], qk_bias[:, 2:4], mask_odd[0:HALF, :], None, ALU.mult)
                    for j in range(4):
                        dve.wait_ge(proj_ready, 2 * j + 2)
                        chain(dve.tensor_tensor(h[:, 2 * j:2 * j + 2, :],
                                                bank[j][:, 0:2 * DIM].rearrange("p (w m) -> p w m", w=2),
                                                h_plus[:, 2 * j:2 * j + 2, :], ALU.add))
                        for w in (2 * j, 2 * j + 1):
                            last = dve.bn_stats(stats[:, w, :], h[:, w, :])
                    last.then_inc(h_ready_b, 1)
                    dve.wait_ge(h_ready_b, 1)
                    for w in range(GRID):
                        last = dve.bn_aggr(mean_var[:, w, :], stats[:, w, :])
                    last.then_inc(var_b, 1)
                    dve.wait_ge(std_b, 1)
                    chain(dve.reciprocal(rstd[:, :], std[:, :]))
                    chain(dve.scalar_tensor_tensor(out=shift[:, :], in0=mean_var[:, :, 0], scalar=-1.0,
                                                   in1=rstd[:, :], op0=ALU.mult, op1=ALU.mult))
                    for w in range(GRID):
                        last = dve.tensor_scalar(y[:, w, :], h[:, w, :], rstd[:, w:w + 1], shift[:, w:w + 1],
                                                 ALU.mult, ALU.add)
                    last.then_inc(y_b, 1)
                    for g in (1, 3):
                        dve.wait_ge(yT_b, g + 1)
                        dve.tensor_copy(yT_columns(yT, g), transposed_tiles(bank[4 + g])).then_inc(yT_odd, 1)
                    for j in range(3):
                        tiles, n, prod = gate_tiles(j)
                        dve.wait_ge(gate_ready, tiles.stop)
                        last = dve.tensor_tensor(logits[:, tiles, :], prod[:, :, LORA:WIDE],
                                                 gate_bias[:, :].unsqueeze(1).to_broadcast([P, n, EXPERTS]), ALU.add)
                    chain(last)
                    spread = [P, GRID, EXPERTS]
                    chain(dve.tensor_reduce(route_max[:, :], logits[:, :, :], AX.X, ALU.max))
                    dve.tensor_tensor(route_exp[:, :, :], logits[:, :, :],
                                      route_max[:, :].unsqueeze(2).to_broadcast(spread), ALU.subtract)\
                        .then_inc(route_shifted, 1)
                    dve.wait_ge(route_exped, 1)
                    chain(dve.tensor_reduce(route_sum[:, :], route_exp[:, :, :], AX.X, ALU.add))
                    chain(dve.reciprocal(route_max[:, :], route_sum[:, :]))
                    chain(dve.tensor_tensor(route[:, :, :], route_exp[:, :, :],
                                            route_max[:, :].unsqueeze(2).to_broadcast(spread), ALU.mult))
                    cube = [P, GRID, EXPERTS, EXPERTS]
                    other = route[:, :, :].unsqueeze(2).to_broadcast(cube)
                    own = route[:, :, :].unsqueeze(3).to_broadcast(cube)
                    dve.tensor_tensor(beaten[:, :, :, :], other, own, ALU.is_gt)
                    chain(dve.tensor_tensor(tied[:, :, :, :], other, own, ALU.is_equal))
                    chain(dve.tensor_tensor(tied[:, :, :, :], tied[:, :, :, :],
                                            earlier[:, :, :].unsqueeze(1).to_broadcast(cube), ALU.mult))
                    chain(dve.tensor_tensor(beaten[:, :, :, :], beaten[:, :, :, :], tied[:, :, :, :], ALU.add))
                    chain(dve.tensor_reduce(rank[:, :, :], beaten[:, :, :, :], AX.X, ALU.add))
                    chain(dve.tensor_scalar(rank[:, :, :], rank[:, :, :], TOP - 0.5, LORA_SCALE,
                                            ALU.is_lt, ALU.mult))
                    chain(dve.tensor_tensor(dispatch[:, :, :], rank[:, :, :], route[:, :, :], ALU.mult))
                    for j in range(3):
                        tiles, n, prod = gate_tiles(j)
                        dve.tensor_tensor(lora[:, tiles, :].rearrange("p t (e r) -> p t e r", r=RANK),
                                          prod[:, :, 0:LORA].rearrange("p t (e r) -> p t e r", r=RANK),
                                          dispatch[:, tiles, :].unsqueeze(3).to_broadcast([P, n, EXPERTS, RANK]),
                                          ALU.mult).then_inc(lora_ready, 1)
                    dve.wait_ge(loraT_ready, 8)
                    dve.tensor_copy(loraT[:, BANK:2 * BANK], bank[1][:, :]).then_inc(loraT_copied, 1)

                @block.scalar
                def _(act):
                    act.wait_ge(var_b, 1)
                    act.activation(std[:, :], mean_var[:, :, 1], ACT.Sqrt, bias=eps[:, :]).then_inc(std_b, 1)
                    for g in (0, 2):
                        act.wait_ge(yT_b, g + 1)
                        act.copy(yT_columns(yT, g), transposed_tiles(bank[4 + g])).then_inc(yT_even, 1)
                    act.wait_ge(route_shifted, 1)
                    act.activation(route_exp[:, :, :], route_exp[:, :, :], ACT.Exp).then_inc(route_exped, 1)
                    act.wait_ge(loraT_ready, 4)
                    act.copy(loraT[:, 0:BANK], bank[0][:, :]).then_inc(loraT_copied, 1)

                @block.gpsimd
                def _(pool):
                    pool.wait_ge(h_ready_b, 1)
                    pool.tensor_tensor(h_plus[:, :, :], h[:, :, :],
                                       ffn_bias[:, :].unsqueeze(1).to_broadcast([P, GRID, DIM]), ALU.add)\
                        .then_inc(h_plus_b, 1)

        with nc.Fori(0, ROUNDS) as q:
            with nc.Block(no_gpsimd_drain=True) as block:
                @block.tensor
                def _(pe):
                    pe.wait_ge(tokens_ready, 3)
                    project_q_k(pe, wT[1], True)
                    project_v(pe, wT[1], True)
                    pe.wait_ge(q_copied, 1)
                    pe.wait_ge(k_even_copied, 1)
                    pe.wait_ge(k_odd_copied, 1)
                    for c in range(GROUPS):
                        scores(pe, c)
                    for c in range(GROUPS):
                        transpose_probs(pe, c)
                    for c in range(GROUPS):
                        pe.wait_ge(probsT_copied[c], 1)
                        head_matmuls(pe, first(c), probsT, v_of, HEAD, c).then_inc(kv_ready[c], 1)
                    transpose_mixed(pe)

                @block.vector
                def _(dve):
                    for kc in range(2):
                        dve.tensor_copy(yT_round[:, kc, :, :, :], twice(yT[:, kc, :], q)).then_inc(tokens_ready, 1)
                    dve.tensor_copy(loraT_round[:, :, :, :], twice(loraT[:, :], q)).then_inc(tokens_ready, 1)
                    dve.wait_ge(k_ready, 1)
                    for m in range(2):
                        last = dve.tensor_scalar(k_round[:, 0, m, :],
                                                 K_BANK[0:HALF, m * ROUND_TOKENS:(m + 1) * ROUND_TOKENS],
                                                 qk_bias[:, 2 + m:3 + m], mask_even[0:HALF, :], ALU.add, ALU.mult)
                    last.then_inc(k_even_copied, 1)
                    for j in range(2):
                        dve.wait_ge(v_ready, j + 1)
                        dve.tensor_tensor(v_round[:, 2 * j:2 * j + 2, :],
                                          V_BANK[j][:, 0:2 * DIM].rearrange("p (b m) -> p b m", b=2),
                                          v_bias[:, :].unsqueeze(1).to_broadcast([P, 2, DIM]), ALU.add)\
                            .then_inc(v_copied, 1)
                    for c in range(GROUPS):
                        shift_scores(dve, c)
                    for c in range(GROUPS):
                        invert_sums(dve, c)
                    for c in range(GROUPS):
                        dve.wait_ge(kv_ready[c], 1)
                        dve.tensor_copy(mixed_of(c), narrow(first(c)[:, 0:BLOCKS * HEAD])).then_inc(mixed_ready, 1)

                @block.scalar
                def _(act):
                    act.wait_ge(q_ready, 1)
                    for m in range(2):
                        last = act.activation(q_round[:, m, :],
                                              Q_BANK[0:HALF, m * ROUND_TOKENS:(m + 1) * ROUND_TOKENS],
                                              ACT.Identity, bias=qk_bias[:, m:m + 1])
                    last.then_inc(q_copied, 1)
                    act.wait_ge(k_ready, 1)
                    act.wait_ge(k_even_copied, 1)
                    for m in range(2):
                        last = act.activation(k_round[:, 1, m, :],
                                              K_BANK[0:HALF, m * ROUND_TOKENS:(m + 1) * ROUND_TOKENS],
                                              ACT.Identity, scale=mask_odd[0:HALF, :], bias=k_bias_odd[:, m:m + 1])
                    last.then_inc(k_odd_copied, 1)
                    for c in range(GROUPS):
                        exponentiate(act, c)
                    for c in range(GROUPS):
                        act.wait_ge(probsT_ready[c], 1)
                        act.copy(probsT[:, c, :, :], blocks(second(c)[:, :])).then_inc(probsT_copied[c], 1)
                    act.wait_ge(mixedT_ready, 1)
                    for e in range(2):
                        act.copy(round_mixedT(q, e), mixedT_psum(e)).then_inc(mixedT_copied, 1)

                @block.gpsimd
                def _(pool):
                    for c in range(GROUPS):
                        normalise_rows(pool, c)
            nc.all_engine_barrier(sems_to_clear=round_sems)

        final_ready = sem("final_ready")
        final_summed = sem("final_summed")
        stored = sem("stored")
        with nc.Block() as block:
            @block.tensor
            def _(pe):
                project_out(pe, 1, final_ready)

            @block.vector
            def _(dve):
                for j in range(4):
                    dve.wait_ge(final_ready, 2 * j + 2)
                    dve.tensor_tensor(y[:, 2 * j:2 * j + 2, :],
                                      bank[j][:, 0:2 * DIM].rearrange("p (w m) -> p w m", w=2),
                                      h_plus[:, 2 * j:2 * j + 2, :], ALU.add).then_inc(final_summed, 1)

            @block.sync
            def _(sp):
                rows = out.rearrange("b (h w) c -> (b h) w c", w=GRID)
                for j in range(4):
                    sp.wait_ge(final_summed, j + 1)
                    sp.dma_start(rows[:, 2 * j:2 * j + 2, :], y[:, 2 * j:2 * j + 2, :]).then_inc(stored, 16)
                sp.wait_ge(stored, 4 * 16)


def twice(columns, q):
    ap = columns[:, bass.ds(q * ROUND_TOKENS, ROUND_TOKENS)].rearrange("p (b t) -> p b t", b=QUAD)
    return ap.unsqueeze(2).to_broadcast([ap.shape[0], QUAD, 2, TOKENS])


def x_channel(x, c):
    return x.rearrange("b c (h r) w -> c b h (r w)", r=PATCH)[c]


def transposed_tiles(b):
    return b[0:HALF, :].rearrange("p (w b h) -> p w b h", w=4, h=GRID)


def yT_columns(yT, g):
    first = 4 * (g // 2)
    return yT[:, g % 2, :].rearrange("p (b w h) -> p w b h", w=GRID, h=GRID)[:, first:first + 4, :, :]


_INS = ['x', 'L0_tok_ln1_g', 'L0_tok_ln1_b', 'L0_tok_W', 'L0_tok_b', 'L0_tok_ln2_g', 'L0_tok_ln2_b',
        'L0_attn_w_qkv', 'L0_attn_w_proj', 'L0_attn_b_proj', 'L0_ffn_W_qkv', 'L0_ffn_b_qkv',
        'L0_ffn_W_gate', 'L0_ffn_b_gate', 'L0_ffn_A', 'L0_ffn_B_lora', 'L0_ffn_W_proj', 'L0_ffn_b_proj']
_OUTS = [((IMAGES, TOKENS, DIM), 'float32')]


def kernel(**inputs):
    import numpy as _np
    import concourse.bacc as _bacc
    from concourse import mybir as _mybir
    from concourse.bass_utils import run_bass_kernel_spmd as _run

    nc = _bacc.Bacc("TRN2", target_bir_lowering=False, num_devices=1)
    arrays, args = {}, []
    for name in _INS:
        a = _np.ascontiguousarray(inputs[name])
        arrays[f"in_{name}_dram"] = a
        args.append(nc.dram_tensor(f"in_{name}_dram", a.shape, _mybir.dt.from_np(a.dtype), kind="ExternalInput").ap())
    for i, (shape, dtype) in enumerate(_OUTS):
        dt = _mybir.dt.from_np(_np.dtype(dtype))
        args.append(nc.dram_tensor(f"out_{i}_dram", shape, dt, kind="ExternalOutput").ap())
    vit_tower_kernel(nc, *args)
    r = _run(nc, [arrays], core_ids=[0])
    return r.results[0]["out_0_dram"]
```

```python
from contextlib import ExitStack

import concourse.bass as bass
from concourse import mybir

F32 = mybir.dt.float32
ALU = mybir.AluOpType
ACT = mybir.ActivationFunctionType
AX = mybir.AxisListType

P = 128
IMAGES, CHANNELS, SIDE, PATCH = 16, 3, 128, 16
GRID = SIDE // PATCH
TOKENS = GRID * GRID
PIXELS = PATCH * PATCH * CHANNELS
DIM, HEADS = 192, 12
HEAD = DIM // HEADS
HALF = DIM // 2
GROUPS = 3
PAIRS = HEADS // 2
EXPERTS, RANK = 8, 16
LORA = EXPERTS * RANK
LORA_SCALE = 2.0
TOP = 2
EPS = 1e-5
STEPS = 6
SCALE = float(HEAD) ** -0.5
CHUNKS = PIXELS // P
BANK = 512
QUAD = 4
ROUNDS = IMAGES // QUAD
ROUND_TOKENS = QUAD * TOKENS
BLOCKS = 8
GRAM_V = TOKENS + HEAD
PER_GRAM_BANK = BANK // GRAM_V
GRAM_BANKS = GROUPS * BLOCKS // PER_GRAM_BANK
SLOTS = 4


def vit_tower_kernel(nc, x, tok_ln1_g, tok_ln1_b, tok_W, tok_b, tok_ln2_g, tok_ln2_b,
                     attn_w_qkv, attn_w_proj, attn_b_proj, ffn_W_qkv, ffn_b_qkv, ffn_W_gate,
                     ffn_b_gate, ffn_A, ffn_B_lora, ffn_W_proj, ffn_b_proj, out):
    with ExitStack() as ctx:
        def sb(name, shape):
            return ctx.enter_context(nc.sbuf_tensor(name, shape, F32))

        def sem(name):
            return ctx.enter_context(nc.semaphore(name))

        def sems(name, n=GROUPS):
            return [sem(f"{name}_{i}") for i in range(n)]

        bank = [ctx.enter_context(nc.psum_tensor(f"bank{i}", [P, BANK], F32)) for i in range(8)]

        ident = sb("ident", [P, P])
        clock_feed = ctx.enter_context(nc.sbuf_tensor("clock_feed", [P, BANK], mybir.dt.bfloat16))
        ident_pair = sb("ident_pair", [P, TOKENS])
        mask_even = sb("mask_even", [P, 1])
        mask_odd = sb("mask_odd", [P, 1])
        eps = sb("eps", [P, 1])
        earlier = sb("earlier", [P, EXPERTS, EXPERTS])
        w_tok = sb("w_tok", [P, 2, CHANNELS, DIM])
        w_tok_g = sb("w_tok_g", [P, 2, CHANNELS, DIM])
        ln1_g = sb("ln1_g", [P, 2, CHANNELS])
        ln1_b = sb("ln1_b", [P, 2, CHANNELS])
        tok_bias = sb("tok_bias", [P, DIM])
        ln2_g = sb("ln2_g", [P, DIM])
        ln2_b = sb("ln2_b", [P, DIM])
        attn_bias = sb("attn_bias", [P, DIM])
        ffn_bias = sb("ffn_bias", [P, DIM])
        v_bias = sb("v_bias", [P, DIM])
        gate_bias = sb("gate_bias", [P, EXPERTS])
        qk_bias = sb("qk_bias", [HALF, 4])
        k_bias_odd = sb("k_bias_odd", [HALF, 2])
        qkv_raw = [sb(f"qkv_raw{i}", [HALF, 6, DIM]) for i in range(2)]
        proj_raw = [sb(f"proj_raw{i}", [HALF, 2, DIM]) for i in range(2)]
        proj_parity = [sb(f"proj_parity{i}", [HALF, 2, DIM]) for i in range(2)]
        qk_bias_raw = sb("qk_bias_raw", [4, HALF])
        a_raw = sb("a_raw", [LORA, DIM])
        gate_raw = sb("gate_raw", [EXPERTS, DIM])
        b_raw = sb("b_raw", [HALF, 6, EXPERTS, RANK])
        wT = [sb(f"wT{i}", [HALF, 2, 3 * DIM]) for i in range(2)]
        projT = [sb(f"projT{i}", [HALF, 2, DIM]) for i in range(2)]
        aT_gate = sb("aT_gate", [HALF, 2, LORA + EXPERTS])
        bT = sb("bT", [LORA, 3 * DIM])
        pix_stats = sb("pix_stats", [P, GRID, CHANNELS * 6])
        stats = sb("stats", [P, GRID, 6])
        mean_var = sb("mean_var", [P, GRID, 2])
        std = sb("std", [P, GRID])
        rstd = sb("rstd", [P, GRID])
        shift = sb("shift", [P, GRID])
        h = sb("h", [P, GRID, DIM])
        h_plus = sb("h_plus", [P, GRID, DIM])
        y = sb("y", [P, GRID, DIM])
        yT = sb("yT", [HALF, 2, IMAGES * TOKENS])
        loraT = sb("loraT", [LORA, IMAGES * TOKENS])
        mixedT = sb("mixedT", [HALF, 2, GRID, IMAGES * GRID])
        halves = (slice(0, TOKENS), slice(TOKENS, P))

        def keep_clock(pe, spare, n, columns=BANK):
            for _ in range(n):
                pe.matmul(spare[:, 0:columns], clock_feed[:, 0:P], clock_feed[:, 0:columns], start=True, stop=True)

        with ExitStack() as stage:
            def sem_a(name):
                return stage.enter_context(nc.semaphore(name))

            def sb_a(name, shape):
                return stage.enter_context(nc.sbuf_tensor(name, shape, F32))

            pixels = sb_a("pixels", [P, CHANNELS, PATCH, GRID, PATCH])
            patches = sb_a("patches", [P, GRID, PIXELS])
            patchesT = sb_a("patchesT", [P, GRID, PIXELS])
            pix_loaded = [sem_a(f"pix_loaded{c}") for c in range(CHANNELS)]
            tok_w_loaded = sem_a("tok_w_loaded")
            tok_rows_loaded = sem_a("tok_rows_loaded")
            attn_w_loaded = sem_a("attn_w_loaded")
            ffn_w_loaded = sem_a("ffn_w_loaded")
            ffn_rows_loaded = sem_a("ffn_rows_loaded")
            ident_zeroed = sem_a("ident_zeroed")
            ident_ready = sem_a("ident_ready")
            consts_ready = sem_a("consts_ready")
            w_scaled = sem_a("w_scaled")
            feed_ready = sem_a("feed_ready")
            parity_ready = sem_a("parity_ready")
            dve_step = sem_a("dve_step_a")
            var_ready = sem_a("var_ready")
            std_ready = sem_a("std_ready")
            rstd_ready = sem_a("rstd_ready")
            patch_dve = sem_a("patch_dve")
            patch_act = sem_a("patch_act")
            patchT_ready = sem_a("patchT_ready")
            patchT_copied = [sem_a("patchT_copied_act"), sem_a("patchT_copied_dve")]
            bias_row_ready = sem_a("bias_row_ready")
            bias_row_copied = sem_a("bias_row_copied")
            tok_ready = sem_a("tok_ready")
            wT_ready = sem_a("wT_ready")
            wT_copied = sem_a("wT_copied")
            h_ready = sem_a("h_ready")
            h_plus_ready = sem_a("h_plus_ready")
            y_ready = sem_a("y_ready")
            yT_ready = sem_a("yT_ready")
            yT_copied = sem_a("yT_copied")

            def weight_groups():
                groups = []
                for i in range(2):
                    for kc in range(2):
                        for th in range(2):
                            ins = [qkv_raw[i][:, 3 * th + t, kc * HALF:(kc + 1) * HALF] for t in range(3)]
                            groups.append((ins, HALF, wT[i][:, kc, th * 3 * HALF:(th + 1) * 3 * HALF]))
                    ins = [proj_parity[i][:, o, e * HALF:(e + 1) * HALF] for e in range(2) for o in range(2)]
                    groups.append((ins, HALF, projT[i][:, :, :].rearrange("p e o -> p (e o)")))
                for kc in range(2):
                    ins = [a_raw[:, kc * HALF:(kc + 1) * HALF], gate_raw[:, kc * HALF:(kc + 1) * HALF]]
                    groups.append((ins, HALF, aT_gate[:, kc, :]))
                for th in range(2):
                    ins = [b_raw[:, 3 * th + t, :, :].rearrange("p n r -> p (n r)") for t in range(3)]
                    groups.append((ins, LORA, bT[:, th * 3 * HALF:(th + 1) * 3 * HALF]))
                groups.append(([qk_bias_raw[:, :]], HALF, qk_bias[:, :]))
                return groups

            w_groups = weight_groups()
            attn_groups = 5

            with nc.Block() as block:
                @block.sync
                def _(sp):
                    for c in range(CHANNELS):
                        sp.dma_start(pixels[:, c, :, :, :].rearrange("p r w s -> p (r w s)"),
                                     x_channel(x, c)).then_inc(pix_loaded[c], 16)
                    sp.dma_start(w_tok[:, :, :, :],
                                 tok_W.rearrange("(a p c) m -> p a c m", a=2, c=CHANNELS)).then_inc(tok_w_loaded, 16)
                    sp.dma_start(qkv_raw[0][:, :, :],
                                 attn_w_qkv.rearrange("(t p) i -> p t i", p=HALF)).then_inc(attn_w_loaded, 16)
                    sp.dma_start(proj_raw[0][:, :, :],
                                 attn_w_proj.rearrange("(t p) i -> p t i", p=HALF)).then_inc(attn_w_loaded, 16)
                    sp.dma_start(qkv_raw[1][:, :, :],
                                 ffn_W_qkv.rearrange("(t p) i -> p t i", p=HALF)).then_inc(ffn_w_loaded, 16)
                    sp.dma_start(proj_raw[1][:, :, :],
                                 ffn_W_proj.rearrange("(t p) i -> p t i", p=HALF)).then_inc(ffn_w_loaded, 16)
                    sp.dma_start(a_raw[:, :], ffn_A.rearrange("n r d -> (n r) d")).then_inc(ffn_w_loaded, 16)
                    sp.dma_start(gate_raw[:, :], ffn_W_gate).then_inc(ffn_w_loaded, 16)
                    sp.dma_start(qk_bias_raw[:, :],
                                 ffn_b_qkv[0:2 * DIM].rearrange("(t p) -> t p", p=HALF)).then_inc(ffn_w_loaded, 16)
                    for t in range(6):
                        sp.dma_start(b_raw[:, t, :, :],
                                     ffn_B_lora[:, t * HALF:(t + 1) * HALF, :].rearrange("n p r -> p n r"))\
                            .then_inc(ffn_w_loaded, 16)
                    sp.wait_ge(ffn_rows_loaded, 3 * 16)

                def row(dram):
                    return dram.rearrange("(a d) -> a d", a=1).to_broadcast([P, dram.shape[0]])

                @block.gpsimd
                def _(pool):
                    pool.memset(ident[:, :], 0.0).then_inc(ident_zeroed, 1)
                    pool.memset(clock_feed[:, :], 1.0).then_inc(feed_ready, 1)
                    pool.memset(eps[:, :], EPS).then_inc(consts_ready, 1)
                    pool.memset(earlier[:, :, :], 1.0).then_inc(ident_zeroed, 1)
                    pool.wait_ge(ident_zeroed, 2)
                    pool.affine_select(out=ident[:, :], in_=ident[:, :], compare_op=ALU.not_equal, fill=1.0,
                                       base=0, pattern=[[-1, P]], channel_multiplier=1).then_inc(ident_ready, 1)
                    pool.affine_select(out=earlier[:, :, :], in_=earlier[:, :, :], compare_op=ALU.is_gt, fill=0.0,
                                       base=0, pattern=[[1, EXPERTS], [-1, EXPERTS]], channel_multiplier=0)\
                        .then_inc(consts_ready, 1)
                    pool.wait_ge(tok_w_loaded, 3 * 16)
                    pool.tensor_tensor(w_tok_g[:, :, :, :].rearrange("p a c m -> p (a c) m"),
                                       w_tok[:, :, :, :].rearrange("p a c m -> p (a c) m"),
                                       ln1_g[:, :, :].rearrange("p a c -> p (a c)").unsqueeze(2)
                                       .to_broadcast([P, CHUNKS, DIM]), ALU.mult).then_inc(w_scaled, 1)
                    for i, (loaded, n) in enumerate(((attn_w_loaded, 2), (ffn_w_loaded, 11))):
                        pool.wait_ge(loaded, n * 16)
                        for o in range(2):
                            last = pool.tensor_copy(
                                proj_parity[i][:, o, :].rearrange("p (e g d) -> p e g d", e=2, d=HEAD),
                                proj_raw[i][:, o, :].rearrange("p (g e d) -> p e g d", e=2, d=HEAD))
                        last.then_inc(parity_ready, 1)
                    pool.wait_ge(h_ready, 1)
                    pool.tensor_tensor(h_plus[:, :, :], h[:, :, :],
                                       attn_bias[:, :].unsqueeze(1).to_broadcast([P, GRID, DIM]), ALU.add)\
                        .then_inc(h_plus_ready, 1)

                @block.vector
                def _(dve):
                    done = [0]

                    def chain(ins):
                        ins.then_inc(dve_step, 1)
                        done[0] += 1
                        dve.wait_ge(dve_step, done[0])

                    for c in range(CHANNELS):
                        dve.wait_ge(pix_loaded[c], 16)
                        for w in range(GRID):
                            last = dve.bn_stats(pix_stats[:, w, 6 * c:6 * c + 6], pixels[:, c, :, w, :])
                    chain(last)
                    for w in range(GRID):
                        last = dve.bn_aggr(mean_var[:, w, :], pix_stats[:, w, :])
                    last.then_inc(var_ready, 1)
                    dve.wait_ge(ident_ready, 1)
                    dve.tensor_tensor(ident_pair[:, :], ident[:, 0:TOKENS], ident[:, TOKENS:P], ALU.add)
                    chain(dve.tensor_reduce(mask_even[:, :],
                                            ident[:, :].rearrange("p (g e d) -> p g e d", e=2, d=HEAD)[:, :, 0, :],
                                            AX.XY, ALU.add))
                    dve.tensor_scalar(mask_odd[:, :], mask_even[:, :], -1.0, 1.0, ALU.mult, ALU.add)

                    def inverse_std(n):
                        dve.wait_ge(std_ready, n)
                        chain(dve.reciprocal(rstd[:, :], std[:, :]))
                        dve.scalar_tensor_tensor(out=shift[:, :], in0=mean_var[:, :, 0], scalar=-1.0,
                                                 in1=rstd[:, :], op0=ALU.mult, op1=ALU.mult)\
                            .then_inc(rstd_ready, 1)
                        dve.wait_ge(rstd_ready, n)

                    inverse_std(1)
                    for w in range(0, GRID, 2):
                        dve.tensor_scalar(patches[:, w, :].rearrange("p (a s) -> p a s", s=PATCH),
                                          pixels[:, :, :, w, :].rearrange("p c r s -> p (c r) s"),
                                          rstd[:, w:w + 1], shift[:, w:w + 1], ALU.mult, ALU.add)\
                            .then_inc(patch_dve, 1)
                    for w in range(1, GRID, 2):
                        dve.wait_ge(patchT_ready, 2 * w + 2)
                        for b in range(2):
                            last = dve.tensor_copy(patchesT[:, w, b * 384:(b + 1) * 384],
                                                   bank[2 * (w % 2) + b][:, 0:384])
                        last.then_inc(patchT_copied[1], 1)
                    dve.wait_ge(bias_row_ready, 1)
                    dve.wait_ge(tok_rows_loaded, 4 * 16)
                    dve.tensor_tensor(tok_bias[:, :], bank[0][:, 0:DIM], tok_bias[:, :], ALU.add)\
                        .then_inc(bias_row_copied, 1)
                    dve.wait_ge(bias_row_copied, 1)
                    for j in range(4):
                        dve.wait_ge(tok_ready, 2 * j + 2)
                        last = dve.tensor_tensor(y[:, 2 * j:2 * j + 2, :],
                                                 bank[4 + j][:, 0:2 * DIM].rearrange("p (w m) -> p w m", w=2),
                                                 tok_bias[:, :].unsqueeze(1).to_broadcast([P, 2, DIM]), ALU.add)
                    chain(last)

                    def norm_stats(src):
                        for w in range(GRID):
                            last = dve.bn_stats(stats[:, w, :], src[:, w, :])
                        chain(last)
                        for w in range(GRID):
                            last = dve.bn_aggr(mean_var[:, w, :], stats[:, w, :])
                        last.then_inc(var_ready, 1)

                    def normalise(dst, src):
                        for w in range(GRID):
                            last = dve.tensor_scalar(dst[:, w, :], src[:, w, :], rstd[:, w:w + 1],
                                                     shift[:, w:w + 1], ALU.mult, ALU.add)
                        return last

                    norm_stats(y)
                    inverse_std(2)
                    chain(normalise(y, y))
                    chain(dve.tensor_tensor(y[:, :, :], y[:, :, :],
                                            ln2_g[:, :].unsqueeze(1).to_broadcast([P, GRID, DIM]), ALU.mult))
                    dve.tensor_tensor(h[:, :, :], y[:, :, :],
                                      ln2_b[:, :].unsqueeze(1).to_broadcast([P, GRID, DIM]), ALU.add)\
                        .then_inc(h_ready, 1)
                    dve.wait_ge(h_ready, 1)
                    norm_stats(h)
                    inverse_std(3)
                    normalise(y, h).then_inc(y_ready, 1)
                    for g in (1, 3):
                        dve.wait_ge(yT_ready, g + 1)
                        dve.tensor_copy(yT_columns(yT, g), transposed_tiles(bank[4 + g])).then_inc(yT_copied, 1)

                @block.scalar
                def _(act):
                    act.dma_start(ln1_g[:, :, :],
                                  tok_ln1_g.rearrange("(a p c) -> p a c", a=2, c=CHANNELS)).then_inc(tok_w_loaded, 16)
                    act.dma_start(ln1_b[:, :, :],
                                  tok_ln1_b.rearrange("(a p c) -> p a c", a=2, c=CHANNELS)).then_inc(tok_w_loaded, 16)
                    act.dma_start(tok_bias[:, :], row(tok_b)).then_inc(tok_rows_loaded, 16)
                    act.dma_start(ln2_g[:, :], row(tok_ln2_g)).then_inc(tok_rows_loaded, 16)
                    act.dma_start(ln2_b[:, :], row(tok_ln2_b)).then_inc(tok_rows_loaded, 16)
                    act.dma_start(attn_bias[:, :], row(attn_b_proj)).then_inc(tok_rows_loaded, 16)
                    act.dma_start(ffn_bias[:, :], row(ffn_b_proj)).then_inc(ffn_rows_loaded, 16)
                    act.dma_start(v_bias[:, :], row(ffn_b_qkv[2 * DIM:3 * DIM])).then_inc(ffn_rows_loaded, 16)
                    act.dma_start(gate_bias[:, :], row(ffn_b_gate)).then_inc(ffn_rows_loaded, 16)

                    def std_of(n):
                        act.wait_ge(var_ready, n)
                        act.wait_ge(consts_ready, 1)
                        act.activation(std[:, :], mean_var[:, :, 1], ACT.Sqrt, bias=eps[:, :])\
                            .then_inc(std_ready, 1)

                    std_of(1)
                    act.wait_ge(rstd_ready, 1)
                    for w in range(1, GRID, 2):
                        act.activation(patches[:, w, :].rearrange("p (a s) -> p a s", s=PATCH),
                                       pixels[:, :, :, w, :].rearrange("p c r s -> p (c r) s"),
                                       ACT.Identity, scale=rstd[:, w:w + 1], bias=shift[:, w:w + 1])\
                            .then_inc(patch_act, 1)
                    for w in range(0, GRID, 2):
                        act.wait_ge(patchT_ready, 2 * w + 2)
                        for b in range(2):
                            last = act.copy(patchesT[:, w, b * 384:(b + 1) * 384],
                                            bank[2 * (w % 2) + b][:, 0:384])
                        last.then_inc(patchT_copied[0], 1)

                    def weights(first, end):
                        for g in range(first, end):
                            ins, rows, dst = w_groups[g]
                            act.wait_ge(wT_ready, g + 1)
                            act.copy(dst, bank[g % 4][0:rows, 0:dst.free_size()]).then_inc(wT_copied, 1)

                    weights(0, 4)
                    std_of(2)
                    weights(4, 9)
                    std_of(3)
                    weights(9, len(w_groups))
                    for g in (0, 2):
                        act.wait_ge(yT_ready, g + 1)
                        act.copy(yT_columns(yT, g), transposed_tiles(bank[4 + g])).then_inc(yT_copied, 1)

                @block.tensor
                def _(pe):
                    pe.wait_ge(ident_ready, 1)
                    pe.wait_ge(feed_ready, 1)

                    def transpose_tile(w):
                        pe.wait_ge(patch_act if w % 2 else patch_dve, w // 2 + 1)
                        if w >= 2:
                            pe.wait_ge(patchT_copied[w % 2], w // 2)
                        for k in range(CHUNKS):
                            t = pe.transpose(bank[2 * (w % 2) + k // 3][:, (k % 3) * P:(k % 3 + 1) * P],
                                             patches[:, w, k * P:(k + 1) * P], ident[:, :])
                            if k % 3 == 2:
                                t.then_inc(patchT_ready, 1)

                    def project_tile(w):
                        pe.wait_ge(patchT_copied[w % 2], w // 2 + 1)
                        dst = bank[4 + w // 2][:, (w % 2) * DIM:(w % 2 + 1) * DIM]
                        for k in range(CHUNKS):
                            t = pe.matmul(dst, patchesT[:, w, k * P:(k + 1) * P], w_tok_g[:, k % 2, k // 2, :],
                                          start=(k == 0), stop=(k == CHUNKS - 1))
                        t.then_inc(tok_ready, 1)

                    transpose_tile(0)
                    transpose_tile(1)
                    pe.wait_ge(w_scaled, 1)
                    for w in range(GRID):
                        project_tile(w)
                        if w + 2 < GRID:
                            transpose_tile(w + 2)
                    for k in range(CHUNKS):
                        t = pe.matmul(bank[0][:, 0:DIM], ln1_b[:, k % 2, k // 2:k // 2 + 1].to_broadcast([P, P]),
                                      w_tok[:, k % 2, k // 2, :], start=(k == 0), stop=(k == CHUNKS - 1))
                    t.then_inc(bias_row_ready, 1)
                    for g, (ins, rows, dst) in enumerate(w_groups):
                        if g == 0:
                            pe.wait_ge(attn_w_loaded, 2 * 16)
                            pe.wait_ge(parity_ready, 1)
                            pe.wait_ge(bias_row_copied, 1)
                        if g == attn_groups:
                            pe.wait_ge(ffn_w_loaded, 11 * 16)
                            pe.wait_ge(parity_ready, 2)
                        if g >= 4:
                            pe.wait_ge(wT_copied, g - 3)
                        at = 0
                        for src in ins:
                            cols = src.shape[0]
                            t = pe.transpose(bank[g % 4][0:rows, at:at + cols], src, ident[0:cols, 0:cols])
                            at += cols
                        t.then_inc(wT_ready, 1)
                    pe.wait_ge(y_ready, 1)
                    for g in range(4):
                        for w in range(4):
                            t = pe.transpose(bank[4 + g][0:HALF, w * P:(w + 1) * P],
                                             y[:, 4 * (g // 2) + w, (g % 2) * HALF:(g % 2 + 1) * HALF], ident[:, :])
                        t.then_inc(yT_ready, 1)

        yT_round = sb("yT_round", [HALF, 2, QUAD, 2, TOKENS])
        loraT_round = sb("loraT_round", [LORA, QUAD, 2, TOKENS])
        q_round = sb("q_round", [HALF, 2, ROUND_TOKENS])
        k_round = sb("k_round", [HALF, 2, 2, ROUND_TOKENS])
        v_round = sb("v_round", [P, QUAD, DIM])
        row_max = sb("row_max", [P, GROUPS, BLOCKS])
        row_sum = sb("row_sum", [P, GROUPS, BLOCKS])
        row_inv = sb("row_inv", [P, GROUPS, BLOCKS])
        expd = sb("expd", [P, GROUPS, BLOCKS, TOKENS])
        probs = sb("probs", [P, GROUPS, BLOCKS, TOKENS])
        probsT = sb("probsT", [P, GROUPS, BLOCKS, TOKENS])
        gram_v = sb("gram_v", [P, GROUPS, BLOCKS, GRAM_V])
        col_sum = sb("col_sum", [P, GROUPS, BLOCKS])
        neg_max = sb("neg_max", [BLOCKS, GROUPS, 2])
        neg_inv = sb("neg_inv", [BLOCKS, GROUPS, 2, TOKENS])
        neg_inv_all = sb("neg_inv_all", [P, GROUPS, BLOCKS])
        resid_first = sb("resid_first", [P, GROUPS, BLOCKS, TOKENS])
        resid = sb("resid", [P, GROUPS, BLOCKS, TOKENS])
        square = sb("square", [P, GROUPS, BLOCKS, TOKENS])
        step = sb("step", [P, GROUPS, BLOCKS, TOKENS])
        kv = sb("kv", [P, GROUPS, BLOCKS, HEAD])
        kv_next = sb("kv_next", [P, GROUPS, BLOCKS, HEAD])
        mixed = sb("mixed", [P, QUAD, PAIRS, HEAD])
        logits = sb("logits", [P, GRID, EXPERTS])
        route_max = sb("route_max", [P, GRID])
        route_sum = sb("route_sum", [P, GRID])
        route_exp = sb("route_exp", [P, GRID, EXPERTS])
        route = sb("route", [P, GRID, EXPERTS])
        beaten = sb("beaten", [P, GRID, EXPERTS, EXPERTS])
        tied = sb("tied", [P, GRID, EXPERTS, EXPERTS])
        rank = sb("rank", [P, GRID, EXPERTS])
        dispatch = sb("dispatch", [P, GRID, EXPERTS])
        lora = sb("lora", [P, GRID, LORA])

        tokens_ready = sem("tokens_ready")
        q_ready, k_ready, v_ready = sem("q_ready"), sem("k_ready"), sem("v_ready")
        q_copied, k_even_copied, k_odd_copied = sem("q_copied"), sem("k_even_copied"), sem("k_odd_copied")
        v_copied = sem("v_copied")
        scores_ready = sems("scores_ready")
        max_ready = sems("max_ready")
        shifted = sems("shifted")
        exp_ready = sems("exp_ready")
        sum_ready = sems("sum_ready")
        inv_ready = sems("inv_ready")
        probs_ready = sems("probs_ready")
        probsT_ready = sems("probsT_ready")
        probsT_copied = sems("probsT_copied")
        col_sum_ready = sems("col_sum_ready")
        col_sumT_ready = sems("col_sumT_ready")
        neg_max_ready = sems("neg_max_ready")
        neg_inv_ready = sems("neg_inv_ready")
        neg_inv_spread = sems("neg_inv_spread")
        neg_inv_copied = sems("neg_inv_copied")
        gram_scaled_ready = sems("gram_scaled_ready")
        gram_ready = sems("gram_ready", GRAM_BANKS)
        kv_ready = sem("kv_ready")
        kv_moved = sem("kv_moved")
        kv_copied = sem("kv_copied")
        first_resid_ready = sem("first_resid_ready")
        square_ready = sems("square_ready")
        square_copied = sems("square_copied")
        step_ready = sems("step_ready")
        resid_ready = sems("resid_ready")
        resid_copied = sems("resid_copied")
        tail_ready = sems("tail_ready")
        mixed_ready = sem("mixed_ready")
        mixedT_ready = sem("mixedT_ready")
        mixedT_copied = sem("mixedT_copied")
        round_sems = range(tokens_ready.num, mixedT_copied.num + 1)

        FEED_NARROW = 3
        Q_BANK, K_BANK, V_BANK = bank[3], bank[4], (bank[5], bank[6])

        def blocks(ap):
            return ap.rearrange("p (n t) -> p n t", t=TOKENS)

        def chunk_blocks(c):
            for n in range(BLOCKS):
                yield n, n % QUAD, GROUPS * (n // QUAD) + c

        def project_q_k(pe, weights, lora_on, ahead):
            tokens = bass.ds(ahead * ROUND_TOKENS, ROUND_TOKENS)
            for dst, ready, at in ((Q_BANK, q_ready, 0), (K_BANK, k_ready, DIM)):
                for m in range(2):
                    o = at + m * HALF
                    for kc in range(2):
                        t = pe.matmul(dst[0:HALF, m * ROUND_TOKENS:(m + 1) * ROUND_TOKENS],
                                      weights[:, kc, o:o + HALF], yT[:, kc, tokens],
                                      start=(kc == 0), stop=(kc == 1 and not lora_on))
                    if lora_on:
                        t = pe.matmul(dst[0:HALF, m * ROUND_TOKENS:(m + 1) * ROUND_TOKENS],
                                      bT[:, o:o + HALF], loraT[:, tokens], start=False, stop=True)
                t.then_inc(ready, 1)

        def project_v(pe, weights, lora_on):
            for b in range(QUAD):
                dst = V_BANK[b // 2][:, (b % 2) * DIM:(b % 2 + 1) * DIM]
                for kc in range(2):
                    t = pe.matmul(dst, yT_round[:, kc, b, :, :].rearrange("p r t -> p (r t)"),
                                  weights[:, kc, 2 * DIM:3 * DIM], start=(kc == 0),
                                  stop=(kc == 1 and not lora_on))
                if lora_on:
                    t = pe.matmul(dst, loraT_round[:, b, :, :].rearrange("p r t -> p (r t)"),
                                  bT[:, 2 * DIM:3 * DIM], start=False, stop=True)
                if b % 2:
                    t.then_inc(v_ready, 1)

        def scores(pe):
            for c in range(GROUPS):
                keep_clock(pe, SCORE_BANK[c], FEED_NARROW)
                rows = slice(32 * c, 32 * c + 32)
                for slot in range(SLOTS):
                    half, image_pair = slot // 2, slot % 2
                    for image in range(2):
                        cols = slice((2 * image_pair + image) * TOKENS, (2 * image_pair + image + 1) * TOKENS)
                        t = pe.matmul(SCORE_BANK[c][halves[image], slot * P:(slot + 1) * P],
                                      q_round[rows, half, cols], k_round[rows, :, half, cols],
                                      start=True, stop=True)
                t.then_inc(scores_ready[c], 1)

        def transpose_probs(pe, c, dst):
            for slot in range(SLOTS):
                t = pe.transpose(dst[:, slot * P:(slot + 1) * P],
                                 probs[:, c, 2 * slot:2 * slot + 2, :].rearrange("p n t -> p (n t)"), ident[:, :])
            t.then_inc(probsT_ready[c], 1)

        def head_matmuls(pe, dst, lhsT, rhs_of, width, c):
            for n, b, pair in chunk_blocks(c):
                for e in range(2):
                    t = pe.matmul(dst[halves[e], n * width:(n + 1) * width], lhsT[halves[e], c, n, :],
                                  rhs_of(e, n, b, pair), start=True, stop=True)
            return t

        def v_of(e, n, b, pair):
            head = 2 * pair + e
            return v_round[halves[e], b, head * HEAD:(head + 1) * HEAD]

        def transpose_mixed(pe, dst):
            for b in range(QUAD):
                t = pe.transpose(dst[0:HALF, b * P:(b + 1) * P],
                                 mixed[:, b, :, :].rearrange("p g d -> p (g d)"), ident[:, :])
            return t


        def shift_scores(dve, c):
            dve.wait_ge(scores_ready[c], 1)
            dve.tensor_reduce(row_max[:, c, :], blocks(SCORE_BANK[c][:, :]), AX.X, ALU.max).then_inc(max_ready[c], 1)
            dve.wait_ge(max_ready[c], 1)
            dve.tensor_tensor(expd[:, c, :, :], blocks(SCORE_BANK[c][:, :]),
                              row_max[:, c, :].unsqueeze(2).to_broadcast([P, BLOCKS, TOKENS]), ALU.subtract)\
                .then_inc(shifted[c], 1)

        def exponentiate(act, c):
            act.wait_ge(shifted[c], 1)
            act.activation(expd[:, c, :, :], expd[:, c, :, :], ACT.Exp, scale=SCALE).then_inc(exp_ready[c], 1)

        def invert_sums(dve, c):
            dve.wait_ge(exp_ready[c], 1)
            dve.tensor_reduce(row_sum[:, c, :], expd[:, c, :, :], AX.X, ALU.add).then_inc(sum_ready[c], 1)
            dve.wait_ge(sum_ready[c], 1)
            dve.reciprocal(row_inv[:, c, :], row_sum[:, c, :]).then_inc(inv_ready[c], 1)

        def normalise_rows(pool, c):
            pool.wait_ge(inv_ready[c], 1)
            pool.tensor_tensor(probs[:, c, :, :], expd[:, c, :, :],
                               row_inv[:, c, :].unsqueeze(2).to_broadcast([P, BLOCKS, TOKENS]), ALU.mult)\
                .then_inc(probs_ready[c], 1)

        def mixed_of(c):
            return mixed[:, :, :, :].rearrange("p b (m g) d -> p b m g d", m=2)[:, :, :, c, :]

        def round_mixedT(q, e):
            return mixedT[:, e, :, bass.ds(q * QUAD * GRID, QUAD * GRID)].rearrange("p w (b h) -> p w b h", b=QUAD)

        def mixedT_psum(src, e):
            return src[0:HALF, :].rearrange("p (b e w h) -> p e w b h", b=QUAD, e=2, w=GRID)[:, e, :, :, :]

        def narrow(ap):
            return ap.rearrange("p (m b d) -> p b m d", m=2, d=HEAD)

        def narrow_sb(ap):
            return ap.rearrange("p (m b) d -> p b m d", m=2)

        PHASES = 2 * STEPS
        FEED_START, FEED_END = 6, 4
        Q_K_AT, SCORES_AT, SHIFT_AT, EXP_AT, SUM_AT = 0, 1, (1, 2, 2), (2, 3, 3), 3
        TRANSPOSE_AT, COL_SUM_AT, SPREAD_AT, GRAM_AT = 5, 6, 7, 9
        SCORE_BANK = (bank[3], bank[4], bank[7])
        PROBS_T_BANK = (bank[5], bank[6], bank[3])
        GRAM_BANK = (bank[4], bank[7], bank[6], bank[5])
        MIXED_BANK = bank[3]
        MIX_AT = 4

        def gram_at(n, c):
            block = c * BLOCKS + n
            return block // PER_GRAM_BANK, block % PER_GRAM_BANK * GRAM_V

        def inverse_phase_pe(pe, s):
            t = s // 2
            for c in range(GROUPS):
                feed = 2 if c == 0 and s - 1 == SPREAD_AT else 1
                if s % 2 == 0:
                    r = resid if t else resid_first
                    if t:
                        pe.wait_ge(resid_copied[c], t)
                    keep_clock(pe, bank[c], feed)
                    head_matmuls(pe, bank[c], r, lambda e, n, b, pair: r[halves[e], c, n, :], TOKENS, c)\
                        .then_inc(square_ready[c], 1)
                else:
                    pe.wait_ge(square_copied[c], t + 1)
                    pe.wait_ge(step_ready[c], t + 1)
                    keep_clock(pe, bank[c], feed)
                    head_matmuls(pe, bank[c], square, lambda e, n, b, pair: step[halves[e], c, n, :], TOKENS, c)\
                        .then_inc(resid_ready[c], 1)

        def inverse_tail_pe(pe):
            pe.wait_ge(kv_moved, 1)
            for c in range(GROUPS):
                pe.wait_ge(resid_copied[c], STEPS)
                keep_clock(pe, bank[c], FEED_NARROW)
                head_matmuls(pe, bank[c], resid, lambda e, n, b, pair: kv[halves[e], c, n, :], HEAD, c).then_inc(tail_ready[c], 1)

        def softmax_gap_pe(pe, s, mix, ahead):
            if s == Q_K_AT:
                project_q_k(pe, wT[0], False, ahead)
            if s == SCORES_AT:
                pe.wait_ge(tokens_ready, 2)
                project_v(pe, wT[0], False)
                pe.wait_ge(q_copied, 1)
                pe.wait_ge(k_even_copied, 1)
                pe.wait_ge(k_odd_copied, 1)
                scores(pe)
            if s == TRANSPOSE_AT:
                pe.wait_ge(v_copied, 2)
                for c in range(GROUPS):
                    pe.wait_ge(probs_ready[c], 1)
                    if mix and PROBS_T_BANK[c] is MIXED_BANK:
                        pe.wait_ge(mixedT_copied, 2)
                    transpose_probs(pe, c, PROBS_T_BANK[c])
            if s == COL_SUM_AT:
                for c in range(GROUPS):
                    pe.wait_ge(col_sum_ready[c], 1)
                    pe.transpose(GRAM_BANK[c][0:BLOCKS, 0:P], col_sum[:, c, :], ident[:, :])\
                        .then_inc(col_sumT_ready[c], 1)
            if s == SPREAD_AT:
                for c in range(GROUPS):
                    pe.wait_ge(neg_inv_ready[c], 1)
                    pe.matmul(GRAM_BANK[c][:, P:P + BLOCKS], neg_inv[:, c, :, :].rearrange("p e t -> p (e t)"),
                              ident[0:BLOCKS, 0:BLOCKS], start=True, stop=True).then_inc(neg_inv_spread[c], 1)
            if s == GRAM_AT:
                for c in range(GROUPS):
                    pe.wait_ge(neg_inv_copied[c], 1)
                for c in range(GROUPS):
                    pe.wait_ge(gram_scaled_ready[c], 1)
                    keep_clock(pe, GRAM_BANK[c + 1], 1)
                    for n in range(BLOCKS):
                        j, at = gram_at(n, c)
                        for e in range(2):
                            t = pe.matmul(GRAM_BANK[j][halves[e], at:at + GRAM_V], probsT[halves[e], c, n, :],
                                          gram_v[halves[e], c, n, :], start=True, stop=True)
                        if at == (PER_GRAM_BANK - 1) * GRAM_V:
                            t.then_inc(gram_ready[j], 1)

        def nystrom_pe(pe, inverse, softmax, mix, ahead):
            keep_clock(pe, bank[7], FEED_START)
            for s in range(PHASES):
                if inverse:
                    inverse_phase_pe(pe, s)
                if softmax:
                    softmax_gap_pe(pe, s, mix, ahead)
                if mix and s == MIX_AT:
                    if softmax:
                        pe.wait_ge(shifted[0], 1)
                    transpose_mixed(pe, MIXED_BANK).then_inc(mixedT_ready, 1)
            if inverse:
                inverse_tail_pe(pe)
                keep_clock(pe, bank[7], FEED_END)

        def nystrom_dve(dve, inverse, softmax, ahead):
            if softmax:
                for kc in range(2):
                    dve.tensor_copy(yT_round[:, kc, :, :, :], twice(yT[:, kc, :], ahead)).then_inc(tokens_ready, 1)
            for s in range(PHASES):
                if inverse and s % 2 == 0:
                    t = s // 2
                    for c in range(GROUPS):
                        dve.wait_ge(square_copied[c], t + 1)
                        dve.scalar_tensor_tensor(out=step[:, c, :, :], in0=(resid if t else resid_first)[:, c, :, :],
                                                 scalar=3.0, in1=square[:, c, :, :], op0=ALU.mult, op1=ALU.add)\
                            .then_inc(step_ready[c], 1)
                if not softmax:
                    continue
                if s == Q_K_AT:
                    dve.wait_ge(k_ready, 1)
                    dve.tensor_scalar(k_round[:, 0, :, :].rearrange("p m t -> p (m t)"), K_BANK[0:HALF, :],
                                      mask_even[0:HALF, :], None, ALU.mult).then_inc(k_even_copied, 1)
                for c in range(GROUPS):
                    if s == SHIFT_AT[c]:
                        shift_scores(dve, c)
                if s == SUM_AT:
                    for c in range(GROUPS):
                        invert_sums(dve, c)
                if s == TRANSPOSE_AT:
                    for c in range(GROUPS):
                        dve.wait_ge(probsT_copied[c], 1)
                        dve.tensor_reduce(col_sum[:, c, :], probsT[:, c, :, :], AX.X, ALU.add)\
                            .then_inc(col_sum_ready[c], 1)
                if s == COL_SUM_AT:
                    for c in range(GROUPS):
                        dve.wait_ge(col_sumT_ready[c], 1)
                        dve.tensor_reduce(neg_max[:, c, :], blocks(GRAM_BANK[c][0:BLOCKS, 0:P]), AX.X, ALU.max,
                                          negate=True).then_inc(neg_max_ready[c], 1)
                        dve.wait_ge(neg_max_ready[c], 1)
                        dve.reciprocal(neg_inv[:, c, :, :],
                                       neg_max[:, c, :].unsqueeze(2).to_broadcast([BLOCKS, 2, TOKENS]))\
                            .then_inc(neg_inv_ready[c], 1)
                if s == SPREAD_AT:
                    for c in range(GROUPS):
                        dve.wait_ge(neg_inv_spread[c], 1)
                        dve.tensor_copy(neg_inv_all[:, c, :], GRAM_BANK[c][:, P:P + BLOCKS])\
                            .then_inc(neg_inv_copied[c], 1)
                if s == GRAM_AT:
                    if inverse:
                        dve.wait_ge(kv_moved, 1)
                    flat_resid = resid_first[:, :, :, :].rearrange("p c n t -> p (c n) t")
                    flat_kv = kv_next[:, :, :, :].rearrange("p c n d -> p (c n) d")
                    for j in range(GRAM_BANKS):
                        dve.wait_ge(gram_ready[j], 1)
                        first = j * PER_GRAM_BANK
                        own = slice(first, first + PER_GRAM_BANK)
                        both = GRAM_BANK[j][:, 0:PER_GRAM_BANK * GRAM_V].rearrange("p (n m) -> p n m", m=GRAM_V)
                        dve.tensor_tensor(flat_resid[:, own, :], both[:, :, 0:TOKENS],
                                          ident_pair[:, :].unsqueeze(1).to_broadcast([P, PER_GRAM_BANK, TOKENS]),
                                          ALU.add).then_inc(first_resid_ready, 1)
                        dve.tensor_copy(flat_kv[:, own, :], both[:, :, TOKENS:GRAM_V]).then_inc(kv_copied, 1)
            if inverse:
                for c in range(GROUPS):
                    dve.wait_ge(tail_ready[c], 1)
                    dve.tensor_tensor(mixed_of(c), narrow_sb(kv[:, c, :, :]),
                                      narrow(bank[c][:, 0:BLOCKS * HEAD]), ALU.subtract).then_inc(mixed_ready, 1)

        def nystrom_act(act, inverse, softmax, mix, before):
            for s in range(PHASES):
                t = s // 2
                if inverse:
                    for c in range(GROUPS):
                        if s % 2 == 0:
                            act.wait_ge(square_ready[c], t + 1)
                            act.copy(square[:, c, :, :], blocks(bank[c][:, :])).then_inc(square_copied[c], 1)
                        else:
                            act.wait_ge(resid_ready[c], t + 1)
                            act.mul(resid[:, c, :, :], blocks(bank[c][:, :]), 0.25).then_inc(resid_copied[c], 1)
                if mix and s == MIX_AT:
                    act.wait_ge(mixedT_ready, 1)
                    for e in range(2):
                        act.copy(round_mixedT(before, e), mixedT_psum(MIXED_BANK, e)).then_inc(mixedT_copied, 1)
                if not softmax:
                    continue
                if s == Q_K_AT:
                    act.wait_ge(q_ready, 1)
                    act.copy(q_round[:, :, :].rearrange("p m t -> p (m t)"), Q_BANK[0:HALF, :]).then_inc(q_copied, 1)
                    act.wait_ge(k_ready, 1)
                    act.wait_ge(k_even_copied, 1)
                    act.activation(k_round[:, 1, :, :].rearrange("p m t -> p (m t)"), K_BANK[0:HALF, :],
                                   ACT.Copy, scale=mask_odd[0:HALF, :]).then_inc(k_odd_copied, 1)
                if s == SCORES_AT:
                    for j in range(2):
                        act.wait_ge(v_ready, j + 1)
                        for image in range(2):
                            for e in range(2):
                                last = act.copy(
                                    gram_v[halves[e], :, 2 * j + image:BLOCKS:QUAD, TOKENS:GRAM_V]
                                    .rearrange("p c m d -> p m c d"),
                                    V_BANK[j][halves[e], image * DIM:(image + 1) * DIM]
                                    .rearrange("p (m c e d) -> p e m c d", m=2, c=GROUPS, e=2)[:, e, :, :, :])
                        last.then_inc(v_copied, 1)
                for c in range(GROUPS):
                    if s == EXP_AT[c]:
                        exponentiate(act, c)
                if s == TRANSPOSE_AT:
                    for c in range(GROUPS):
                        act.wait_ge(probsT_ready[c], 1)
                        act.copy(probsT[:, c, :, :], blocks(PROBS_T_BANK[c][:, :])).then_inc(probsT_copied[c], 1)

        def nystrom_pool(pool, inverse, softmax):
            if inverse:
                pool.tensor_copy(kv[:, :, :, :].rearrange("p c n d -> p (c n d)"),
                                 kv_next[:, :, :, :].rearrange("p c n d -> p (c n d)")).then_inc(kv_moved, 1)
            if softmax:
                for c in range(GROUPS):
                    normalise_rows(pool, c)
                for c in range(GROUPS):
                    pool.wait_ge(probsT_copied[c], 1)
                    pool.wait_ge(neg_inv_copied[c], 1)
                    pool.tensor_tensor(gram_v[:, c, :, 0:TOKENS], probsT[:, c, :, :],
                                       neg_inv_all[:, c, :].unsqueeze(2).to_broadcast([P, BLOCKS, TOKENS]),
                                       ALU.mult).then_inc(gram_scaled_ready[c], 1)

        def nystrom_block(inverse=None, softmax=None, mix=None):
            with nc.Block(no_gpsimd_drain=True) as block:
                @block.tensor
                def _(pe):
                    nystrom_pe(pe, inverse is not None, softmax is not None, mix is not None, softmax)

                @block.vector
                def _(dve):
                    nystrom_dve(dve, inverse is not None, softmax is not None, softmax)

                @block.scalar
                def _(act):
                    nystrom_act(act, inverse is not None, softmax is not None, mix is not None, mix)

                @block.gpsimd
                def _(pool):
                    nystrom_pool(pool, inverse is not None, softmax is not None)
            nc.all_engine_barrier(sems_to_clear=round_sems)

        nystrom_block(softmax=0)
        nystrom_block(inverse=0, softmax=1)
        with nc.Fori(1, ROUNDS - 1) as q:
            nystrom_block(inverse=q, softmax=q + 1, mix=q - 1)
        nystrom_block(inverse=ROUNDS - 1, mix=ROUNDS - 2)

        def project_out(pe, i, ready):
            for w in range(GRID):
                for e in range(2):
                    t = pe.matmul(bank[w // 2][:, (w % 2) * DIM:(w % 2 + 1) * DIM], mixedT[:, e, w, :],
                                  projT[i][:, e, :], start=(e == 0), stop=(e == 1))
                t.then_inc(ready, 1)

        with ExitStack() as stage:
            def sem_b(name):
                return stage.enter_context(nc.semaphore(name))

            last_mixedT_ready = sem_b("last_mixedT_ready")
            last_mixedT_copied = sem_b("last_mixedT_copied")
            proj_ready = sem_b("proj_ready")
            dve_step_b = sem_b("dve_step_b")
            h_ready_b = sem_b("h_ready_b")
            h_plus_b = sem_b("h_plus_b")
            var_b = sem_b("var_b")
            std_b = sem_b("std_b")
            y_b = sem_b("y_b")
            yT_b = sem_b("yT_b")
            yT_even = sem_b("yT_even")
            yT_odd = sem_b("yT_odd")
            gate_ready = sem_b("gate_ready")
            route_shifted = sem_b("route_shifted")
            route_exped = sem_b("route_exped")
            lora_ready = sem_b("lora_ready")
            loraT_ready = sem_b("loraT_ready")
            loraT_copied = sem_b("loraT_copied")
            PER_BANK = 3
            WIDE = LORA + EXPERTS

            def gate_tiles(j):
                n = min(PER_BANK, GRID - PER_BANK * j)
                return slice(PER_BANK * j, PER_BANK * j + n), n, \
                    bank[4 + j][:, 0:n * WIDE].rearrange("p (t e) -> p t e", e=WIDE)

            with nc.Block() as block:
                @block.tensor
                def _(pe):
                    transpose_mixed(pe, bank[4]).then_inc(last_mixedT_ready, 1)
                    pe.wait_ge(last_mixedT_copied, 2)
                    project_out(pe, 0, proj_ready)
                    pe.wait_ge(y_b, 1)
                    for g in range(4):
                        for w in range(4):
                            t = pe.transpose(bank[4 + g][0:HALF, w * P:(w + 1) * P],
                                             y[:, 4 * (g // 2) + w, (g % 2) * HALF:(g % 2 + 1) * HALF], ident[:, :])
                        t.then_inc(yT_b, 1)
                    pe.wait_ge(yT_even, 2)
                    pe.wait_ge(yT_odd, 2)
                    for t in range(GRID):
                        for kc in range(2):
                            m = pe.matmul(bank[4 + t // PER_BANK][:, (t % PER_BANK) * WIDE:(t % PER_BANK + 1) * WIDE],
                                          yT[:, kc, t * P:(t + 1) * P], aT_gate[:, kc, :],
                                          start=(kc == 0), stop=(kc == 1))
                        m.then_inc(gate_ready, 1)
                    for j in range(3):
                        pe.wait_ge(lora_ready, j + 1)
                        tiles = gate_tiles(j)[0]
                        for t in range(tiles.start, tiles.stop):
                            pe.transpose(bank[t // 4][:, (t % 4) * P:(t % 4 + 1) * P], lora[:, t, :], ident[:, :])\
                                .then_inc(loraT_ready, 1)

                @block.vector
                def _(dve):
                    done = [0]

                    def chain(ins):
                        ins.then_inc(dve_step_b, 1)
                        done[0] += 1
                        dve.wait_ge(dve_step_b, done[0])

                    dve.tensor_scalar(k_bias_odd[:, :], qk_bias[:, 2:4], mask_odd[0:HALF, :], None, ALU.mult)
                    for j in range(4):
                        dve.wait_ge(proj_ready, 2 * j + 2)
                        chain(dve.tensor_tensor(h[:, 2 * j:2 * j + 2, :],
                                                bank[j][:, 0:2 * DIM].rearrange("p (w m) -> p w m", w=2),
                                                h_plus[:, 2 * j:2 * j + 2, :], ALU.add))
                        for w in (2 * j, 2 * j + 1):
                            last = dve.bn_stats(stats[:, w, :], h[:, w, :])
                    last.then_inc(h_ready_b, 1)
                    dve.wait_ge(h_ready_b, 1)
                    for w in range(GRID):
                        last = dve.bn_aggr(mean_var[:, w, :], stats[:, w, :])
                    last.then_inc(var_b, 1)
                    dve.wait_ge(std_b, 1)
                    chain(dve.reciprocal(rstd[:, :], std[:, :]))
                    chain(dve.scalar_tensor_tensor(out=shift[:, :], in0=mean_var[:, :, 0], scalar=-1.0,
                                                   in1=rstd[:, :], op0=ALU.mult, op1=ALU.mult))
                    for w in range(GRID):
                        last = dve.tensor_scalar(y[:, w, :], h[:, w, :], rstd[:, w:w + 1], shift[:, w:w + 1],
                                                 ALU.mult, ALU.add)
                    last.then_inc(y_b, 1)
                    for g in (1, 3):
                        dve.wait_ge(yT_b, g + 1)
                        dve.tensor_copy(yT_columns(yT, g), transposed_tiles(bank[4 + g])).then_inc(yT_odd, 1)
                    for j in range(3):
                        tiles, n, prod = gate_tiles(j)
                        dve.wait_ge(gate_ready, tiles.stop)
                        last = dve.tensor_tensor(logits[:, tiles, :], prod[:, :, LORA:WIDE],
                                                 gate_bias[:, :].unsqueeze(1).to_broadcast([P, n, EXPERTS]), ALU.add)
                    chain(last)
                    spread = [P, GRID, EXPERTS]
                    chain(dve.tensor_reduce(route_max[:, :], logits[:, :, :], AX.X, ALU.max))
                    dve.tensor_tensor(route_exp[:, :, :], logits[:, :, :],
                                      route_max[:, :].unsqueeze(2).to_broadcast(spread), ALU.subtract)\
                        .then_inc(route_shifted, 1)
                    dve.wait_ge(route_exped, 1)
                    chain(dve.tensor_reduce(route_sum[:, :], route_exp[:, :, :], AX.X, ALU.add))
                    chain(dve.reciprocal(route_max[:, :], route_sum[:, :]))
                    chain(dve.tensor_tensor(route[:, :, :], route_exp[:, :, :],
                                            route_max[:, :].unsqueeze(2).to_broadcast(spread), ALU.mult))
                    cube = [P, GRID, EXPERTS, EXPERTS]
                    other = route[:, :, :].unsqueeze(2).to_broadcast(cube)
                    own = route[:, :, :].unsqueeze(3).to_broadcast(cube)
                    dve.tensor_tensor(beaten[:, :, :, :], other, own, ALU.is_gt)
                    chain(dve.tensor_tensor(tied[:, :, :, :], other, own, ALU.is_equal))
                    chain(dve.tensor_tensor(tied[:, :, :, :], tied[:, :, :, :],
                                            earlier[:, :, :].unsqueeze(1).to_broadcast(cube), ALU.mult))
                    chain(dve.tensor_tensor(beaten[:, :, :, :], beaten[:, :, :, :], tied[:, :, :, :], ALU.add))
                    chain(dve.tensor_reduce(rank[:, :, :], beaten[:, :, :, :], AX.X, ALU.add))
                    chain(dve.tensor_scalar(rank[:, :, :], rank[:, :, :], TOP - 0.5, LORA_SCALE,
                                            ALU.is_lt, ALU.mult))
                    chain(dve.tensor_tensor(dispatch[:, :, :], rank[:, :, :], route[:, :, :], ALU.mult))
                    for j in range(3):
                        tiles, n, prod = gate_tiles(j)
                        dve.tensor_tensor(lora[:, tiles, :].rearrange("p t (e r) -> p t e r", r=RANK),
                                          prod[:, :, 0:LORA].rearrange("p t (e r) -> p t e r", r=RANK),
                                          dispatch[:, tiles, :].unsqueeze(3).to_broadcast([P, n, EXPERTS, RANK]),
                                          ALU.mult).then_inc(lora_ready, 1)
                    dve.wait_ge(loraT_ready, 8)
                    dve.tensor_copy(loraT[:, BANK:2 * BANK], bank[1][:, :]).then_inc(loraT_copied, 1)

                @block.scalar
                def _(act):
                    act.wait_ge(last_mixedT_ready, 1)
                    for e in range(2):
                        act.copy(round_mixedT(ROUNDS - 1, e), mixedT_psum(bank[4], e))\
                            .then_inc(last_mixedT_copied, 1)
                    act.wait_ge(var_b, 1)
                    act.activation(std[:, :], mean_var[:, :, 1], ACT.Sqrt, bias=eps[:, :]).then_inc(std_b, 1)
                    for g in (0, 2):
                        act.wait_ge(yT_b, g + 1)
                        act.copy(yT_columns(yT, g), transposed_tiles(bank[4 + g])).then_inc(yT_even, 1)
                    act.wait_ge(route_shifted, 1)
                    act.activation(route_exp[:, :, :], route_exp[:, :, :], ACT.Exp).then_inc(route_exped, 1)
                    act.wait_ge(loraT_ready, 4)
                    act.copy(loraT[:, 0:BANK], bank[0][:, :]).then_inc(loraT_copied, 1)

                @block.gpsimd
                def _(pool):
                    pool.wait_ge(h_ready_b, 1)
                    pool.tensor_tensor(h_plus[:, :, :], h[:, :, :],
                                       ffn_bias[:, :].unsqueeze(1).to_broadcast([P, GRID, DIM]), ALU.add)\
                        .then_inc(h_plus_b, 1)

        def attention_pe(pe, back, front, ahead):
            keep_clock(pe, bank[7], FEED_START)
            if front:
                project_q_k(pe, wT[1], True, ahead)
            if back:
                for c in range(GROUPS):
                    transpose_probs(pe, c, bank[c])
            if front:
                pe.wait_ge(q_copied, 1)
                pe.wait_ge(k_even_copied, 1)
                pe.wait_ge(k_odd_copied, 1)
                scores(pe)
            if back:
                for c in range(GROUPS):
                    pe.wait_ge(probsT_copied[c], 1)
                    keep_clock(pe, bank[c], FEED_NARROW)
                    head_matmuls(pe, bank[c], probsT, v_of, HEAD, c).then_inc(kv_ready, 1)
            if front:
                pe.wait_ge(tokens_ready, 3)
                project_v(pe, wT[1], True)
            if back:
                pe.wait_ge(mixed_ready, GROUPS)
                transpose_mixed(pe, bank[0]).then_inc(mixedT_ready, 1)
            keep_clock(pe, bank[1], FEED_END)

        def attention_dve(dve, back, front):
            if front:
                dve.wait_ge(k_ready, 1)
                for m in range(2):
                    last = dve.tensor_scalar(k_round[:, 0, m, :],
                                             K_BANK[0:HALF, m * ROUND_TOKENS:(m + 1) * ROUND_TOKENS],
                                             qk_bias[:, 2 + m:3 + m], mask_even[0:HALF, :], ALU.add, ALU.mult)
                last.then_inc(k_even_copied, 1)
                for c in range(GROUPS):
                    shift_scores(dve, c)
                for c in range(GROUPS):
                    invert_sums(dve, c)
            if back:
                for c in range(GROUPS):
                    dve.wait_ge(kv_ready, c + 1)
                    dve.tensor_copy(mixed_of(c), narrow(bank[c][:, 0:BLOCKS * HEAD])).then_inc(mixed_ready, 1)
            if front:
                for j in range(2):
                    dve.wait_ge(v_ready, j + 1)
                    dve.tensor_tensor(v_round[:, 2 * j:2 * j + 2, :],
                                      V_BANK[j][:, 0:2 * DIM].rearrange("p (b m) -> p b m", b=2),
                                      v_bias[:, :].unsqueeze(1).to_broadcast([P, 2, DIM]), ALU.add)\
                        .then_inc(v_copied, 1)

        def attention_act(act, back, front, now, ahead):
            if front:
                for kc in range(2):
                    act.copy(yT_round[:, kc, :, :, :], twice(yT[:, kc, :], ahead)).then_inc(tokens_ready, 1)
                act.copy(loraT_round[:, :, :, :], twice(loraT[:, :], ahead)).then_inc(tokens_ready, 1)
                act.wait_ge(q_ready, 1)
                for m in range(2):
                    last = act.activation(q_round[:, m, :],
                                          Q_BANK[0:HALF, m * ROUND_TOKENS:(m + 1) * ROUND_TOKENS],
                                          ACT.Identity, bias=qk_bias[:, m:m + 1])
                last.then_inc(q_copied, 1)
                act.wait_ge(k_ready, 1)
                act.wait_ge(k_even_copied, 1)
                for m in range(2):
                    last = act.activation(k_round[:, 1, m, :],
                                          K_BANK[0:HALF, m * ROUND_TOKENS:(m + 1) * ROUND_TOKENS],
                                          ACT.Identity, scale=mask_odd[0:HALF, :], bias=k_bias_odd[:, m:m + 1])
                last.then_inc(k_odd_copied, 1)
            if back:
                for c in range(GROUPS):
                    act.wait_ge(probsT_ready[c], 1)
                    act.copy(probsT[:, c, :, :], blocks(bank[c][:, :])).then_inc(probsT_copied[c], 1)
            if front:
                for c in range(GROUPS):
                    exponentiate(act, c)
            if back:
                act.wait_ge(mixedT_ready, 1)
                for e in range(2):
                    act.copy(round_mixedT(now, e), mixedT_psum(bank[0], e)).then_inc(mixedT_copied, 1)

        def attention_block(back=None, front=None):
            with nc.Block(no_gpsimd_drain=True) as block:
                @block.tensor
                def _(pe):
                    attention_pe(pe, back is not None, front is not None, front)

                @block.vector
                def _(dve):
                    attention_dve(dve, back is not None, front is not None)

                @block.scalar
                def _(act):
                    attention_act(act, back is not None, front is not None, back, front)

                @block.gpsimd
                def _(pool):
                    if front is not None:
                        for c in range(GROUPS):
                            if back is not None:
                                pool.wait_ge(probsT_ready[c], 1)
                            normalise_rows(pool, c)
            nc.all_engine_barrier(sems_to_clear=round_sems)

        attention_block(front=0)
        with nc.Fori(0, ROUNDS - 1) as q:
            attention_block(back=q, front=q + 1)
        attention_block(back=ROUNDS - 1)

        final_ready = sem("final_ready")
        final_summed = sem("final_summed")
        stored = sem("stored")
        with nc.Block() as block:
            @block.tensor
            def _(pe):
                project_out(pe, 1, final_ready)

            @block.vector
            def _(dve):
                for j in range(4):
                    dve.wait_ge(final_ready, 2 * j + 2)
                    dve.tensor_tensor(y[:, 2 * j:2 * j + 2, :],
                                      bank[j][:, 0:2 * DIM].rearrange("p (w m) -> p w m", w=2),
                                      h_plus[:, 2 * j:2 * j + 2, :], ALU.add).then_inc(final_summed, 1)

            @block.sync
            def _(sp):
                rows = out.rearrange("b (h w) c -> (b h) w c", w=GRID)
                for j in range(4):
                    sp.wait_ge(final_summed, j + 1)
                    sp.dma_start(rows[:, 2 * j:2 * j + 2, :], y[:, 2 * j:2 * j + 2, :]).then_inc(stored, 16)
                sp.wait_ge(stored, 4 * 16)


def twice(columns, q):
    ap = columns[:, bass.ds(q * ROUND_TOKENS, ROUND_TOKENS)].rearrange("p (b t) -> p b t", b=QUAD)
    return ap.unsqueeze(2).to_broadcast([ap.shape[0], QUAD, 2, TOKENS])


def x_channel(x, c):
    return x.rearrange("b c (h r) w -> c b h (r w)", r=PATCH)[c]


def transposed_tiles(b):
    return b[0:HALF, :].rearrange("p (w b h) -> p w b h", w=4, h=GRID)


def yT_columns(yT, g):
    first = 4 * (g // 2)
    return yT[:, g % 2, :].rearrange("p (b w h) -> p w b h", w=GRID, h=GRID)[:, first:first + 4, :, :]


_INS = ['x', 'L0_tok_ln1_g', 'L0_tok_ln1_b', 'L0_tok_W', 'L0_tok_b', 'L0_tok_ln2_g', 'L0_tok_ln2_b',
        'L0_attn_w_qkv', 'L0_attn_w_proj', 'L0_attn_b_proj', 'L0_ffn_W_qkv', 'L0_ffn_b_qkv',
        'L0_ffn_W_gate', 'L0_ffn_b_gate', 'L0_ffn_A', 'L0_ffn_B_lora', 'L0_ffn_W_proj', 'L0_ffn_b_proj']
_OUTS = [((IMAGES, TOKENS, DIM), 'float32')]


def kernel(**inputs):
    import numpy as _np
    import concourse.bacc as _bacc
    from concourse import mybir as _mybir
    from concourse.bass_utils import run_bass_kernel_spmd as _run

    nc = _bacc.Bacc("TRN2", target_bir_lowering=False, num_devices=1)
    arrays, args = {}, []
    for name in _INS:
        a = _np.ascontiguousarray(inputs[name])
        arrays[f"in_{name}_dram"] = a
        args.append(nc.dram_tensor(f"in_{name}_dram", a.shape, _mybir.dt.from_np(a.dtype), kind="ExternalInput").ap())
    for i, (shape, dtype) in enumerate(_OUTS):
        dt = _mybir.dt.from_np(_np.dtype(dtype))
        args.append(nc.dram_tensor(f"out_{i}_dram", shape, dt, kind="ExternalOutput").ap())
    vit_tower_kernel(nc, *args)
    r = _run(nc, [arrays], core_ids=[0])
    return r.results[0]["out_0_dram"]
```

```python
from contextlib import ExitStack

import concourse.bass as bass
from concourse import mybir

F32 = mybir.dt.float32
ALU = mybir.AluOpType
ACT = mybir.ActivationFunctionType
AX = mybir.AxisListType

P = 128
IMAGES, CHANNELS, SIDE, PATCH = 16, 3, 128, 16
GRID = SIDE // PATCH
TOKENS = GRID * GRID
PIXELS = PATCH * PATCH * CHANNELS
DIM, HEADS = 192, 12
HEAD = DIM // HEADS
HALF = DIM // 2
GROUPS = 3
PAIRS = HEADS // 2
EXPERTS, RANK = 8, 16
LORA = EXPERTS * RANK
LORA_SCALE = 2.0
TOP = 2
EPS = 1e-5
STEPS = 6
SCALE = float(HEAD) ** -0.5
CHUNKS = PIXELS // P
BANK = 512
QUAD = 4
ROUNDS = IMAGES // QUAD
PAIRS_OF_TILES = GRID // 2
ROUND_TOKENS = QUAD * TOKENS
BLOCKS = 8
GRAM_V = TOKENS + HEAD
PER_GRAM_BANK = BANK // GRAM_V
GRAM_BANKS = GROUPS * BLOCKS // PER_GRAM_BANK
PAD = TOKENS - HEAD
SLOTS = 4
FEED_WARM_UP = 30
FEED_START, FEED_END = 6, 4
FEED_NORM, FEED_ROUTER = 5, 14
FEED_SOFTMAX = 21
FEED_ATTENTION = 2
FEED_NARROW = 3
FEED_TINY = 2
FEED_COLUMNS = 384
FEED_BESIDE = 256
FEED_PV = BANK


def vit_tower_kernel(nc, x, tok_ln1_g, tok_ln1_b, tok_W, tok_b, tok_ln2_g, tok_ln2_b,
                     attn_w_qkv, attn_w_proj, attn_b_proj, ffn_W_qkv, ffn_b_qkv, ffn_W_gate,
                     ffn_b_gate, ffn_A, ffn_B_lora, ffn_W_proj, ffn_b_proj, out):
    with ExitStack() as ctx:
        def sb(name, shape):
            return ctx.enter_context(nc.sbuf_tensor(name, shape, F32))

        def sem(name):
            return ctx.enter_context(nc.semaphore(name))

        def sems(name, n=GROUPS):
            return [sem(f"{name}_{i}") for i in range(n)]

        bank = [ctx.enter_context(nc.psum_tensor(f"bank{i}", [P, BANK], F32)) for i in range(8)]

        ident = sb("ident", [P, P])
        clock_feed = ctx.enter_context(nc.sbuf_tensor("clock_feed", [P, BANK], mybir.dt.bfloat16))
        ident_pair = sb("ident_pair", [P, TOKENS])
        mask_even = sb("mask_even", [P, 1])
        mask_odd = sb("mask_odd", [P, 1])
        eps = sb("eps", [P, 1])
        earlier = sb("earlier", [P, EXPERTS, EXPERTS])
        w_tok = sb("w_tok", [P, 2, CHANNELS, DIM])
        w_tok_g = sb("w_tok_g", [P, 2, CHANNELS, DIM])
        ln1_g = sb("ln1_g", [P, 2, CHANNELS])
        ln1_b = sb("ln1_b", [P, 2, CHANNELS])
        tok_bias = sb("tok_bias", [P, DIM])
        ln2_g = sb("ln2_g", [P, DIM])
        ln2_b = sb("ln2_b", [P, DIM])
        attn_bias = sb("attn_bias", [P, DIM])
        ffn_bias = sb("ffn_bias", [P, DIM])
        v_bias = sb("v_bias", [P, DIM])
        gate_bias = sb("gate_bias", [P, EXPERTS])
        qk_bias = sb("qk_bias", [HALF, 4])
        k_bias_odd = sb("k_bias_odd", [HALF, 2])
        qkv_raw = [sb(f"qkv_raw{i}", [HALF, 6, DIM]) for i in range(2)]
        proj_raw = [sb(f"proj_raw{i}", [HALF, 2, DIM]) for i in range(2)]
        proj_parity = [sb(f"proj_parity{i}", [HALF, 2, DIM]) for i in range(2)]
        qk_bias_raw = sb("qk_bias_raw", [4, HALF])
        a_raw = sb("a_raw", [LORA, DIM])
        gate_raw = sb("gate_raw", [EXPERTS, DIM])
        b_raw = sb("b_raw", [HALF, 6, EXPERTS, RANK])
        wT = [sb(f"wT{i}", [HALF, 2, 3 * DIM]) for i in range(2)]
        projT = [sb(f"projT{i}", [HALF, 2, DIM]) for i in range(2)]
        aT_gate = sb("aT_gate", [HALF, 2, LORA + EXPERTS])
        bT = sb("bT", [LORA, 3 * DIM])
        pix_stats = sb("pix_stats", [P, GRID, CHANNELS * 6])
        stats = sb("stats", [P, GRID, 6])
        mean_var = sb("mean_var", [P, GRID, 2])
        std = sb("std", [P, GRID])
        rstd = sb("rstd", [P, GRID])
        shift = sb("shift", [P, GRID])
        h = sb("h", [P, GRID, DIM])
        h_plus = sb("h_plus", [P, GRID, DIM])
        y = sb("y", [P, GRID, DIM])
        yT = sb("yT", [HALF, 2, IMAGES * TOKENS])
        loraT = sb("loraT", [LORA, IMAGES * TOKENS])
        mixedT = sb("mixedT", [HALF, 2, GRID, IMAGES * GRID])
        halves = (slice(0, TOKENS), slice(TOKENS, P))

        def keep_clock(pe, spare, n, columns=BANK):
            for _ in range(n if columns else 0):
                pe.matmul(spare[:, 0:columns], clock_feed[:, 0:P], clock_feed[:, 0:columns], start=True, stop=True)

        def transpose_yT(pe, j):
            for half in range(2):
                for w in range(2):
                    at = (2 * half + w) * P
                    t = pe.transpose(bank[4 + j][0:HALF, at:at + P],
                                     y[:, 2 * j + w, half * HALF:(half + 1) * HALF], ident[:, :])
            return t

        def copy_yT(act, j):
            for half in range(2):
                last = act.copy(
                    yT[:, half, :].rearrange("p (b w h) -> p w b h", w=GRID, h=GRID)[:, 2 * j:2 * j + 2, :, :],
                    bank[4 + j][0:HALF, half * 2 * P:(half + 1) * 2 * P]
                    .rearrange("p (w b h) -> p w b h", w=2, h=GRID))
            return last

        yT_round = sb("yT_round", [HALF, 2, QUAD, 2, TOKENS])
        loraT_round = sb("loraT_round", [LORA, QUAD, 2, TOKENS])
        q_round = sb("q_round", [HALF, 2, ROUND_TOKENS])
        k_round = sb("k_round", [HALF, 2, 2, ROUND_TOKENS])
        v_flat = sb("v_flat", [P, QUAD * DIM + PAD])
        v_round = v_flat[:, 0:QUAD * DIM].rearrange("p (b m) -> p b m", b=QUAD)
        kv_flat = sb("kv_flat", [P, GROUPS * BLOCKS * HEAD + PAD])
        kv = kv_flat[:, 0:GROUPS * BLOCKS * HEAD].rearrange("p (c n d) -> p c n d", c=GROUPS, n=BLOCKS)
        row_max = sb("row_max", [P, GROUPS, BLOCKS])
        row_sum = sb("row_sum", [P, GROUPS, BLOCKS])
        row_inv = sb("row_inv", [P, GROUPS, BLOCKS])
        expd = sb("expd", [P, GROUPS, BLOCKS, TOKENS])
        probs = sb("probs", [P, GROUPS, BLOCKS, TOKENS])
        probsT = sb("probsT", [P, GROUPS, BLOCKS, TOKENS])
        gram_v = sb("gram_v", [P, GROUPS, BLOCKS, GRAM_V])
        col_sum = sb("col_sum", [P, GROUPS, BLOCKS])
        neg_max = sb("neg_max", [BLOCKS, GROUPS, 2])
        neg_inv = sb("neg_inv", [BLOCKS, GROUPS, 2])
        neg_inv_all = sb("neg_inv_all", [P, GROUPS, BLOCKS])
        resid_first = sb("resid_first", [P, GROUPS, BLOCKS, TOKENS])
        kv_next = sb("kv_next", [P, GROUPS, BLOCKS, HEAD])

        tokens_ready = sem("tokens_ready")
        q_ready, k_ready, v_ready = sem("q_ready"), sem("k_ready"), sem("v_ready")
        q_copied, k_even_copied, k_odd_copied = sem("q_copied"), sem("k_even_copied"), sem("k_odd_copied")
        v_copied = sem("v_copied")
        scores_ready = sems("scores_ready")
        max_ready = sems("max_ready")
        shifted = sems("shifted")
        exp_ready = sems("exp_ready")
        sum_ready = sems("sum_ready")
        inv_ready = sems("inv_ready")
        probs_ready = sems("probs_ready")
        probsT_ready = sems("probsT_ready")
        probsT_copied = sems("probsT_copied")
        col_sum_ready = sems("col_sum_ready")
        col_sumT_ready = sems("col_sumT_ready")
        neg_max_ready = sems("neg_max_ready")
        neg_inv_ready = sems("neg_inv_ready")
        neg_inv_spread = sems("neg_inv_spread")
        neg_inv_copied = sems("neg_inv_copied")
        gram_scaled_ready = sems("gram_scaled_ready")
        gram_ready = sems("gram_ready", GRAM_BANKS)
        kv_ready = sem("kv_ready")
        kv_moved = sem("kv_moved")
        square_ready = sems("square_ready")
        square_copied = sems("square_copied")
        step_ready = sems("step_ready")
        resid_ready = sems("resid_ready")
        resid_copied = sems("resid_copied")
        tail_ready = sems("tail_ready")
        mixed_ready = sem("mixed_ready")
        mixedT_ready = sem("mixedT_ready")
        mixedT_copied = sem("mixedT_copied")
        round_sems = range(tokens_ready.num, mixedT_copied.num + 1)

        Q_BANK, K_BANK, V_BANK = (bank[5], bank[6]), (bank[3], bank[4]), (bank[5], bank[6])

        def blocks(ap):
            return ap.rearrange("p (n t) -> p n t", t=TOKENS)

        def chunk_blocks(c):
            for n in range(BLOCKS):
                yield n, n % QUAD, GROUPS * (n // QUAD) + c

        def project_q_k(pe, weights, lora_on, ahead, pieces=range(4), parts=(True, True)):
            tokens = bass.ds(ahead * ROUND_TOKENS, ROUND_TOKENS)
            for i in pieces:
                dst = (Q_BANK + K_BANK)[i][0:HALF, 0:ROUND_TOKENS]
                o = i * HALF
                if parts[0]:
                    for kc in range(2):
                        t = pe.matmul(dst, weights[:, kc, o:o + HALF], yT[:, kc, tokens],
                                      start=(kc == 0), stop=(kc == 1 and not lora_on))
                if lora_on and parts[1]:
                    t = pe.matmul(dst, bT[:, o:o + HALF], loraT[:, tokens], start=False, stop=True)
                if parts[1]:
                    t.then_inc(q_ready if i < 2 else k_ready, 1)

        def project_v(pe, weights, lora_on, b):
            dst = V_BANK[b // 2][:, (b % 2) * DIM:(b % 2 + 1) * DIM]
            for kc in range(2):
                t = pe.matmul(dst, yT_round[:, kc, b, :, :].rearrange("p r t -> p (r t)"),
                              weights[:, kc, 2 * DIM:3 * DIM], start=(kc == 0),
                              stop=(kc == 1 and not lora_on))
            if lora_on:
                t = pe.matmul(dst, loraT_round[:, b, :, :].rearrange("p r t -> p (r t)"),
                              bT[:, 2 * DIM:3 * DIM], start=False, stop=True)
            if b % 2:
                t.then_inc(v_ready, 1)

        def scores(pe, c):
            rows = slice(32 * c, 32 * c + 32)
            for slot in range(SLOTS):
                half, image_pair = slot // 2, slot % 2
                for image in range(2):
                    cols = slice((2 * image_pair + image) * TOKENS, (2 * image_pair + image + 1) * TOKENS)
                    t = pe.matmul(SCORE_BANK[c][halves[image], slot * P:(slot + 1) * P],
                                  q_round[rows, half, cols], k_round[rows, :, half, cols],
                                  start=True, stop=True)
            t.then_inc(scores_ready[c], 1)

        def scores_and_v(pe, weights, lora_on, v_first, last_v=True):
            pe.wait_ge(q_copied, 2)
            pe.wait_ge(k_even_copied, 2)
            pe.wait_ge(k_odd_copied, 2)
            if v_first:
                pe.wait_ge(tokens_ready, 3 if lora_on else 2)
                project_v(pe, weights, lora_on, 0)
            for c in range(GROUPS):
                keep_clock(pe, SCORE_BANK[c], 1, FEED_COLUMNS)
                scores(pe, c)
                if c == 0 and not v_first:
                    pe.wait_ge(tokens_ready, 3 if lora_on else 2)
                    project_v(pe, weights, lora_on, 0)
                if c < GROUPS - 1 or last_v:
                    project_v(pe, weights, lora_on, c + 1)

        def transpose_probs_slot(pe, c, slot, dst):
            t = pe.transpose(dst[:, slot * P:(slot + 1) * P],
                             probs[:, c, 2 * slot:2 * slot + 2, :].rearrange("p n t -> p (n t)"), ident[:, :])
            if slot == SLOTS - 1:
                t.then_inc(probsT_ready[c], 1)

        def head_matmuls(pe, dst, lhsT, rhs_of, c):
            for n, b, pair in chunk_blocks(c):
                for e in range(2):
                    t = pe.matmul(dst[halves[e], n * TOKENS:(n + 1) * TOKENS], lhsT[halves[e], c, n, :],
                                  rhs_of(e, n, b, pair), start=True, stop=True)
            return t

        def v_of(e, n, b, pair):
            at = b * DIM + (2 * pair + e) * HEAD
            return v_flat[halves[e], at:at + TOKENS]

        def kv_of(c):
            return lambda e, n, b, pair: kv_flat[halves[e], (c * BLOCKS + n) * HEAD:(c * BLOCKS + n) * HEAD + TOKENS]

        def transpose_mixed(pe, dst):
            for b in range(QUAD):
                t = pe.transpose(dst[0:HALF, b * P:(b + 1) * P],
                                 mixed[:, b, :, :].rearrange("p g d -> p (g d)"), ident[:, :])
            return t


        def shift_scores(dve, c):
            dve.wait_ge(scores_ready[c], 1)
            dve.tensor_reduce(row_max[:, c, :], blocks(SCORE_BANK[c][:, :]), AX.X, ALU.max).then_inc(max_ready[c], 1)
            dve.wait_ge(max_ready[c], 1)
            dve.tensor_tensor(expd[:, c, :, :], blocks(SCORE_BANK[c][:, :]),
                              row_max[:, c, :].unsqueeze(2).to_broadcast([P, BLOCKS, TOKENS]), ALU.subtract)\
                .then_inc(shifted[c], 1)

        def exponentiate(act, c):
            act.wait_ge(shifted[c], 1)
            act.activation(expd[:, c, :, :], expd[:, c, :, :], ACT.Exp, scale=SCALE).then_inc(exp_ready[c], 1)

        def invert_sums(dve, c):
            dve.wait_ge(exp_ready[c], 1)
            dve.tensor_reduce(row_sum[:, c, :], expd[:, c, :, :], AX.X, ALU.add).then_inc(sum_ready[c], 1)
            dve.wait_ge(sum_ready[c], 1)
            dve.reciprocal(row_inv[:, c, :], row_sum[:, c, :]).then_inc(inv_ready[c], 1)

        def normalise_rows(pool, c):
            pool.wait_ge(inv_ready[c], 1)
            pool.tensor_tensor(probs[:, c, :, :], expd[:, c, :, :],
                               row_inv[:, c, :].unsqueeze(2).to_broadcast([P, BLOCKS, TOKENS]), ALU.mult)\
                .then_inc(probs_ready[c], 1)

        def mixed_of(c):
            return mixed[:, :, :, :].rearrange("p b (m g) d -> p b m g d", m=2)[:, :, :, c, :]

        def round_mixedT(q, e):
            return mixedT[:, e, :, bass.ds(q * QUAD * GRID, QUAD * GRID)].rearrange("p w (b h) -> p w b h", b=QUAD)

        def mixedT_psum(src, e):
            return src[0:HALF, :].rearrange("p (b e w h) -> p e w b h", b=QUAD, e=2, w=GRID)[:, e, :, :, :]

        def narrow(ap):
            return ap.rearrange("p (m b) d -> p b m d", m=2)

        PHASES = 2 * STEPS
        Q_K_AT, SCORES_AT, SHIFT_AT, EXP_AT, SUM_AT, V_AT = 0, 1, (1, 2, 2), (2, 3, 3), 3, 3
        TRANSPOSE_FROM, TRANSPOSED_AT = 5, (6, 7, 8)
        COL_SUM_AT, SPREAD_AT, GRAM_AT = 9, 10, 11
        SCORE_BANK = (bank[3], bank[4], bank[7])
        PROBS_T_BANK = (bank[5], bank[6], bank[3])
        GRAM_BANK = (bank[4], bank[7], bank[6], bank[5])
        MIXED_BANK = bank[3]
        MIX_AT = 4
        IDLE_FEED = {Q_K_AT: 2, SCORES_AT: 6, TRANSPOSE_FROM: 12, COL_SUM_AT: 8, SPREAD_AT: 4, GRAM_AT: 5}

        def gram_at(n, c):
            block = c * BLOCKS + n
            return block // PER_GRAM_BANK, block % PER_GRAM_BANK * GRAM_V

        def inverse_chunk_pe(pe, s, c, feed):
            t = s // 2
            if s % 2 == 0:
                r = resid if t else resid_first
                if t:
                    pe.wait_ge(resid_copied[c], t)
                keep_clock(pe, bank[c], 1, feed)
                head_matmuls(pe, bank[c], r, lambda e, n, b, pair: r[halves[e], c, n, :], c)\
                    .then_inc(square_ready[c], 1)
            else:
                pe.wait_ge(square_copied[c], t + 1)
                pe.wait_ge(step_ready[c], t + 1)
                keep_clock(pe, bank[c], 1, feed)
                head_matmuls(pe, bank[c], square, lambda e, n, b, pair: step[halves[e], c, n, :], c)\
                    .then_inc(resid_ready[c], 1)

        def inverse_tail_pe(pe):
            pe.wait_ge(kv_moved, 1)
            for c in range(GROUPS):
                pe.wait_ge(resid_copied[c], STEPS)
                keep_clock(pe, bank[c], 1, FEED_COLUMNS)
                head_matmuls(pe, bank[c], resid, kv_of(c), c).then_inc(tail_ready[c], 1)

        def feed_columns(s, c, softmax):
            if softmax and s * GROUPS + c < 6:
                return 0
            return FEED_BESIDE if softmax and TRANSPOSE_FROM <= s <= TRANSPOSED_AT[-1] else FEED_COLUMNS

        def dense_piece_pe(pe, s, c, mix, ahead):
            if s * GROUPS + c < 4:
                project_q_k(pe, wT[0], False, ahead, (s * GROUPS + c,))
            if TRANSPOSE_FROM <= s <= TRANSPOSED_AT[-1]:
                chunk, slot = divmod((s - TRANSPOSE_FROM) * GROUPS + c, SLOTS)
                if slot == 0:
                    if chunk == 0:
                        pe.wait_ge(v_copied, 2)
                    pe.wait_ge(probs_ready[chunk], 1)
                    if mix and PROBS_T_BANK[chunk] is MIXED_BANK:
                        pe.wait_ge(mixedT_copied, 2)
                transpose_probs_slot(pe, chunk, slot, PROBS_T_BANK[chunk])

        def softmax_gap_pe(pe, s):
            if s == SCORES_AT:
                scores_and_v(pe, wT[0], False, True)
            if s == COL_SUM_AT:
                for c in range(GROUPS):
                    pe.wait_ge(col_sum_ready[c], 1)
                    pe.transpose(GRAM_BANK[c][0:BLOCKS, 0:P], col_sum[:, c, :], ident[:, :])\
                        .then_inc(col_sumT_ready[c], 1)
            if s == SPREAD_AT:
                keep_clock(pe, GRAM_BANK[-1], FEED_TINY)
                for c in range(GROUPS):
                    pe.wait_ge(neg_inv_ready[c], 1)
                    for e in range(2):
                        t = pe.matmul(GRAM_BANK[c][halves[e], P:P + BLOCKS],
                                      neg_inv[:, c, e:e + 1].to_broadcast([BLOCKS, TOKENS]),
                                      ident[0:BLOCKS, 0:BLOCKS], start=True, stop=True)
                    t.then_inc(neg_inv_spread[c], 1)
                keep_clock(pe, GRAM_BANK[-1], FEED_TINY)
            if s == GRAM_AT:
                for c in range(GROUPS):
                    pe.wait_ge(neg_inv_copied[c], 1)
                for c in range(GROUPS):
                    pe.wait_ge(gram_scaled_ready[c], 1)
                    keep_clock(pe, GRAM_BANK[c + 1], 1, FEED_COLUMNS)
                    for n in range(BLOCKS):
                        j, at = gram_at(n, c)
                        for e in range(2):
                            t = pe.matmul(GRAM_BANK[j][halves[e], at:at + GRAM_V], probsT[halves[e], c, n, :],
                                          gram_v[halves[e], c, n, :], start=True, stop=True)
                        if at == (PER_GRAM_BANK - 1) * GRAM_V:
                            t.then_inc(gram_ready[j], 1)

        def nystrom_pe(pe, inverse, softmax, mix, ahead):
            if inverse:
                keep_clock(pe, bank[7], FEED_START)
            for s in range(PHASES):
                if not inverse and s != SCORES_AT:
                    keep_clock(pe, bank[0], IDLE_FEED.get(s, 0))
                for c in range(GROUPS):
                    if inverse:
                        inverse_chunk_pe(pe, s, c, feed_columns(s, c, softmax))
                    if softmax:
                        dense_piece_pe(pe, s, c, mix, ahead)
                if not inverse and s == SCORES_AT:
                    keep_clock(pe, bank[0], IDLE_FEED[s])
                if softmax:
                    softmax_gap_pe(pe, s)
                if mix and s == MIX_AT:
                    if softmax:
                        pe.wait_ge(shifted[0], 1)
                    transpose_mixed(pe, MIXED_BANK).then_inc(mixedT_ready, 1)
            if inverse:
                inverse_tail_pe(pe)
            keep_clock(pe, bank[0] if not inverse else bank[3] if softmax else bank[7], FEED_END)

        def scale_transposed(engine, c):
            engine.tensor_tensor(gram_v[:, c, :, 0:TOKENS], probsT[:, c, :, :],
                                 neg_inv_all[:, c, :].unsqueeze(2).to_broadcast([P, BLOCKS, TOKENS]),
                                 ALU.mult).then_inc(gram_scaled_ready[c], 1)

        def nystrom_dve(dve, inverse, softmax, ahead):
            if softmax:
                for kc in range(2):
                    dve.tensor_copy(yT_round[:, kc, :, :, :], twice(yT[:, kc, :], ahead)).then_inc(tokens_ready, 1)
            for s in range(PHASES):
                if inverse and s % 2 == 0:
                    t = s // 2
                    for c in range(GROUPS):
                        dve.wait_ge(square_copied[c], t + 1)
                        dve.scalar_tensor_tensor(out=step[:, c, :, :], in0=(resid if t else resid_first)[:, c, :, :],
                                                 scalar=3.0, in1=square[:, c, :, :], op0=ALU.mult, op1=ALU.add)\
                            .then_inc(step_ready[c], 1)
                if not softmax:
                    continue
                if s == Q_K_AT:
                    for m in range(2):
                        dve.wait_ge(k_ready, m + 1)
                        dve.tensor_scalar(k_round[:, 0, m, :], K_BANK[m][0:HALF, 0:ROUND_TOKENS],
                                          mask_even[0:HALF, :], None, ALU.mult).then_inc(k_even_copied, 1)
                for c in range(GROUPS):
                    if s == SHIFT_AT[c]:
                        shift_scores(dve, c)
                if s == SUM_AT:
                    for c in range(GROUPS):
                        invert_sums(dve, c)
                if s in TRANSPOSED_AT:
                    c = TRANSPOSED_AT.index(s)
                    dve.wait_ge(probsT_copied[c], 1)
                    dve.tensor_reduce(col_sum[:, c, :], probsT[:, c, :, :], AX.X, ALU.add)\
                        .then_inc(col_sum_ready[c], 1)
                if s == COL_SUM_AT:
                    for c in range(GROUPS):
                        dve.wait_ge(col_sumT_ready[c], 1)
                        dve.tensor_reduce(neg_max[:, c, :], blocks(GRAM_BANK[c][0:BLOCKS, 0:P]), AX.X, ALU.max,
                                          negate=True).then_inc(neg_max_ready[c], 1)
                        dve.wait_ge(neg_max_ready[c], 1)
                        dve.reciprocal(neg_inv[:, c, :], neg_max[:, c, :]).then_inc(neg_inv_ready[c], 1)
                if s == SPREAD_AT:
                    for c in range(GROUPS):
                        dve.wait_ge(neg_inv_spread[c], 1)
                        dve.tensor_copy(neg_inv_all[:, c, :], GRAM_BANK[c][:, P:P + BLOCKS])\
                            .then_inc(neg_inv_copied[c], 1)
                    for c in (0, 2):
                        dve.wait_ge(neg_inv_copied[c], 1)
                        scale_transposed(dve, c)
                if s == GRAM_AT:
                    if inverse:
                        dve.wait_ge(kv_moved, 1)
                    flat_resid = resid_first[:, :, :, :].rearrange("p c n t -> p (c n) t")
                    flat_kv = kv_next[:, :, :, :].rearrange("p c n d -> p (c n) d")
                    for j in range(GRAM_BANKS):
                        dve.wait_ge(gram_ready[j], 1)
                        first = j * PER_GRAM_BANK
                        own = slice(first, first + PER_GRAM_BANK)
                        both = GRAM_BANK[j][:, 0:PER_GRAM_BANK * GRAM_V].rearrange("p (n m) -> p n m", m=GRAM_V)
                        dve.tensor_tensor(flat_resid[:, own, :], both[:, :, 0:TOKENS],
                                          ident_pair[:, :].unsqueeze(1).to_broadcast([P, PER_GRAM_BANK, TOKENS]),
                                          ALU.add)
                        dve.tensor_copy(flat_kv[:, own, :], both[:, :, TOKENS:GRAM_V])
            if inverse:
                for c in range(GROUPS):
                    dve.wait_ge(tail_ready[c], 1)
                    dve.tensor_tensor(mixed_of(c), narrow(kv[:, c, :, :]),
                                      narrow(blocks(bank[c][:, :])[:, :, 0:HEAD]), ALU.subtract).then_inc(mixed_ready, 1)

        def nystrom_act(act, inverse, softmax, mix, before):
            for s in range(PHASES):
                t = s // 2
                if inverse:
                    for c in range(GROUPS):
                        if s % 2 == 0:
                            act.wait_ge(square_ready[c], t + 1)
                            act.copy(square[:, c, :, :], blocks(bank[c][:, :])).then_inc(square_copied[c], 1)
                        else:
                            act.wait_ge(resid_ready[c], t + 1)
                            act.mul(resid[:, c, :, :], blocks(bank[c][:, :]), 0.25).then_inc(resid_copied[c], 1)
                if mix and s == MIX_AT:
                    act.wait_ge(mixedT_ready, 1)
                    for e in range(2):
                        act.copy(round_mixedT(before, e), mixedT_psum(MIXED_BANK, e)).then_inc(mixedT_copied, 1)
                if not softmax:
                    continue
                if s == Q_K_AT:
                    for m in range(2):
                        act.wait_ge(q_ready, m + 1)
                        act.copy(q_round[:, m, :], Q_BANK[m][0:HALF, 0:ROUND_TOKENS]).then_inc(q_copied, 1)
                    for m in range(2):
                        act.wait_ge(k_even_copied, m + 1)
                        act.activation(k_round[:, 1, m, :], K_BANK[m][0:HALF, 0:ROUND_TOKENS],
                                       ACT.Copy, scale=mask_odd[0:HALF, :]).then_inc(k_odd_copied, 1)
                for c in range(GROUPS):
                    if s == EXP_AT[c]:
                        exponentiate(act, c)
                if s == V_AT:
                    for j in range(2):
                        act.wait_ge(v_ready, j + 1)
                        for image in range(2):
                            for e in range(2):
                                last = act.copy(
                                    gram_v[halves[e], :, 2 * j + image:BLOCKS:QUAD, TOKENS:GRAM_V]
                                    .rearrange("p c m d -> p m c d"),
                                    V_BANK[j][halves[e], image * DIM:(image + 1) * DIM]
                                    .rearrange("p (m c e d) -> p e m c d", m=2, c=GROUPS, e=2)[:, e, :, :, :])
                        last.then_inc(v_copied, 1)
                if s in TRANSPOSED_AT:
                    c = TRANSPOSED_AT.index(s)
                    act.wait_ge(probsT_ready[c], 1)
                    act.copy(probsT[:, c, :, :], blocks(PROBS_T_BANK[c][:, :])).then_inc(probsT_copied[c], 1)

        def nystrom_pool(pool, inverse, softmax):
            if inverse:
                pool.tensor_copy(kv_flat[:, 0:GROUPS * BLOCKS * HEAD],
                                 kv_next[:, :, :, :].rearrange("p c n d -> p (c n d)")).then_inc(kv_moved, 1)
            if softmax:
                for c in range(GROUPS):
                    normalise_rows(pool, c)
                pool.wait_ge(neg_inv_copied[1], 1)
                scale_transposed(pool, 1)

        def nystrom_block(inverse=None, softmax=None, mix=None):
            with nc.Block(no_gpsimd_drain=True) as block:
                @block.tensor
                def _(pe):
                    nystrom_pe(pe, inverse is not None, softmax is not None, mix is not None, softmax)

                @block.vector
                def _(dve):
                    nystrom_dve(dve, inverse is not None, softmax is not None, softmax)

                @block.scalar
                def _(act):
                    nystrom_act(act, inverse is not None, softmax is not None, mix is not None, mix)

                @block.gpsimd
                def _(pool):
                    nystrom_pool(pool, inverse is not None, softmax is not None)
            nc.all_engine_barrier(sems_to_clear=round_sems)

        def project_out(pe, i, ready):
            for w in range(GRID):
                for e in range(2):
                    t = pe.matmul(bank[w // 2][:, (w % 2) * DIM:(w % 2 + 1) * DIM], mixedT[:, e, w, :],
                                  projT[i][:, e, :], start=(e == 0), stop=(e == 1))
                t.then_inc(ready, 1)

        def attention_pe(pe, back, front, ahead, begun=False):
            if not begun:
                keep_clock(pe, bank[7], FEED_ATTENTION)
            if front:
                project_q_k(pe, wT[1], True, ahead, parts=(not begun, True))
            if not back:
                keep_clock(pe, bank[1], FEED_NARROW)
            if back:
                for c in range(GROUPS):
                    for slot in range(SLOTS):
                        transpose_probs_slot(pe, c, slot, bank[c])
            if front:
                keep_clock(pe, SCORE_BANK[-1], FEED_TINY)
                scores_and_v(pe, wT[1], True, False, last_v=not back)
            if back:
                for c in range(GROUPS):
                    pe.wait_ge(probsT_copied[c], 1)
                    keep_clock(pe, bank[c], 1, FEED_PV)
                    head_matmuls(pe, bank[c], probsT, v_of, c).then_inc(kv_ready, 1)
            if back and front:
                project_v(pe, wT[1], True, QUAD - 1)
            if back:
                pe.wait_ge(mixed_ready, GROUPS)
                transpose_mixed(pe, bank[0]).then_inc(mixedT_ready, 1)
            keep_clock(pe, bank[1], FEED_END if back else FEED_SOFTMAX)

        def attention_dve(dve, back, front):
            if front:
                for m in range(2):
                    dve.wait_ge(k_ready, m + 1)
                    dve.tensor_scalar(k_round[:, 0, m, :], K_BANK[m][0:HALF, 0:ROUND_TOKENS],
                                      qk_bias[:, 2 + m:3 + m], mask_even[0:HALF, :], ALU.add, ALU.mult)\
                        .then_inc(k_even_copied, 1)
                for c in range(GROUPS):
                    shift_scores(dve, c)
                for c in range(GROUPS):
                    invert_sums(dve, c)
            if back:
                for c in range(GROUPS):
                    dve.wait_ge(kv_ready, c + 1)
                    dve.tensor_copy(mixed_of(c), narrow(blocks(bank[c][:, :])[:, :, 0:HEAD])).then_inc(mixed_ready, 1)
            if front:
                for j in range(2):
                    dve.wait_ge(v_ready, j + 1)
                    dve.tensor_tensor(v_round[:, 2 * j:2 * j + 2, :],
                                      V_BANK[j][:, 0:2 * DIM].rearrange("p (b m) -> p b m", b=2),
                                      v_bias[:, :].unsqueeze(1).to_broadcast([P, 2, DIM]), ALU.add)\
                        .then_inc(v_copied, 1)

        def spread_tokens(act, ahead):
            for kc in range(2):
                act.copy(yT_round[:, kc, :, :, :], twice(yT[:, kc, :], ahead)).then_inc(tokens_ready, 1)

        def attention_act(act, back, front, now, ahead, begun=False):
            if front:
                if not begun:
                    spread_tokens(act, ahead)
                act.copy(loraT_round[:, :, :, :], twice(loraT[:, :], ahead)).then_inc(tokens_ready, 1)
                for m in range(2):
                    act.wait_ge(q_ready, m + 1)
                    act.activation(q_round[:, m, :], Q_BANK[m][0:HALF, 0:ROUND_TOKENS],
                                   ACT.Identity, bias=qk_bias[:, m:m + 1]).then_inc(q_copied, 1)
                for m in range(2):
                    act.wait_ge(k_even_copied, m + 1)
                    act.activation(k_round[:, 1, m, :], K_BANK[m][0:HALF, 0:ROUND_TOKENS],
                                   ACT.Identity, scale=mask_odd[0:HALF, :], bias=k_bias_odd[:, m:m + 1])\
                        .then_inc(k_odd_copied, 1)
            if back:
                for c in range(GROUPS):
                    act.wait_ge(probsT_ready[c], 1)
                    act.copy(probsT[:, c, :, :], blocks(bank[c][:, :])).then_inc(probsT_copied[c], 1)
            if front:
                for c in range(GROUPS):
                    exponentiate(act, c)
            if back:
                act.wait_ge(mixedT_ready, 1)
                for e in range(2):
                    act.copy(round_mixedT(now, e), mixedT_psum(bank[0], e)).then_inc(mixedT_copied, 1)

        def attention_block(back=None, front=None):
            with nc.Block(no_gpsimd_drain=True) as block:
                @block.tensor
                def _(pe):
                    attention_pe(pe, back is not None, front is not None, front)

                @block.vector
                def _(dve):
                    attention_dve(dve, back is not None, front is not None)

                @block.scalar
                def _(act):
                    attention_act(act, back is not None, front is not None, back, front)

                @block.gpsimd
                def _(pool):
                    if front is not None:
                        for c in range(GROUPS):
                            if back is not None:
                                pool.wait_ge(probsT_ready[c], 1)
                            normalise_rows(pool, c)
            nc.all_engine_barrier(sems_to_clear=round_sems)

        with ExitStack() as stage:
            def sem_a(name):
                return stage.enter_context(nc.semaphore(name))

            def sb_a(name, shape):
                return stage.enter_context(nc.sbuf_tensor(name, shape, F32))

            T_SLOTS = 4
            pixels = sb_a("pixels", [P, CHANNELS, PATCH, GRID, PATCH])
            patches = sb_a("patches", [P, GRID, PIXELS])
            patchesT = sb_a("patchesT", [P, T_SLOTS, PIXELS])
            pix_loaded = [sem_a(f"pix_loaded{c}") for c in range(CHANNELS)]
            tok_w_loaded = sem_a("tok_w_loaded")
            tok_rows_loaded = sem_a("tok_rows_loaded")
            attn_w_loaded = sem_a("attn_w_loaded")
            ffn_w_loaded = sem_a("ffn_w_loaded")
            ffn_rows_loaded = sem_a("ffn_rows_loaded")
            ident_zeroed = sem_a("ident_zeroed")
            ident_ready = sem_a("ident_ready")
            consts_ready = sem_a("consts_ready")
            w_scaled = sem_a("w_scaled")
            feed_ready = sem_a("feed_ready")
            parity_ready = sem_a("parity_ready")
            dve_step = sem_a("dve_step_a")
            var_ready = sem_a("var_ready")
            std_ready = sem_a("std_ready")
            patch_ready = sem_a("patch_ready")
            patchT_ready = sem_a("patchT_ready")
            patchT_copied = sem_a("patchT_copied")
            bias_row_ready = sem_a("bias_row_ready")
            bias_row_copied = sem_a("bias_row_copied")
            tok_ready = sem_a("tok_ready")
            wT_ready = sem_a("wT_ready")
            wT_copied = sem_a("wT_copied")
            h_ready = sem_a("h_ready")
            shift_ready = sem_a("shift_ready")
            y_ready = sem_a("y_ready")
            yT_ready = sem_a("yT_ready")
            yT_copied = sem_a("yT_copied")

            def weight_groups():
                groups = []
                for i in range(2):
                    for kc in range(2):
                        for th in range(2):
                            ins = [qkv_raw[i][:, 3 * th + t, kc * HALF:(kc + 1) * HALF] for t in range(3)]
                            groups.append((ins, HALF, wT[i][:, kc, th * 3 * HALF:(th + 1) * 3 * HALF]))
                    ins = [proj_parity[i][:, o, e * HALF:(e + 1) * HALF] for e in range(2) for o in range(2)]
                    groups.append((ins, HALF, projT[i][:, :, :].rearrange("p e o -> p (e o)")))
                for kc in range(2):
                    ins = [a_raw[:, kc * HALF:(kc + 1) * HALF], gate_raw[:, kc * HALF:(kc + 1) * HALF]]
                    groups.append((ins, HALF, aT_gate[:, kc, :]))
                for th in range(2):
                    ins = [b_raw[:, 3 * th + t, :, :].rearrange("p n r -> p (n r)") for t in range(3)]
                    groups.append((ins, LORA, bT[:, th * 3 * HALF:(th + 1) * 3 * HALF]))
                groups.append(([qk_bias_raw[:, :]], HALF, qk_bias[:, :]))
                return groups

            w_groups = weight_groups()
            attn_groups = 5
            early_groups = len(w_groups) - 3

            with nc.Block() as block:
                @block.sync
                def _(sp):
                    for c in range(CHANNELS):
                        sp.dma_start(pixels[:, c, :, :, :].rearrange("p r w s -> p (r w s)"),
                                     x_channel(x, c)).then_inc(pix_loaded[c], 16)
                    sp.dma_start(w_tok[:, :, :, :],
                                 tok_W.rearrange("(a p c) m -> p a c m", a=2, c=CHANNELS)).then_inc(tok_w_loaded, 16)
                    sp.dma_start(qkv_raw[0][:, :, :],
                                 attn_w_qkv.rearrange("(t p) i -> p t i", p=HALF)).then_inc(attn_w_loaded, 16)
                    sp.dma_start(proj_raw[0][:, :, :],
                                 attn_w_proj.rearrange("(t p) i -> p t i", p=HALF)).then_inc(attn_w_loaded, 16)
                    sp.dma_start(qkv_raw[1][:, :, :],
                                 ffn_W_qkv.rearrange("(t p) i -> p t i", p=HALF)).then_inc(ffn_w_loaded, 16)
                    sp.dma_start(proj_raw[1][:, :, :],
                                 ffn_W_proj.rearrange("(t p) i -> p t i", p=HALF)).then_inc(ffn_w_loaded, 16)
                    sp.dma_start(a_raw[:, :], ffn_A.rearrange("n r d -> (n r) d")).then_inc(ffn_w_loaded, 16)
                    sp.dma_start(gate_raw[:, :], ffn_W_gate).then_inc(ffn_w_loaded, 16)
                    sp.dma_start(qk_bias_raw[:, :],
                                 ffn_b_qkv[0:2 * DIM].rearrange("(t p) -> t p", p=HALF)).then_inc(ffn_w_loaded, 16)
                    for t in range(6):
                        sp.dma_start(b_raw[:, t, :, :],
                                     ffn_B_lora[:, t * HALF:(t + 1) * HALF, :].rearrange("n p r -> p n r"))\
                            .then_inc(ffn_w_loaded, 16)
                    sp.wait_ge(ffn_rows_loaded, 3 * 16)

                def row(dram):
                    return dram.rearrange("(a d) -> a d", a=1).to_broadcast([P, dram.shape[0]])

                @block.gpsimd
                def _(pool):
                    pool.memset(ident[:, :], 0.0).then_inc(ident_zeroed, 1)
                    pool.memset(clock_feed[:, :], 1.0).then_inc(feed_ready, 1)
                    pool.memset(v_flat[:, QUAD * DIM:], 0.0)
                    pool.memset(kv_flat[:, GROUPS * BLOCKS * HEAD:], 0.0)
                    pool.memset(eps[:, :], EPS).then_inc(consts_ready, 1)
                    pool.memset(earlier[:, :, :], 1.0).then_inc(ident_zeroed, 1)
                    pool.wait_ge(ident_zeroed, 2)
                    pool.affine_select(out=ident[:, :], in_=ident[:, :], compare_op=ALU.not_equal, fill=1.0,
                                       base=0, pattern=[[-1, P]], channel_multiplier=1).then_inc(ident_ready, 1)
                    pool.affine_select(out=earlier[:, :, :], in_=earlier[:, :, :], compare_op=ALU.is_gt, fill=0.0,
                                       base=0, pattern=[[1, EXPERTS], [-1, EXPERTS]], channel_multiplier=0)\
                        .then_inc(consts_ready, 1)
                    pool.wait_ge(tok_w_loaded, 3 * 16)
                    pool.tensor_tensor(w_tok_g[:, :, :, :].rearrange("p a c m -> p (a c) m"),
                                       w_tok[:, :, :, :].rearrange("p a c m -> p (a c) m"),
                                       ln1_g[:, :, :].rearrange("p a c -> p (a c)").unsqueeze(2)
                                       .to_broadcast([P, CHUNKS, DIM]), ALU.mult).then_inc(w_scaled, 1)
                    for i, (loaded, n) in enumerate(((attn_w_loaded, 2), (ffn_w_loaded, 11))):
                        pool.wait_ge(loaded, n * 16)
                        for o in range(2):
                            last = pool.tensor_copy(
                                proj_parity[i][:, o, :].rearrange("p (e g d) -> p e g d", e=2, d=HEAD),
                                proj_raw[i][:, o, :].rearrange("p (g e d) -> p e g d", e=2, d=HEAD))
                        last.then_inc(parity_ready, 1)
                    for j in range(PAIRS_OF_TILES):
                        pool.wait_ge(h_ready, j + 1)
                        pool.tensor_tensor(h_plus[:, 2 * j:2 * j + 2, :], h[:, 2 * j:2 * j + 2, :],
                                           attn_bias[:, :].unsqueeze(1).to_broadcast([P, 2, DIM]), ALU.add)
                    nystrom_pool(pool, False, True)

                @block.vector
                def _(dve):
                    done = [0]

                    def chain(ins):
                        ins.then_inc(dve_step, 1)
                        done[0] += 1
                        dve.wait_ge(dve_step, done[0])

                    for c in range(CHANNELS):
                        dve.wait_ge(pix_loaded[c], 16)
                        for w in range(GRID):
                            last = dve.bn_stats(pix_stats[:, w, 6 * c:6 * c + 6], pixels[:, c, :, w, :])
                    chain(last)
                    for w in range(GRID):
                        last = dve.bn_aggr(mean_var[:, w, :], pix_stats[:, w, :])
                    last.then_inc(var_ready, 1)
                    dve.wait_ge(ident_ready, 1)
                    dve.tensor_tensor(ident_pair[:, :], ident[:, 0:TOKENS], ident[:, TOKENS:P], ALU.add)
                    chain(dve.tensor_reduce(mask_even[:, :],
                                            ident[:, :].rearrange("p (g e d) -> p g e d", e=2, d=HEAD)[:, :, 0, :],
                                            AX.XY, ALU.add))
                    dve.tensor_scalar(mask_odd[:, :], mask_even[:, :], -1.0, 1.0, ALU.mult, ALU.add)

                    def inverse_std(n, tiles):
                        dve.wait_ge(std_ready, n)
                        chain(dve.reciprocal(rstd[:, tiles], std[:, tiles]))

                    inverse_std(1, slice(0, GRID))
                    for w in range(GRID):
                        dve.tensor_scalar(patches[:, w, :].rearrange("p (a s) -> p a s", s=PATCH),
                                          pixels[:, :, :, w, :].rearrange("p c r s -> p (c r) s"),
                                          mean_var[:, w, 0:1], rstd[:, w:w + 1], ALU.subtract, ALU.mult)\
                            .then_inc(patch_ready, 1)
                    dve.wait_ge(bias_row_ready, 1)
                    dve.wait_ge(tok_rows_loaded, 4 * 16)
                    dve.tensor_tensor(tok_bias[:, :], bank[7][:, 0:DIM], tok_bias[:, :], ALU.add)\
                        .then_inc(bias_row_copied, 1)
                    dve.wait_ge(bias_row_copied, 1)

                    def norm_stats(src, tiles):
                        for w in tiles:
                            last = dve.bn_stats(stats[:, w, :], src[:, w, :])
                        chain(last)
                        for w in tiles:
                            last = dve.bn_aggr(mean_var[:, w, :], stats[:, w, :])
                        last.then_inc(var_ready, 1)

                    for j in range(PAIRS_OF_TILES):
                        pair, tiles = slice(2 * j, 2 * j + 2), range(2 * j, 2 * j + 2)
                        dve.wait_ge(tok_ready, 2 * j + 2)
                        chain(dve.tensor_tensor(y[:, pair, :],
                                                bank[4 + j][:, 0:2 * DIM].rearrange("p (w m) -> p w m", w=2),
                                                tok_bias[:, :].unsqueeze(1).to_broadcast([P, 2, DIM]), ALU.add))
                        norm_stats(y, tiles)
                        inverse_std(2 * j + 2, pair)
                        for w in tiles:
                            last = dve.scalar_tensor_tensor(out=y[:, w, :], in0=y[:, w, :],
                                                            scalar=mean_var[:, w, 0:1], in1=ln2_g[:, :],
                                                            op0=ALU.subtract, op1=ALU.mult)
                        chain(last)
                        for w in tiles:
                            last = dve.scalar_tensor_tensor(out=h[:, w, :], in0=y[:, w, :],
                                                            scalar=rstd[:, w:w + 1], in1=ln2_b[:, :],
                                                            op0=ALU.mult, op1=ALU.add)
                        last.then_inc(h_ready, 1)
                        dve.wait_ge(h_ready, j + 1)
                        norm_stats(h, tiles)
                        inverse_std(2 * j + 3, pair)
                        dve.scalar_tensor_tensor(out=shift[:, pair], in0=mean_var[:, pair, 0], scalar=-1.0,
                                                 in1=rstd[:, pair], op0=ALU.mult, op1=ALU.mult)\
                            .then_inc(shift_ready, 1)
                    dve.wait_ge(yT_copied, PAIRS_OF_TILES)
                    nystrom_dve(dve, False, True, 0)

                @block.scalar
                def _(act):
                    act.dma_start(ln1_g[:, :, :],
                                  tok_ln1_g.rearrange("(a p c) -> p a c", a=2, c=CHANNELS)).then_inc(tok_w_loaded, 16)
                    act.dma_start(ln1_b[:, :, :],
                                  tok_ln1_b.rearrange("(a p c) -> p a c", a=2, c=CHANNELS)).then_inc(tok_w_loaded, 16)
                    act.dma_start(tok_bias[:, :], row(tok_b)).then_inc(tok_rows_loaded, 16)
                    act.dma_start(ln2_g[:, :], row(tok_ln2_g)).then_inc(tok_rows_loaded, 16)
                    act.dma_start(ln2_b[:, :], row(tok_ln2_b)).then_inc(tok_rows_loaded, 16)
                    act.dma_start(attn_bias[:, :], row(attn_b_proj)).then_inc(tok_rows_loaded, 16)
                    act.dma_start(ffn_bias[:, :], row(ffn_b_proj)).then_inc(ffn_rows_loaded, 16)
                    act.dma_start(v_bias[:, :], row(ffn_b_qkv[2 * DIM:3 * DIM])).then_inc(ffn_rows_loaded, 16)
                    act.dma_start(gate_bias[:, :], row(ffn_b_gate)).then_inc(ffn_rows_loaded, 16)

                    def std_of(n, tiles):
                        act.wait_ge(var_ready, n)
                        act.wait_ge(consts_ready, 1)
                        act.activation(std[:, tiles], mean_var[:, tiles, 1], ACT.Sqrt, bias=eps[:, :])\
                            .then_inc(std_ready, 1)

                    def copy_patchT(w):
                        act.wait_ge(patchT_ready, 2 * w + 2)
                        if w >= T_SLOTS:
                            act.wait_ge(tok_ready, w - T_SLOTS + 1)
                        for b in range(2):
                            last = act.copy(patchesT[:, w % T_SLOTS, b * 384:(b + 1) * 384],
                                            bank[2 * (w % 2) + b][:, 0:384])
                        last.then_inc(patchT_copied, 1)

                    def weights(first, end):
                        for g in range(first, end):
                            ins, rows, dst = w_groups[g]
                            act.wait_ge(wT_ready, g + 1)
                            act.copy(dst, bank[g % 4][0:rows, 0:dst.free_size()]).then_inc(wT_copied, 1)

                    def copy_tokensT(j):
                        act.wait_ge(yT_ready, j + 1)
                        copy_yT(act, j).then_inc(yT_copied, 1)

                    def normalise(j):
                        act.wait_ge(shift_ready, j + 1)
                        for w in (2 * j, 2 * j + 1):
                            last = act.activation(y[:, w, :], h[:, w, :], ACT.Identity,
                                                  scale=rstd[:, w:w + 1], bias=shift[:, w:w + 1])
                        last.then_inc(y_ready, 1)

                    std_of(1, slice(0, GRID))
                    for w in range(GRID):
                        copy_patchT(w)
                        if w in (5, 7):
                            normalise((w - 5) // 2)
                        if w >= 3:
                            n = w - 3
                            std_of(n + 2, slice(n // 2 * 2, n // 2 * 2 + 2))
                    copy_tokensT(0)
                    std_of(7, slice(4, 6))
                    copy_tokensT(1)
                    normalise(2)
                    std_of(8, slice(6, 8))
                    copy_tokensT(2)
                    weights(0, 7)
                    std_of(9, slice(6, 8))
                    weights(7, 9)
                    normalise(3)
                    weights(9, early_groups)
                    copy_tokensT(PAIRS_OF_TILES - 1)
                    weights(early_groups, len(w_groups))
                    nystrom_act(act, False, True, False, None)

                @block.tensor
                def _(pe):
                    pe.wait_ge(ident_ready, 1)
                    pe.wait_ge(feed_ready, 1)

                    keep_clock(pe, bank[0], FEED_WARM_UP)
                    pe.wait_ge(tok_w_loaded, 3 * 16)
                    for k in range(CHUNKS):
                        t = pe.matmul(bank[7][:, 0:DIM], ln1_b[:, k % 2, k // 2:k // 2 + 1].to_broadcast([P, P]),
                                      w_tok[:, k % 2, k // 2, :], start=(k == 0), stop=(k == CHUNKS - 1))
                    t.then_inc(bias_row_ready, 1)

                    def transpose_tile(w):
                        pe.wait_ge(patch_ready, w + 1)
                        if w >= 2:
                            pe.wait_ge(patchT_copied, w - 1)
                        for k in range(CHUNKS):
                            t = pe.transpose(bank[2 * (w % 2) + k // 3][:, (k % 3) * P:(k % 3 + 1) * P],
                                             patches[:, w, k * P:(k + 1) * P], ident[:, :])
                            if k % 3 == 2:
                                t.then_inc(patchT_ready, 1)

                    def project_tile(w):
                        pe.wait_ge(patchT_copied, w + 1)
                        if w == 6:
                            pe.wait_ge(bias_row_copied, 1)
                        dst = bank[4 + w // 2][:, (w % 2) * DIM:(w % 2 + 1) * DIM]
                        for k in range(CHUNKS):
                            t = pe.matmul(dst, patchesT[:, w % T_SLOTS, k * P:(k + 1) * P], w_tok_g[:, k % 2, k // 2, :],
                                          start=(k == 0), stop=(k == CHUNKS - 1))
                        t.then_inc(tok_ready, 1)

                    transpose_tile(0)
                    transpose_tile(1)
                    pe.wait_ge(w_scaled, 1)
                    for w in range(GRID):
                        project_tile(w)
                        if w + 2 < GRID:
                            transpose_tile(w + 2)
                    for j in range(PAIRS_OF_TILES - 1):
                        pe.wait_ge(y_ready, j + 1)
                        transpose_yT(pe, j).then_inc(yT_ready, 1)
                    pe.wait_ge(yT_copied, 1)
                    for g, (ins, rows, dst) in enumerate(w_groups):
                        if g % 2 == 0:
                            keep_clock(pe, bank[4], 1)
                        if g == early_groups:
                            pe.wait_ge(y_ready, PAIRS_OF_TILES)
                            transpose_yT(pe, PAIRS_OF_TILES - 1).then_inc(yT_ready, 1)
                        if g == 0:
                            pe.wait_ge(attn_w_loaded, 2 * 16)
                            pe.wait_ge(parity_ready, 1)
                        if g == attn_groups:
                            pe.wait_ge(ffn_w_loaded, 11 * 16)
                            pe.wait_ge(parity_ready, 2)
                        if g >= 4:
                            pe.wait_ge(wT_copied, g - 3)
                        at = 0
                        for src in ins:
                            cols = src.shape[0]
                            t = pe.transpose(bank[g % 4][0:rows, at:at + cols], src, ident[0:cols, 0:cols])
                            at += cols
                        t.then_inc(wT_ready, 1)
                    pe.wait_ge(wT_copied, len(w_groups))
                    pe.wait_ge(yT_copied, PAIRS_OF_TILES)
                    nystrom_pe(pe, False, True, False, 0)
            nc.all_engine_barrier(sems_to_clear=round_sems)

        resid = sb("resid", [P, GROUPS, BLOCKS, TOKENS])
        square = sb("square", [P, GROUPS, BLOCKS, TOKENS])
        step = sb("step", [P, GROUPS, BLOCKS, TOKENS])
        mixed = sb("mixed", [P, QUAD, PAIRS, HEAD])
        logits = sb("logits", [P, GRID, EXPERTS])
        route_max = sb("route_max", [P, GRID])
        route_sum = sb("route_sum", [P, GRID])
        route_exp = sb("route_exp", [P, GRID, EXPERTS])
        route = sb("route", [P, GRID, EXPERTS])
        beaten = sb("beaten", [P, GRID, EXPERTS, EXPERTS])
        tied = sb("tied", [P, GRID, EXPERTS, EXPERTS])
        rank = sb("rank", [P, GRID, EXPERTS])
        dispatch = sb("dispatch", [P, GRID, EXPERTS])
        lora = sb("lora", [P, GRID, LORA])

        nystrom_block(inverse=0, softmax=1)
        with nc.Fori(1, ROUNDS - 1) as q:
            nystrom_block(inverse=q, softmax=q + 1, mix=q - 1)

        with ExitStack() as stage:
            def sem_b(name):
                return stage.enter_context(nc.semaphore(name))

            last_mixedT_ready = sem_b("last_mixedT_ready")
            last_mixedT_copied = sem_b("last_mixedT_copied")
            proj_ready = sem_b("proj_ready")
            dve_step_b = sem_b("dve_step_b")
            var_b = sem_b("var_b")
            std_b = sem_b("std_b")
            y_b = sem_b("y_b")
            yT_b = sem_b("yT_b")
            yT_copied_b = sem_b("yT_copied_b")
            gate_ready = sem_b("gate_ready")
            route_shifted = sem_b("route_shifted")
            route_exped = sem_b("route_exped")
            lora_ready = sem_b("lora_ready")
            loraT_ready = sem_b("loraT_ready")
            loraT_copied = sem_b("loraT_copied")
            WIDE = LORA + EXPERTS
            ROUTED = GRID // 2

            GATE_BANK = (bank[0], bank[1], bank[2], bank[7])
            LORA_T_BANK = (bank[0], bank[1])

            def gate_tiles(j):
                return GATE_BANK[j][:, 0:2 * WIDE].rearrange("p (t e) -> p t e", e=WIDE)

            with nc.Block() as block:
                @block.tensor
                def _(pe):
                    nystrom_pe(pe, True, False, True, None)
                    pe.wait_ge(mixed_ready, GROUPS)
                    transpose_mixed(pe, bank[4]).then_inc(last_mixedT_ready, 1)
                    keep_clock(pe, bank[5], FEED_START)
                    pe.wait_ge(last_mixedT_copied, 2)
                    project_out(pe, 0, proj_ready)
                    for j in range(PAIRS_OF_TILES):
                        keep_clock(pe, bank[4 + j], FEED_NORM)
                        pe.wait_ge(y_b, j + 1)
                        transpose_yT(pe, j).then_inc(yT_b, 1)
                    keep_clock(pe, bank[0], FEED_NARROW)
                    pe.wait_ge(yT_copied_b, PAIRS_OF_TILES)
                    for t in range(GRID):
                        for kc in range(2):
                            m = pe.matmul(GATE_BANK[t // 2][:, (t % 2) * WIDE:(t % 2 + 1) * WIDE],
                                          yT[:, kc, t * P:(t + 1) * P], aT_gate[:, kc, :],
                                          start=(kc == 0), stop=(kc == 1))
                        if t % 2:
                            m.then_inc(gate_ready, 1)
                    for r in range(2):
                        if r == 0:
                            project_q_k(pe, wT[1], True, 0, parts=(True, False))
                        else:
                            keep_clock(pe, bank[1], FEED_ROUTER)
                        for t in range(ROUTED * r, ROUTED * r + ROUTED):
                            pe.wait_ge(lora_ready, t // 2 + 1)
                            pe.transpose(LORA_T_BANK[r][:, (t % 4) * P:(t % 4 + 1) * P], lora[:, t, :], ident[:, :])\
                                .then_inc(loraT_ready, 1)
                    pe.wait_ge(loraT_copied, 1)
                    keep_clock(pe, bank[0], FEED_NARROW)
                    pe.wait_ge(loraT_copied, 2)
                    attention_pe(pe, False, True, 0, begun=True)

                @block.vector
                def _(dve):
                    done = [0]

                    def chain(ins):
                        ins.then_inc(dve_step_b, 1)
                        done[0] += 1
                        dve.wait_ge(dve_step_b, done[0])

                    nystrom_dve(dve, True, False, None)
                    dve.tensor_scalar(k_bias_odd[:, :], qk_bias[:, 2:4], mask_odd[0:HALF, :], None, ALU.mult)

                    def residual(j):
                        dve.wait_ge(proj_ready, 2 * j + 2)
                        chain(dve.tensor_tensor(h[:, 2 * j:2 * j + 2, :],
                                                bank[j][:, 0:2 * DIM].rearrange("p (w m) -> p w m", w=2),
                                                h_plus[:, 2 * j:2 * j + 2, :], ALU.add))
                        for w in (2 * j, 2 * j + 1):
                            last = dve.bn_stats(stats[:, w, :], h[:, w, :])
                        chain(last)
                        for w in (2 * j, 2 * j + 1):
                            last = dve.bn_aggr(mean_var[:, w, :], stats[:, w, :])
                        last.then_inc(var_b, 1)

                    def normalise(j):
                        dve.wait_ge(std_b, j + 1)
                        chain(dve.reciprocal(rstd[:, 2 * j:2 * j + 2], std[:, 2 * j:2 * j + 2]))
                        for w in (2 * j, 2 * j + 1):
                            last = dve.tensor_scalar(y[:, w, :], h[:, w, :], mean_var[:, w, 0:1],
                                                     rstd[:, w:w + 1], ALU.subtract, ALU.mult)
                        last.then_inc(y_b, 1)

                    residual(0)
                    for j in range(PAIRS_OF_TILES - 1):
                        residual(j + 1)
                        normalise(j)
                    normalise(PAIRS_OF_TILES - 1)

                    spread = [P, ROUTED, EXPERTS]
                    cube = [P, ROUTED, EXPERTS, EXPERTS]
                    for r in range(2):
                        own_tiles = slice(ROUTED * r, ROUTED * r + ROUTED)
                        for j in (2 * r, 2 * r + 1):
                            dve.wait_ge(gate_ready, j + 1)
                            last = dve.tensor_tensor(logits[:, 2 * j:2 * j + 2, :], gate_tiles(j)[:, :, LORA:WIDE],
                                                     gate_bias[:, :].unsqueeze(1).to_broadcast([P, 2, EXPERTS]),
                                                     ALU.add)
                        chain(last)
                        chain(dve.tensor_reduce(route_max[:, own_tiles], logits[:, own_tiles, :], AX.X, ALU.max))
                        dve.tensor_tensor(route_exp[:, own_tiles, :], logits[:, own_tiles, :],
                                          route_max[:, own_tiles].unsqueeze(2).to_broadcast(spread), ALU.subtract)\
                            .then_inc(route_shifted, 1)
                        dve.wait_ge(route_exped, r + 1)
                        chain(dve.tensor_reduce(route_sum[:, own_tiles], route_exp[:, own_tiles, :], AX.X, ALU.add))
                        chain(dve.reciprocal(route_max[:, own_tiles], route_sum[:, own_tiles]))
                        chain(dve.tensor_tensor(route[:, own_tiles, :], route_exp[:, own_tiles, :],
                                                route_max[:, own_tiles].unsqueeze(2).to_broadcast(spread), ALU.mult))
                        other = route[:, own_tiles, :].unsqueeze(2).to_broadcast(cube)
                        own = route[:, own_tiles, :].unsqueeze(3).to_broadcast(cube)
                        dve.tensor_tensor(beaten[:, own_tiles, :, :], other, own, ALU.is_gt)
                        chain(dve.tensor_tensor(tied[:, own_tiles, :, :], other, own, ALU.is_equal))
                        chain(dve.tensor_tensor(tied[:, own_tiles, :, :], tied[:, own_tiles, :, :],
                                                earlier[:, :, :].unsqueeze(1).to_broadcast(cube), ALU.mult))
                        chain(dve.tensor_tensor(beaten[:, own_tiles, :, :], beaten[:, own_tiles, :, :],
                                                tied[:, own_tiles, :, :], ALU.add))
                        chain(dve.tensor_reduce(rank[:, own_tiles, :], beaten[:, own_tiles, :, :], AX.X, ALU.add))
                        chain(dve.tensor_scalar(rank[:, own_tiles, :], rank[:, own_tiles, :], TOP - 0.5, LORA_SCALE,
                                                ALU.is_lt, ALU.mult))
                        chain(dve.tensor_tensor(dispatch[:, own_tiles, :], rank[:, own_tiles, :],
                                                route[:, own_tiles, :], ALU.mult))
                        for j in (2 * r, 2 * r + 1):
                            pair = slice(2 * j, 2 * j + 2)
                            dve.tensor_tensor(lora[:, pair, :].rearrange("p t (e r) -> p t e r", r=RANK),
                                              gate_tiles(j)[:, :, 0:LORA].rearrange("p t (e r) -> p t e r", r=RANK),
                                              dispatch[:, pair, :].unsqueeze(3).to_broadcast([P, 2, EXPERTS, RANK]),
                                              ALU.mult).then_inc(lora_ready, 1)
                    attention_dve(dve, False, True)

                @block.scalar
                def _(act):
                    nystrom_act(act, True, False, True, ROUNDS - 2)
                    act.wait_ge(last_mixedT_ready, 1)
                    for e in range(2):
                        act.copy(round_mixedT(ROUNDS - 1, e), mixedT_psum(bank[4], e))\
                            .then_inc(last_mixedT_copied, 1)

                    def std_of(j):
                        act.wait_ge(var_b, j + 1)
                        act.activation(std[:, 2 * j:2 * j + 2], mean_var[:, 2 * j:2 * j + 2, 1], ACT.Sqrt,
                                       bias=eps[:, :]).then_inc(std_b, 1)

                    def copy_tokensT(j):
                        act.wait_ge(yT_b, j + 1)
                        copy_yT(act, j).then_inc(yT_copied_b, 1)

                    for j in range(PAIRS_OF_TILES):
                        std_of(j)
                    for j in range(PAIRS_OF_TILES):
                        copy_tokensT(j)
                    act.wait_ge(yT_copied_b, PAIRS_OF_TILES)
                    spread_tokens(act, 0)
                    for r in range(2):
                        tiles = slice(ROUTED * r, ROUTED * r + ROUTED)
                        act.wait_ge(route_shifted, r + 1)
                        act.activation(route_exp[:, tiles, :], route_exp[:, tiles, :], ACT.Exp)\
                            .then_inc(route_exped, 1)
                    for r in range(2):
                        act.wait_ge(loraT_ready, ROUTED * r + ROUTED)
                        act.copy(loraT[:, r * BANK:(r + 1) * BANK], LORA_T_BANK[r][:, :]).then_inc(loraT_copied, 1)
                    act.wait_ge(loraT_copied, 2)
                    attention_act(act, False, True, None, 0, begun=True)

                @block.gpsimd
                def _(pool):
                    nystrom_pool(pool, True, False)
                    for j in range(PAIRS_OF_TILES):
                        pool.wait_ge(var_b, j + 1)
                        pool.tensor_tensor(h_plus[:, 2 * j:2 * j + 2, :], h[:, 2 * j:2 * j + 2, :],
                                           ffn_bias[:, :].unsqueeze(1).to_broadcast([P, 2, DIM]), ALU.add)
                    for c in range(GROUPS):
                        normalise_rows(pool, c)
            nc.all_engine_barrier(sems_to_clear=round_sems)

        with nc.Fori(0, ROUNDS - 1) as q:
            attention_block(back=q, front=q + 1)

        final_ready = sem("final_ready")
        final_summed = sem("final_summed")
        stored = sem("stored")
        with nc.Block() as block:
            @block.tensor
            def _(pe):
                attention_pe(pe, True, False, None)
                pe.wait_ge(mixedT_copied, 2)
                project_out(pe, 1, final_ready)

            @block.scalar
            def _(act):
                attention_act(act, True, False, ROUNDS - 1, None)

            @block.vector
            def _(dve):
                attention_dve(dve, True, False)
                for j in range(4):
                    dve.wait_ge(final_ready, 2 * j + 2)
                    dve.tensor_tensor(y[:, 2 * j:2 * j + 2, :],
                                      bank[j][:, 0:2 * DIM].rearrange("p (w m) -> p w m", w=2),
                                      h_plus[:, 2 * j:2 * j + 2, :], ALU.add).then_inc(final_summed, 1)

            @block.sync
            def _(sp):
                rows = out.rearrange("b (h w) c -> (b h) w c", w=GRID)
                for j in range(4):
                    sp.wait_ge(final_summed, j + 1)
                    sp.dma_start(rows[:, 2 * j:2 * j + 2, :], y[:, 2 * j:2 * j + 2, :]).then_inc(stored, 16)
                sp.wait_ge(stored, 4 * 16)


def twice(columns, q):
    ap = columns[:, bass.ds(q * ROUND_TOKENS, ROUND_TOKENS)].rearrange("p (b t) -> p b t", b=QUAD)
    return ap.unsqueeze(2).to_broadcast([ap.shape[0], QUAD, 2, TOKENS])


def x_channel(x, c):
    return x.rearrange("b c (h r) w -> c b h (r w)", r=PATCH)[c]


_INS = ['x', 'L0_tok_ln1_g', 'L0_tok_ln1_b', 'L0_tok_W', 'L0_tok_b', 'L0_tok_ln2_g', 'L0_tok_ln2_b',
        'L0_attn_w_qkv', 'L0_attn_w_proj', 'L0_attn_b_proj', 'L0_ffn_W_qkv', 'L0_ffn_b_qkv',
        'L0_ffn_W_gate', 'L0_ffn_b_gate', 'L0_ffn_A', 'L0_ffn_B_lora', 'L0_ffn_W_proj', 'L0_ffn_b_proj']
_OUTS = [((IMAGES, TOKENS, DIM), 'float32')]


def kernel(**inputs):
    import numpy as _np
    import concourse.bacc as _bacc
    from concourse import mybir as _mybir
    from concourse.bass_utils import run_bass_kernel_spmd as _run

    nc = _bacc.Bacc("TRN2", target_bir_lowering=False, num_devices=1)
    arrays, args = {}, []
    for name in _INS:
        a = _np.ascontiguousarray(inputs[name])
        arrays[f"in_{name}_dram"] = a
        args.append(nc.dram_tensor(f"in_{name}_dram", a.shape, _mybir.dt.from_np(a.dtype), kind="ExternalInput").ap())
    for i, (shape, dtype) in enumerate(_OUTS):
        dt = _mybir.dt.from_np(_np.dtype(dtype))
        args.append(nc.dram_tensor(f"out_{i}_dram", shape, dt, kind="ExternalOutput").ap())
    vit_tower_kernel(nc, *args)
    r = _run(nc, [arrays], core_ids=[0])
    return r.results[0]["out_0_dram"]
```
